# Optimizing a Trainium2 kernel written in Bass

```python
import numpy as np
import jax
import jax.numpy as jnp

def _softmax(x, axis=-1):
    return jax.nn.softmax(x, axis=axis)

def _gelu(x):
    return jax.nn.gelu(x, approximate=True)

def _silu(x):
    return jax.nn.silu(x)

def _sigmoid(x):
    return jax.nn.sigmoid(x)

def _layernorm(x, axis=-1, eps=1e-05):
    m = jnp.mean(x, axis=axis, keepdims=True)
    v = jnp.var(x, axis=axis, keepdims=True)
    return (x - m) / jnp.sqrt(v + eps)

def _scatter_add(tgt, idx, src, axis=0):
    return tgt.at[idx].add(src)

def _segment_sum(src, seg, n):
    return jax.ops.segment_sum(src, seg, n)
kernel_name = 'mk_xattn_seq_d2_seqx_r8_ae75f2'

def setup_inputs(seed: int=0):
    np.random.seed(seed)
    _w = jnp.asarray

    def _rec_inputs():
        import jax
        import jax.numpy as jnp
        _rk = jax.random.key(seed)
        x = -0.0002928 + 1 * jax.random.normal(jax.random.fold_in(_rk, 1), (4, 256, 256), jnp.float32)
        _lenS = 256 - jax.random.randint(jax.random.fold_in(_rk, 7), (4,), 0, max(1, 256 // 4) + 1, jnp.int32)
        _lenS2 = 256 - jax.random.randint(jax.random.fold_in(_rk, 8), (4,), 0, max(1, 256 // 4) + 1, jnp.int32)
        _ctx_2048P = jax.random.normal(jax.random.fold_in(_rk, 11), (4, 16, 256), jnp.float32)
        _ctx_2048c = jax.random.dirichlet(jax.random.fold_in(_rk, 511), 0.3 * jnp.ones((16,), jnp.float32), (4, 256))
        _ctx_2048t = jnp.einsum('bsk,bkd->bsd', _ctx_2048c, _ctx_2048P)
        _ctx_2048t = _ctx_2048t * jax.lax.rsqrt(jnp.mean(jnp.square(_ctx_2048t)) + 1e-12) * 0.953939
        ctx_2048 = -1.39393e-06 + 0.999914 * (_ctx_2048t + 0.3 * jax.random.normal(jax.random.fold_in(_rk, 611), (4, 256, 256), jnp.float32))
        _validS = jnp.arange(256)[None, :] < _lenS[:, None]
        _validS2 = jnp.arange(256)[None, :] < _lenS2[:, None]
        _causal = jnp.tril(jnp.ones((256, 256), dtype=bool))
        mask_1x1xSxS2_fc1 = jnp.where(jnp.broadcast_to(_validS2[0:1, None, None, :], (1, 1, 256, 256)), 1.0, 0.0).astype(jnp.float32)
        mask_Bx1xSxS2_ff1 = jnp.where(jnp.ones((4, 1, 256, 256), dtype=bool), 1.0, 0.0).astype(jnp.float32)
        return (x, ctx_2048, mask_1x1xSxS2_fc1, mask_Bx1xSxS2_ff1)
    x, ctx_2048, mask_1x1xSxS2_fc1, mask_Bx1xSxS2_ff1 = _rec_inputs()

    def _L0_xattn_setup():
        import jax, jax.numpy as jnp
        import numpy as np
        H = 256
        NH = 16
        HD = H // NH
        EPS = 1e-05

        def gelu(x):
            return 0.5 * x * (1.0 + jnp.tanh(0.7978845608028654 * x * (1.0 + 0.044715 * x * x)))

        def layernorm(x, scale, bias):
            m = jnp.mean(x, axis=-1, keepdims=True)
            v = jnp.mean(jnp.square(x - m), axis=-1, keepdims=True)
            return (x - m) * jax.lax.rsqrt(v + EPS) * scale + bias

        def split_heads(x):
            b, s, _ = x.shape
            return x.reshape(b, s, NH, HD).transpose(0, 2, 1, 3)

        def merge_heads(x):
            b, nh, s, hd = x.shape
            return x.transpose(0, 2, 1, 3).reshape(b, s, nh * hd)

        def attention(q, k, v, mask):
            scores = jnp.einsum('bhqd,bhkd->bhqk', q, k) / jnp.sqrt(jnp.float32(HD))
            scores = scores * mask - 10000.0 * (1.0 - mask)
            probs = jax.nn.softmax(scores, axis=-1)
            return jnp.einsum('bhqk,bhkd->bhqd', probs, v)
        key = jax.random.key(seed)
        ks = jax.random.split(key, 16)
        b, s, t = (2, 128, 128)
        w = lambda k, i, o: jax.random.normal(k, (i, o), jnp.float32) * 0.02
        inp = {'hidden_states': jax.random.normal(ks[0], (b, s, H), jnp.float32), 'encoder_states': jax.random.normal(ks[1], (b, t, H), jnp.float32), 'ltor_mask': jnp.tril(jnp.ones((1, 1, s, s), jnp.float32)), 'cross_mask': jnp.ones((b, 1, s, t), jnp.float32), 'ln1_s': jnp.ones((H,), jnp.float32), 'ln1_b': jnp.zeros((H,), jnp.float32), 'w_qkv': w(ks[2], H, 3 * H), 'b_qkv': jnp.zeros((3 * H,), jnp.float32), 'w_ao': w(ks[3], H, H), 'b_ao': jnp.zeros((H,), jnp.float32), 'ln2_s': jnp.ones((H,), jnp.float32), 'ln2_b': jnp.zeros((H,), jnp.float32), 'w_q': w(ks[4], H, H), 'b_q': jnp.zeros((H,), jnp.float32), 'w_kv': w(ks[5], H, 2 * H), 'b_kv': jnp.zeros((2 * H,), jnp.float32), 'w_co': w(ks[6], H, H), 'b_co': jnp.zeros((H,), jnp.float32), 'ln3_s': jnp.ones((H,), jnp.float32), 'ln3_b': jnp.zeros((H,), jnp.float32), 'w1': w(ks[7], H, 4 * H), 'b1': jnp.zeros((4 * H,), jnp.float32), 'w2': w(ks[8], 4 * H, H), 'b2': jnp.zeros((H,), jnp.float32)}
        return inp
    _L0_xattn_all = _L0_xattn_setup()
    _L0_xattn_in = {k: v for k, v in _L0_xattn_all.items() if k in ('ln1_s', 'ln1_b', 'w_qkv', 'b_qkv', 'w_ao', 'b_ao', 'ln2_s', 'ln2_b', 'w_q', 'b_q', 'w_kv', 'b_kv', 'w_co', 'b_co', 'ln3_s', 'ln3_b', 'w1', 'b1', 'w2', 'b2')}
    del _L0_xattn_all

    def _L1_xattn_setup():
        import jax, jax.numpy as jnp
        import numpy as np
        B, Q, S1, S2 = (4, 32, 256, 256)
        D, H, K, F = (256, 16, 128, 1024)
        LN_EPS = 1e-05

        def _layer_norm(x, scale, offset):
            mu = jnp.mean(x, axis=-1, keepdims=True)
            var = jnp.var(x, axis=-1, keepdims=True)
            return (x - mu) * jax.lax.rsqrt(var + LN_EPS) * scale + offset

        def _cross_attention(q_in, kv_in, wq, bq, wk, bk, wv, bv, wo, bo, bias_k, bias_v):
            b, q_len, _ = q_in.shape
            t = kv_in.shape[1]
            qh = (q_in @ wq + bq).reshape(b, q_len, H, K)
            kh = (kv_in @ wk + bk).reshape(b, t, H, K)
            vh = (kv_in @ wv + bv).reshape(b, t, H, K)
            kh = jnp.concatenate([kh, jnp.broadcast_to(bias_k, (b, 1, H, K))], axis=1)
            vh = jnp.concatenate([vh, jnp.broadcast_to(bias_v, (b, 1, H, K))], axis=1)
            scale = jnp.sqrt(jnp.asarray(K, q_in.dtype))
            logits = jnp.einsum('bqhk,bthk->bhqt', qh, kh) / scale
            weights = jax.nn.softmax(logits, axis=-1)
            ctx = jnp.einsum('bhqt,bthk->bqhk', weights, vh).reshape(b, q_len, H * K)
            return ctx @ wo + bo

        def _forward(x, xf_1, xf_2, ln1_scale, ln1_offset, wq1, bq1, wk1, bk1, wv1, bv1, wo1, bo1, bias_k1, bias_v1, ln2_scale, ln2_offset, wq2, bq2, wk2, bk2, wv2, bv2, wo2, bo2, bias_k2, bias_v2, ln_mlp_scale, ln_mlp_offset, w_fc1, b_fc1, w_fc2, b_fc2):
            res = x
            h = _layer_norm(x, ln1_scale, ln1_offset)
            x = res + _cross_attention(h, xf_1, wq1, bq1, wk1, bk1, wv1, bv1, wo1, bo1, bias_k1, bias_v1)
            res = x
            h = _layer_norm(x, ln2_scale, ln2_offset)
            x = res + _cross_attention(h, xf_2, wq2, bq2, wk2, bk2, wv2, bv2, wo2, bo2, bias_k2, bias_v2)
            h = _layer_norm(x, ln_mlp_scale, ln_mlp_offset)
            h = jax.nn.gelu(h @ w_fc1 + b_fc1, approximate=False) @ w_fc2 + b_fc2
            return x + h
        key = jax.random.key(seed)
        ks = iter(jax.random.split(key, 64))

        def rn(shape, s=0.02):
            return jax.random.normal(next(ks), shape, jnp.float32) * s
        inp = {'x': rn((B, Q, D), 1.0), 'xf_1': rn((B, S1, D), 1.0), 'xf_2': rn((B, S2, D), 1.0)}
        for i in (1, 2):
            inp[f'ln{i}_scale'] = jnp.ones((D,), jnp.float32)
            inp[f'ln{i}_offset'] = jnp.zeros((D,), jnp.float32)
            inp[f'wq{i}'] = rn((D, H * K))
            inp[f'bq{i}'] = jnp.zeros((H * K,), jnp.float32)
            inp[f'wk{i}'] = rn((D, H * K))
            inp[f'bk{i}'] = jnp.zeros((H * K,), jnp.float32)
            inp[f'wv{i}'] = rn((D, H * K))
            inp[f'bv{i}'] = jnp.zeros((H * K,), jnp.float32)
            inp[f'wo{i}'] = rn((H * K, D))
            inp[f'bo{i}'] = jnp.zeros((D,), jnp.float32)
            inp[f'bias_k{i}'] = rn((1, 1, H, K))
            inp[f'bias_v{i}'] = rn((1, 1, H, K))
        inp['ln_mlp_scale'] = jnp.ones((D,), jnp.float32)
        inp['ln_mlp_offset'] = jnp.zeros((D,), jnp.float32)
        inp['w_fc1'] = rn((D, F))
        inp['b_fc1'] = jnp.zeros((F,), jnp.float32)
        inp['w_fc2'] = rn((F, D))
        inp['b_fc2'] = jnp.zeros((D,), jnp.float32)
        return inp
    _L1_xattn_all = _L1_xattn_setup()
    _L1_xattn_in = {k: v for k, v in _L1_xattn_all.items() if k in ('ln1_scale', 'ln1_offset', 'wq1', 'bq1', 'wk1', 'bk1', 'wv1', 'bv1', 'wo1', 'bo1', 'bias_k1', 'bias_v1', 'ln2_scale', 'ln2_offset', 'wq2', 'bq2', 'wk2', 'bk2', 'wv2', 'bv2', 'wo2', 'bo2', 'bias_k2', 'bias_v2', 'ln_mlp_scale', 'ln_mlp_offset', 'w_fc1', 'b_fc1', 'w_fc2', 'b_fc2')}
    del _L1_xattn_all
    return {'x': x, 'ctx_2048': ctx_2048, 'mask_1x1xSxS2_fc1': mask_1x1xSxS2_fc1, 'mask_Bx1xSxS2_ff1': mask_Bx1xSxS2_ff1, 'L0_xattn_ln1_s': _L0_xattn_in['ln1_s'], 'L0_xattn_ln1_b': _L0_xattn_in['ln1_b'], 'L0_xattn_w_qkv': _L0_xattn_in['w_qkv'], 'L0_xattn_b_qkv': _L0_xattn_in['b_qkv'], 'L0_xattn_w_ao': _L0_xattn_in['w_ao'], 'L0_xattn_b_ao': _L0_xattn_in['b_ao'], 'L0_xattn_ln2_s': _L0_xattn_in['ln2_s'], 'L0_xattn_ln2_b': _L0_xattn_in['ln2_b'], 'L0_xattn_w_q': _L0_xattn_in['w_q'], 'L0_xattn_b_q': _L0_xattn_in['b_q'], 'L0_xattn_w_kv': _L0_xattn_in['w_kv'], 'L0_xattn_b_kv': _L0_xattn_in['b_kv'], 'L0_xattn_w_co': _L0_xattn_in['w_co'], 'L0_xattn_b_co': _L0_xattn_in['b_co'], 'L0_xattn_ln3_s': _L0_xattn_in['ln3_s'], 'L0_xattn_ln3_b': _L0_xattn_in['ln3_b'], 'L0_xattn_w1': _L0_xattn_in['w1'], 'L0_xattn_b1': _L0_xattn_in['b1'], 'L0_xattn_w2': _L0_xattn_in['w2'], 'L0_xattn_b2': _L0_xattn_in['b2'], 'L1_xattn_ln1_scale': _L1_xattn_in['ln1_scale'], 'L1_xattn_ln1_offset': _L1_xattn_in['ln1_offset'], 'L1_xattn_wq1': _L1_xattn_in['wq1'], 'L1_xattn_bq1': _L1_xattn_in['bq1'], 'L1_xattn_wk1': _L1_xattn_in['wk1'], 'L1_xattn_bk1': _L1_xattn_in['bk1'], 'L1_xattn_wv1': _L1_xattn_in['wv1'], 'L1_xattn_bv1': _L1_xattn_in['bv1'], 'L1_xattn_wo1': _L1_xattn_in['wo1'], 'L1_xattn_bo1': _L1_xattn_in['bo1'], 'L1_xattn_bias_k1': _L1_xattn_in['bias_k1'], 'L1_xattn_bias_v1': _L1_xattn_in['bias_v1'], 'L1_xattn_ln2_scale': _L1_xattn_in['ln2_scale'], 'L1_xattn_ln2_offset': _L1_xattn_in['ln2_offset'], 'L1_xattn_wq2': _L1_xattn_in['wq2'], 'L1_xattn_bq2': _L1_xattn_in['bq2'], 'L1_xattn_wk2': _L1_xattn_in['wk2'], 'L1_xattn_bk2': _L1_xattn_in['bk2'], 'L1_xattn_wv2': _L1_xattn_in['wv2'], 'L1_xattn_bv2': _L1_xattn_in['bv2'], 'L1_xattn_wo2': _L1_xattn_in['wo2'], 'L1_xattn_bo2': _L1_xattn_in['bo2'], 'L1_xattn_bias_k2': _L1_xattn_in['bias_k2'], 'L1_xattn_bias_v2': _L1_xattn_in['bias_v2'], 'L1_xattn_ln_mlp_scale': _L1_xattn_in['ln_mlp_scale'], 'L1_xattn_ln_mlp_offset': _L1_xattn_in['ln_mlp_offset'], 'L1_xattn_w_fc1': _L1_xattn_in['w_fc1'], 'L1_xattn_b_fc1': _L1_xattn_in['b_fc1'], 'L1_xattn_w_fc2': _L1_xattn_in['w_fc2'], 'L1_xattn_b_fc2': _L1_xattn_in['b_fc2']}

def reference(x, ctx_2048, mask_1x1xSxS2_fc1, mask_Bx1xSxS2_ff1, L0_xattn_ln1_s, L0_xattn_ln1_b, L0_xattn_w_qkv, L0_xattn_b_qkv, L0_xattn_w_ao, L0_xattn_b_ao, L0_xattn_ln2_s, L0_xattn_ln2_b, L0_xattn_w_q, L0_xattn_b_q, L0_xattn_w_kv, L0_xattn_b_kv, L0_xattn_w_co, L0_xattn_b_co, L0_xattn_ln3_s, L0_xattn_ln3_b, L0_xattn_w1, L0_xattn_b1, L0_xattn_w2, L0_xattn_b2, L1_xattn_ln1_scale, L1_xattn_ln1_offset, L1_xattn_wq1, L1_xattn_bq1, L1_xattn_wk1, L1_xattn_bk1, L1_xattn_wv1, L1_xattn_bv1, L1_xattn_wo1, L1_xattn_bo1, L1_xattn_bias_k1, L1_xattn_bias_v1, L1_xattn_ln2_scale, L1_xattn_ln2_offset, L1_xattn_wq2, L1_xattn_bq2, L1_xattn_wk2, L1_xattn_bk2, L1_xattn_wv2, L1_xattn_bv2, L1_xattn_wo2, L1_xattn_bo2, L1_xattn_bias_k2, L1_xattn_bias_v2, L1_xattn_ln_mlp_scale, L1_xattn_ln_mlp_offset, L1_xattn_w_fc1, L1_xattn_b_fc1, L1_xattn_w_fc2, L1_xattn_b_fc2):
    import jax
    import jax.numpy as jnp

    def _L0_xattn_ref(hidden_states, encoder_states, ltor_mask, cross_mask, ln1_s, ln1_b, w_qkv, b_qkv, w_ao, b_ao, ln2_s, ln2_b, w_q, b_q, w_kv, b_kv, w_co, b_co, ln3_s, ln3_b, w1, b1, w2, b2):
        import jax, jax.numpy as jnp
        import numpy as np
        H = 256
        NH = 16
        HD = H // NH
        EPS = 1e-05

        def gelu(x):
            return 0.5 * x * (1.0 + jnp.tanh(0.7978845608028654 * x * (1.0 + 0.044715 * x * x)))

        def layernorm(x, scale, bias):
            m = jnp.mean(x, axis=-1, keepdims=True)
            v = jnp.mean(jnp.square(x - m), axis=-1, keepdims=True)
            return (x - m) * jax.lax.rsqrt(v + EPS) * scale + bias

        def split_heads(x):
            b, s, _ = x.shape
            return x.reshape(b, s, NH, HD).transpose(0, 2, 1, 3)

        def merge_heads(x):
            b, nh, s, hd = x.shape
            return x.transpose(0, 2, 1, 3).reshape(b, s, nh * hd)

        def attention(q, k, v, mask):
            scores = jnp.einsum('bhqd,bhkd->bhqk', q, k) / jnp.sqrt(jnp.float32(HD))
            scores = scores * mask - 10000.0 * (1.0 - mask)
            probs = jax.nn.softmax(scores, axis=-1)
            return jnp.einsum('bhqk,bhkd->bhqd', probs, v)
        ln_out = layernorm(hidden_states, ln1_s, ln1_b)
        qkv = ln_out @ w_qkv + b_qkv
        q, k, v = jnp.split(qkv, 3, axis=-1)
        ctx = merge_heads(attention(split_heads(q), split_heads(k), split_heads(v), ltor_mask))
        attn_out = ctx @ w_ao + b_ao
        x = hidden_states + attn_out
        ln_out = layernorm(x, ln2_s, ln2_b)
        q = ln_out @ w_q + b_q
        kv = encoder_states @ w_kv + b_kv
        k, v = jnp.split(kv, 2, axis=-1)
        ctx = merge_heads(attention(split_heads(q), split_heads(k), split_heads(v), cross_mask))
        cross_out = ctx @ w_co + b_co
        x = x + cross_out
        ln_out = layernorm(x, ln3_s, ln3_b)
        mlp_out = gelu(ln_out @ w1 + b1) @ w2 + b2
        return x + mlp_out

    def _L1_xattn_ref(x, xf_1, xf_2, ln1_scale, ln1_offset, wq1, bq1, wk1, bk1, wv1, bv1, wo1, bo1, bias_k1, bias_v1, ln2_scale, ln2_offset, wq2, bq2, wk2, bk2, wv2, bv2, wo2, bo2, bias_k2, bias_v2, ln_mlp_scale, ln_mlp_offset, w_fc1, b_fc1, w_fc2, b_fc2):
        import jax, jax.numpy as jnp
        import numpy as np
        B, Q, S1, S2 = (4, 32, 256, 256)
        D, H, K, F = (256, 16, 128, 1024)
        LN_EPS = 1e-05

        def _layer_norm(x, scale, offset):
            mu = jnp.mean(x, axis=-1, keepdims=True)
            var = jnp.var(x, axis=-1, keepdims=True)
            return (x - mu) * jax.lax.rsqrt(var + LN_EPS) * scale + offset

        def _cross_attention(q_in, kv_in, wq, bq, wk, bk, wv, bv, wo, bo, bias_k, bias_v):
            b, q_len, _ = q_in.shape
            t = kv_in.shape[1]
            qh = (q_in @ wq + bq).reshape(b, q_len, H, K)
            kh = (kv_in @ wk + bk).reshape(b, t, H, K)
            vh = (kv_in @ wv + bv).reshape(b, t, H, K)
            kh = jnp.concatenate([kh, jnp.broadcast_to(bias_k, (b, 1, H, K))], axis=1)
            vh = jnp.concatenate([vh, jnp.broadcast_to(bias_v, (b, 1, H, K))], axis=1)
            scale = jnp.sqrt(jnp.asarray(K, q_in.dtype))
            logits = jnp.einsum('bqhk,bthk->bhqt', qh, kh) / scale
            weights = jax.nn.softmax(logits, axis=-1)
            ctx = jnp.einsum('bhqt,bthk->bqhk', weights, vh).reshape(b, q_len, H * K)
            return ctx @ wo + bo

        def _forward(x, xf_1, xf_2, ln1_scale, ln1_offset, wq1, bq1, wk1, bk1, wv1, bv1, wo1, bo1, bias_k1, bias_v1, ln2_scale, ln2_offset, wq2, bq2, wk2, bk2, wv2, bv2, wo2, bo2, bias_k2, bias_v2, ln_mlp_scale, ln_mlp_offset, w_fc1, b_fc1, w_fc2, b_fc2):
            res = x
            h = _layer_norm(x, ln1_scale, ln1_offset)
            x = res + _cross_attention(h, xf_1, wq1, bq1, wk1, bk1, wv1, bv1, wo1, bo1, bias_k1, bias_v1)
            res = x
            h = _layer_norm(x, ln2_scale, ln2_offset)
            x = res + _cross_attention(h, xf_2, wq2, bq2, wk2, bk2, wv2, bv2, wo2, bo2, bias_k2, bias_v2)
            h = _layer_norm(x, ln_mlp_scale, ln_mlp_offset)
            h = jax.nn.gelu(h @ w_fc1 + b_fc1, approximate=False) @ w_fc2 + b_fc2
            return x + h
        return _forward(x, xf_1, xf_2, ln1_scale, ln1_offset, wq1, bq1, wk1, bk1, wv1, bv1, wo1, bo1, bias_k1, bias_v1, ln2_scale, ln2_offset, wq2, bq2, wk2, bk2, wv2, bv2, wo2, bo2, bias_k2, bias_v2, ln_mlp_scale, ln_mlp_offset, w_fc1, b_fc1, w_fc2, b_fc2)
    x = _L0_xattn_ref(x, ctx_2048, mask_1x1xSxS2_fc1, mask_Bx1xSxS2_ff1, L0_xattn_ln1_s, L0_xattn_ln1_b, L0_xattn_w_qkv, L0_xattn_b_qkv, L0_xattn_w_ao, L0_xattn_b_ao, L0_xattn_ln2_s, L0_xattn_ln2_b, L0_xattn_w_q, L0_xattn_b_q, L0_xattn_w_kv, L0_xattn_b_kv, L0_xattn_w_co, L0_xattn_b_co, L0_xattn_ln3_s, L0_xattn_ln3_b, L0_xattn_w1, L0_xattn_b1, L0_xattn_w2, L0_xattn_b2)
    x = _L1_xattn_ref(x, ctx_2048, ctx_2048, L1_xattn_ln1_scale, L1_xattn_ln1_offset, L1_xattn_wq1, L1_xattn_bq1, L1_xattn_wk1, L1_xattn_bk1, L1_xattn_wv1, L1_xattn_bv1, L1_xattn_wo1, L1_xattn_bo1, L1_xattn_bias_k1, L1_xattn_bias_v1, L1_xattn_ln2_scale, L1_xattn_ln2_offset, L1_xattn_wq2, L1_xattn_bq2, L1_xattn_wk2, L1_xattn_bk2, L1_xattn_wv2, L1_xattn_bv2, L1_xattn_wo2, L1_xattn_bo2, L1_xattn_bias_k2, L1_xattn_bias_v2, L1_xattn_ln_mlp_scale, L1_xattn_ln_mlp_offset, L1_xattn_w_fc1, L1_xattn_b_fc1, L1_xattn_w_fc2, L1_xattn_b_fc2)
    return x

_drawn_inputs = setup_inputs


def setup_inputs(seed=0):
    import zlib

    import numpy as np

    out = dict(_drawn_inputs(seed))
    spreads = {'L0_xattn_ln1_s': (1.0, 0.6),
     'L0_xattn_ln1_b': (0.0, 0.799),
     'L0_xattn_b_qkv': (0.0, 0.284),
     'L0_xattn_b_ao': (0.0, 0.1),
     'L0_xattn_ln2_s': (1.0, 0.6),
     'L0_xattn_ln2_b': (0.0, 2.0),
     'L0_xattn_b_q': (0.0, 2.0),
     'L0_xattn_b_kv': (0.0, 0.295),
     'L0_xattn_b_co': (0.0, 0.1),
     'L0_xattn_ln3_s': (1.0, 0.6),
     'L0_xattn_ln3_b': (0.0, 0.689),
     'L0_xattn_b1': (0.0, 0.284),
     'L0_xattn_b2': (0.0, 0.1),
     'L1_xattn_ln1_scale': (1.0, 0.6),
     'L1_xattn_ln1_offset': (0.0, 0.8),
     'L1_xattn_bq1': (0.0, 0.8),
     'L1_xattn_bk1': (0.0, 2.0),
     'L1_xattn_bv1': (0.0, 0.1),
     'L1_xattn_bo1': (0.0, 0.1),
     'L1_xattn_ln2_scale': (1.0, 0.6),
     'L1_xattn_ln2_offset': (0.0, 0.8),
     'L1_xattn_bq2': (0.0, 0.8),
     'L1_xattn_bk2': (0.0, 2.0),
     'L1_xattn_bv2': (0.0, 0.1),
     'L1_xattn_bo2': (0.0, 0.1),
     'L1_xattn_ln_mlp_scale': (1.0, 0.6),
     'L1_xattn_ln_mlp_offset': (0.0, 0.689),
     'L1_xattn_b_fc1': (0.0, 0.282),
     'L1_xattn_b_fc2': (0.0, 0.1)}
    factors = {'L0_xattn_w_qkv': 4.874,
     'L0_xattn_w_q': 8.0,
     'L1_xattn_wq1': 8.0,
     'L1_xattn_wk1': 8.0,
     'L1_xattn_bias_k1': 64.0,
     'L1_xattn_bias_v1': 64.0,
     'L1_xattn_wq2': 8.0,
     'L1_xattn_wk2': 8.0,
     'L1_xattn_bias_k2': 64.0,
     'L1_xattn_bias_v2': 64.0}
    for name, (base, spread) in spreads.items():
        noise = np.random.default_rng([zlib.crc32(name.encode()), seed]).standard_normal(out[name].shape)
        drawn = base * np.exp(spread * noise) if base else spread * noise
        out[name] = jnp.asarray(drawn.astype(out[name].dtype))
    for name, factor in factors.items():
        out[name] = (out[name] * factor).astype(out[name].dtype)
    return out
```

```python
from contextlib import ExitStack

import concourse.bass as bass
import concourse.mybir as mybir

P = 128
B, S, D = 4, 256, 256
TOK = B * S
NT = TOK // P
KD = D // P
QT = S // P
H0, HD0 = 16, 16
H1, HD1 = 16, 128
FF = 1024
NF = FF // P
CH = 512
PAIRS = H1 // 2
PH = 2
STEPS = 2 * B
EPS = 1e-5
MASKED = 10000.0
SP = S + 2

VEC = {}
_at = 0
for _name, _n in (("ln1_s", 2), ("ln1_b", 2), ("bq_s", 2), ("bk_s", 2), ("bv_s", 2), ("ln2_s", 2), ("ln2_b", 2),
                  ("bq_c", 2), ("bk_c", 2), ("bv_c", 2), ("ln3_s", 2), ("ln3_b", 2), ("b1", 8),
                  ("lnx_s", 4), ("lnx_b", 4), ("bq", 32), ("bk", 32), ("bias_k", 32), ("bias_v", 32),
                  ("lnm_s", 2), ("lnm_b", 2), ("b_fc1", 8)):
    VEC[_name] = _at
    _at += _n
NVEC = _at
ROWS = ("b_ao", "b_co", "b2", "bo1", "bo2", "b_fc2")


def build(nc, x_in, enc_in, mask_self, mask_cross, consts, vec_in, row_in, w_qkv_in, w_ao_in, w_q_in, w_kv_in,
          w_co_in, w1_in, w2_in, wf1_in, wf2_in, wqk_in, wv_in, wo_in, vb_in, out):
    f32, f32r = mybir.dt.float32, mybir.dt.float32r
    ALU = mybir.AluOpType
    ACT = mybir.ActivationFunctionType
    AX = mybir.AxisListType
    ds = bass.ds

    with ExitStack() as ctx:
        def sb(name, shape, dt=f32):
            return in_turn.enter_context(nc.sbuf_tensor(name, shape, dt))

        def sem(name):
            return ctx.enter_context(nc.semaphore(name))

        in_turn = ctx
        x_acc = sb("x_acc", [P, NT, D])
        encT = sb("encT", [P, KD, TOK], f32)
        encTh = sb("encTh", [P, KD, TOK], f32r)
        encTl = sb("encTl", [P, KD, TOK], f32r)
        const = sb("const", [P, P + 2])
        ident = const[:, 0:P]
        even_odd = [const[:, P + e:P + e + 1] for e in range(2)]
        vec = sb("vec", [P, NVEC])
        row = sb("row", [1, len(ROWS), D])
        ones = sb("ones", [1, P])
        neg_half = sb("neg_half", [P, NT])
        stats = sb("stats", [P, NT, 6])
        mean_var = sb("mean_var", [P, NT, 2])
        var_eps = sb("var_eps", [P, NT])
        rstd = sb("rstd", [P, NT])
        xn = sb("xn", [P, NT, D])
        w_up = sb("w_up", [P, KD, FF])
        w_down = sb("w_down", [P, NF, D])
        hT = sb("hT", [P, KD, TOK])
        raw_qk = [sb(f"raw_qk{i}", [P, 2, KD, HD1]) for i in range(2)]
        raw_v = sb("raw_v", [P, KD, 2 * HD1])
        raw_o = sb("raw_o", [P, 2, D])
        raw_vb = sb("raw_vb", [P, 2, 2 * HD1])
        bkh = sb("bkh", [P, PH * H1], f32r)
        bkl = sb("bkl", [P, PH * H1], f32r)
        in_turn = ExitStack()
        gelu = sb("gelu", [P, NF, CH])
        in_turn.close()
        in_turn = ctx
        ch = sb("ch", [P, 2, TOK], f32r)
        cl = sb("cl", [P, 2, TOK], f32r)
        first = ExitStack()
        in_turn = first
        w_qkv = sb("w_qkv", [P, KD, 3 * D])
        w_ao = sb("w_ao", [P, KD, D])
        w_q = sb("w_q", [P, KD, D])
        w_kv = sb("w_kv", [P, KD, 2 * D])
        w_co = sb("w_co", [P, KD, D])
        hb = sb("hb", [P, KD, S])
        encb = sb("encb", [P, KD, S])
        q0 = sb("q0", [P, KD, S])
        k0 = [sb(f"k0_{e}", [P, KD, S]) for e in range(2)]
        v0 = sb("v0", [P, QT, H0, HD0 + 1])
        msk = [sb("msk_s", [P, QT, S]), sb("msk_c", [P, QT, S])]
        pen = [sb("pen_s", [P, QT, S]), sb("pen_c", [P, QT, S])]
        tm = [sb(f"tm{i}", [P, QT, S]) for i in range(2)]
        um = [sb(f"um{i}", [P, QT, S]) for i in range(2)]
        umin = sb("umin", [P, 2, QT])
        p0 = [sb(f"p0_{i}", [P, QT, S]) for i in range(2)]
        pt0 = [sb(f"pt0_{i}", [P, QT, S]) for i in range(2)]
        rsum0 = sb("rsum0", [P, QT, H0])
        cn0 = sb("cn0", [P, QT, H0, HD0])
        ct0 = sb("ct0", [P, KD, S])
        first.close()
        in_turn = ctx
        hTh = sb("hTh", [P, KD, TOK], f32r)
        hTl = sb("hTl", [P, KD, TOK], f32r)
        wqk_h = [sb(f"wqk_h{i}", [P, 2, KD, HD1], f32r) for i in range(2)]
        wqk_l = [sb(f"wqk_l{i}", [P, 2, KD, HD1], f32r) for i in range(2)]
        wv_h = sb("wv_h", [P, KD, 2 * HD1], f32r)
        wv_l = sb("wv_l", [P, KD, 2 * HD1], f32r)
        wo_h = sb("wo_h", [P, 2, D], f32r)
        wo_l = sb("wo_l", [P, 2, D], f32r)
        v_bias = sb("v_bias", [P, 2 * HD1])
        qh = sb("qh", [P, 2, TOK], f32r)
        ql = sb("ql", [P, 2, TOK], f32r)
        kh = sb("kh", [P, 2, B, SP], f32r)
        kl = sb("kl", [P, 2, B, SP], f32r)
        vt = [sb(f"vt{i}", [P, 2, 2 * HD1]) for i in range(2)]
        vh = sb("vh", [P, NT, 2 * HD1], f32r)
        vl = sb("vl", [P, NT, 2 * HD1], f32r)
        mx = sb("mx", [P, 4, QT])
        nm = sb("nm", [P, 4, QT])
        sums = sb("sums", [P, 4, QT])
        rs = sb("rs", [P, 4, QT])
        pr = [sb(f"pr{i}", [P, QT, S + 1]) for i in range(4)]
        pn = [sb(f"pn{i}", [P, QT, S]) for i in range(2)]
        pth = [sb(f"pth{i}", [P, QT, S], f32r) for i in range(2)]
        ptl = [sb(f"ptl{i}", [P, QT, S], f32r) for i in range(2)]

        bank = [ctx.enter_context(nc.psum_tensor(f"bank{i}", [P, CH], f32)) for i in range(8)]

        d_x, d_enc, d_const, d_vec, d_row = sem("d_x"), sem("d_enc"), sem("d_const"), sem("d_vec"), sem("d_row")
        d_ms, d_mc, d_w0, d_up = sem("d_ms"), sem("d_mc"), sem("d_w0"), sem("d_up")
        d_up2 = sem("d_up2")
        d_qk = [sem("d_qk0"), sem("d_qk1")]
        d_v, d_o, d_vb, d_out = sem("d_v"), sem("d_o"), sem("d_vb"), sem("d_out")
        init = sem("init")
        enc_mm, enc_ev = sem("enc_mm"), sem("enc_ev")
        enc_hi, enc_lo = sem("enc_hi"), sem("enc_lo")
        ln_st, ln_mv, ln_eps, ln_rstd, ln_xn = (sem(n) for n in ("ln_st", "ln_mv", "ln_eps", "ln_rstd", "ln_xn"))
        ln_mm, ln_ev = sem("ln_mm"), sem("ln_ev")
        hsp = sem("hsp")
        a_encb, a_pen = sem("a_encb"), sem("a_pen")
        a_qmm, a_qev, a_kmm, a_kev, a_vmm, a_vev = (sem(n) for n in ("a_qmm", "a_qev", "a_kmm", "a_kev", "a_vmm", "a_vev"))
        a_s, a_t, a_u, a_p, a_tmm, a_tev, a_pv = (sem(n) for n in ("a_s", "a_t", "a_u", "a_p", "a_tmm", "a_tev", "a_pv"))
        a_rs, a_cn, a_cmm, a_cev, a_omm, a_x = (sem(n) for n in ("a_rs", "a_cn", "a_cmm", "a_cev", "a_omm", "a_x"))
        m_up, m_gelu, m_down, m_x = (sem(n) for n in ("m_up", "m_gelu", "m_down", "m_x"))
        w_qk, w_v, w_o, w_vb, kb = (sem(n) for n in ("w_qk", "w_v", "w_o", "w_vb", "kb"))
        g_mm, g_hi, g_lo = sem("g_mm"), sem("g_hi"), sem("g_lo")
        v_mm, v_t, v_hi, v_lo = sem("v_mm"), sem("v_t"), sem("v_hi"), sem("v_lo")
        s_mm, s_max, s_nm, s_exp, s_rs, s_pn = (sem(n) for n in ("s_mm", "s_max", "s_nm", "s_exp", "s_rs", "s_pn"))
        t_mm, t_hi, t_lo = sem("t_mm"), sem("t_hi"), sem("t_lo")
        pv_mm, c_hi, c_lo = sem("pv_mm"), sem("c_hi"), sem("c_lo")
        o_mm, o_x = sem("o_mm"), sem("o_x")

        def col(name, i=0):
            return vec[:, ds(VEC[name] + i, 1)]

        def ln_l0(b, k):
            return (2 * b + k, 4 * b + 2 * k, QT, 2 * b)
        LN_MLP0 = (2 * B, 4 * B, NT, 0)

        def ln_l1(ph):
            return (2 * B + 1 + ph, 4 * B + NT + ph * NT, NT, 0)
        LN_MLP1 = (2 * B + 1 + PH, 4 * B + NT * (1 + PH), NT, 0)

        def held(eng, reg, value):
            if isinstance(value, int):
                return value
            eng.reg_mov(reg, value)
            return reg

        block = ctx.enter_context(nc.Block())

        @block.sync
        def _(sp):
            count_reg = sp.alloc_register()
            sp.dma_start(x_acc[:, :, :], x_in.rearrange("(t p) d -> p t d", p=P)).then_inc(d_x, 16)
            sp.dma_start(xn[:, :, :], enc_in.rearrange("(t p) d -> p t d", p=P)).then_inc(d_enc, 16)
            for wt, src in ((w_qkv, w_qkv_in), (w_ao, w_ao_in), (w_q, w_q_in), (w_kv, w_kv_in), (w_co, w_co_in)):
                sp.dma_start(wt[:, :, :], src.rearrange("(k p) n -> p k n", p=P)).then_inc(d_w0, 16)
            sp.dma_start(msk[0][:, :, :], mask_self.rearrange("(t p) k -> p t k", p=P)).then_inc(d_ms, 16)
            sp.dma_start(msk[1][:, :, :], mask_cross[0:S, :].rearrange("(t p) k -> p t k", p=P)).then_inc(d_mc, 16)
            sp.dma_start(w_up[:, :, :], w1_in.rearrange("(k p) n -> p k n", p=P)).then_inc(d_up, 16)
            sp.dma_start(w_down[:, :, :], w2_in.rearrange("(k p) n -> p k n", p=P)).then_inc(d_up, 16)

            def load_pair(n, first):
                for i in range(2):
                    if not first:
                        sp.wait_ge(w_qk, n * 4 + 2 * i - 2)
                    sp.dma_start(raw_qk[i][:, :, :, :], wqk_in[ds(n * 2 + i, 1)].rearrange(
                        "a p (c k m) -> p (a c) k m", c=2, k=KD)).then_inc(d_qk[i], 16)
                    if i == 0:
                        if not first:
                            sp.wait_ge(w_v, n * 2)
                        sp.dma_start(raw_v[:, :, :], wv_in[ds(n, 1)].rearrange(
                            "a p (k m) -> p (a k) m", k=KD)).then_inc(d_v, 16)
                        if not first:
                            sp.wait_ge(w_vb, n)
                        sp.dma_start(raw_vb[:, :, :], vb_in[ds(n, 1)].rearrange(
                            "a (c m) -> a c m", c=2).to_broadcast([P, 2, 2 * HD1])).then_inc(d_vb, 16)
                if not first:
                    sp.wait_ge(w_o, n * 2)
                sp.dma_start(raw_o[:, :, :], wo_in[ds(n, 1)].rearrange(
                    "a p (c m) -> p (a c) m", c=2)).then_inc(d_o, 16)

            load_pair(0, True)
            with sp.Fori(1, B) as b:
                count = held(sp, count_reg, b + 1)
                sp.wait_ge(a_t, b * (2 * H0))
                sp.wait_ge(d_x, 16)
                sp.wait_ge(a_pen, count)
                sp.dma_start(msk[1][:, :, :], mask_cross[ds(b * S, S), :].rearrange(
                    "(t p) k -> p t k", p=P)).then_inc(d_mc, 16)
            sp.wait_ge(m_down, 4)
            sp.dma_start(w_up[:, :, :], wf1_in.rearrange("(k p) n -> p k n", p=P)).then_inc(d_up2, 16)
            sp.dma_start(w_down[:, :, :], wf2_in.rearrange("(k p) n -> p k n", p=P)).then_inc(d_up2, 16)
            with sp.Fori(1, PH * PAIRS) as n:
                load_pair(n, False)
            for j in range(NT // 2):
                sp.wait_ge(m_x, NT // 2 + j + 1)
                sp.dma_start(out[2 * j * P:(2 * j + 2) * P, :].rearrange("(t p) d -> p t d", p=P),
                             x_acc[:, 2 * j:2 * j + 2, :]).then_inc(d_out, 16)
            sp.wait_ge(d_out, 16 * (NT // 2))

        @block.gpsimd
        def _(pool):
            count_reg = pool.alloc_register()
            other_reg = pool.alloc_register()
            pool.dma_start(const[:, :], consts).then_inc(d_const, 16)
            pool.dma_start(vec[:, :], vec_in).then_inc(d_vec, 16)
            pool.dma_start(row[:, :, :], row_in).then_inc(d_row, 16)
            pool.memset(ones[:, :], 1.0).then_inc(init, 1)
            pool.memset(neg_half[:, :], -0.5).then_inc(init, 1)
            pool.memset(v0[:, :, :, HD0:HD0 + 1], 1.0).then_inc(init, 1)
            pool.wait_ge(init, 3)
            pool.wait_ge(d_vec, 16)
            pool.tensor_scalar(bkh[:, :], vec[:, VEC["bias_k"]:VEC["bias_k"] + PH * H1], 1.0, 1.0,
                               ALU.mult, ALU.mult).then_inc(init, 1)
            pool.wait_ge(init, 4)
            pool.tensor_tensor(bkl[:, :], vec[:, VEC["bias_k"]:VEC["bias_k"] + PH * H1], bkh[:, :],
                               ALU.subtract).then_inc(init, 1)
            pool.wait_ge(d_ms, 16)
            pool.tensor_scalar(pen[0][:, :, :], msk[0][:, :, :], -MASKED, MASKED, ALU.mult,
                               ALU.add).then_inc(a_pen, 1)

            def layer_norm(call):
                c, t0, n, _ = call
                count = held(pool, count_reg, t0 + n)
                pool.wait_ge(init, 3)
                pool.wait_ge(ln_mv, count)
                pool.tensor_scalar(var_eps[:, 0:n], mean_var[:, 0:n, 1], 1.0, EPS, ALU.mult,
                                   ALU.add).then_inc(ln_eps, 1)
                pool.wait_ge(ln_eps, c + 1)
                pool.tensor_tensor(rstd[:, 0:n], var_eps[:, 0:n], neg_half[:, 0:n], ALU.pow).then_inc(ln_rstd, 1)

            pool.wait_ge(enc_ev, 2 * NT // 2)
            with pool.Fori(0, B) as b:
                pool.wait_ge(a_vmm, b * 2)
                pool.tensor_copy(encb[:, :, :], encT[:, :, ds(b * S, S)]).then_inc(a_encb, 1)
                count = held(pool, count_reg, b * (4 * H0))
                loaded = held(pool, other_reg, b * 16 + 16)
                pool.wait_ge(init, 3)
                pool.wait_ge(d_mc, loaded)
                pool.wait_ge(a_u, count)
                pool.tensor_scalar(pen[1][:, :, :], msk[1][:, :, :], -MASKED, MASKED, ALU.mult,
                                   ALU.add).then_inc(a_pen, 1)
                layer_norm(ln_l0(b, 0))
                layer_norm(ln_l0(b, 1))
            pool.tensor_scalar(encTh[:, :, :], encT[:, :, :], 1.0, 1.0, ALU.mult, ALU.mult).then_inc(enc_hi, 1)
            pool.wait_ge(enc_hi, 1)
            pool.tensor_tensor(encTl[:, :, :], encT[:, :, :], encTh[:, :, :], ALU.subtract).then_inc(enc_lo, 1)
            layer_norm(LN_MLP0)

            def split_hi(hi, raw, s, inc=1):
                pool.tensor_scalar(hi, raw, 1.0, 1.0, ALU.mult, ALU.mult).then_inc(s, inc)

            def split_lo(lo, raw, hi, s):
                pool.tensor_tensor(lo, raw, hi, ALU.subtract).then_inc(s, 1)

            def qk_hi(n, i):
                count = held(pool, count_reg, n * 8 + 4 * i - 4)
                loaded = held(pool, other_reg, n * 16 + 16)
                pool.wait_ge(init, 3)
                pool.wait_ge(d_qk[i], loaded)
                pool.wait_ge(g_mm, count)
                split_hi(wqk_h[i][:, :, :, :], raw_qk[i][:, :, :, :], w_qk)

            def qk_lo(n, i):
                pool.wait_ge(w_qk, n * 4 + 2 * i + 1)
                split_lo(wqk_l[i][:, :, :, :], raw_qk[i][:, :, :, :], wqk_h[i][:, :, :, :], w_qk)

            def v_hi_(n):
                count = held(pool, count_reg, n * 4)
                loaded = held(pool, other_reg, n * 16 + 16)
                pool.wait_ge(init, 3)
                pool.wait_ge(d_v, loaded)
                pool.wait_ge(v_mm, count)
                split_hi(wv_h[:, :, :], raw_v[:, :, :], w_v)

            def v_lo_(n):
                pool.wait_ge(w_v, n * 2 + 1)
                split_lo(wv_l[:, :, :], raw_v[:, :, :], wv_h[:, :, :], w_v)

            def v_bias_(n):
                pool.wait_ge(d_vb, n * 16 + 16)
                pool.wait_ge(v_t, n * 4)
                split_lo(v_bias[:, :], raw_vb[:, 0, :], raw_vb[:, 1, :], w_vb)

            def o_hi_(n):
                count = held(pool, count_reg, n * 4)
                loaded = held(pool, other_reg, n * 16 + 16)
                pool.wait_ge(init, 3)
                pool.wait_ge(d_o, loaded)
                pool.wait_ge(o_mm, count)
                split_hi(wo_h[:, :, :], raw_o[:, :, :], w_o)

            def o_lo_(n):
                pool.wait_ge(w_o, n * 2 + 1)
                split_lo(wo_l[:, :, :], raw_o[:, :, :], wo_h[:, :, :], w_o)

            def key_bias(n, i, scores_done):
                if scores_done is not None:
                    pool.wait_ge(s_mm, scores_done)
                hd = n * 2 + i
                for dst, src in ((kh, bkh), (kl, bkl)):
                    pool.tensor_copy(dst[:, i, :, S:SP], src[:, ds(hd, 1)].unsqueeze(2).to_broadcast(
                        [P, B, 2])).then_inc(kb, 1)

            def norm(g, s):
                count = held(pool, count_reg, g + 1)
                if s >= 2:
                    turned = held(pool, other_reg, g - 1)
                pool.wait_ge(init, 3)
                if s >= 2:
                    pool.wait_ge(t_mm, turned)
                pool.wait_ge(s_rs, count)
                for t in range(QT):
                    pool.tensor_scalar(pn[s % 2][:, t, :], pr[s % 4][:, t, 0:S], rs[:, s % 4, t:t + 1], 1.0,
                                       ALU.mult, ALU.mult).then_inc(s_pn, 1)

            def pair(n, last):
                for j in range(B):
                    pool.wait_ge(v_hi, n * 4 + j + 1)
                    pool.tensor_tensor(vl[:, 2 * j:2 * j + 2, :], vt[j % 2][:, :, :], vh[:, 2 * j:2 * j + 2, :],
                                       ALU.subtract).then_inc(v_lo, 1)
                key_bias(n, 1, n * STEPS)
                for s in range(STEPS):
                    g = n * STEPS + s
                    if s == 4 and not last:
                        key_bias(n + 1, 0, g)
                    norm(g, s)
                    if not last:
                        if s == 0:
                            qk_hi(n + 1, 0)
                        if s == 1:
                            qk_lo(n + 1, 0)
                        if s == 2:
                            v_hi_(n + 1)
                        if s == 3:
                            v_lo_(n + 1)
                            v_bias_(n + 1)
                        if s == 4:
                            qk_hi(n + 1, 1)
                        if s == 5:
                            qk_lo(n + 1, 1)
                    if s == 6:
                        o_hi_(n)
                    if s == 7:
                        o_lo_(n)

            with pool.Fori(0, PH) as ph:
                n0 = ph * PAIRS
                key_bias(n0, 0, n0 * STEPS)
                count = held(pool, count_reg, n0 * 16 + 16)
                pool.wait_ge(init, 3)
                pool.wait_ge(d_qk[0], count)
                split_hi(wqk_h[0][:, :, :, :], raw_qk[0][:, :, :, :], w_qk)
                qk_lo(n0, 0)
                v_hi_(n0)
                v_lo_(n0)
                v_bias_(n0)
                count = held(pool, count_reg, n0 * 16 + 16)
                used = held(pool, other_reg, n0 * 8)
                pool.wait_ge(init, 3)
                pool.wait_ge(g_mm, used)
                pool.wait_ge(d_qk[1], count)
                split_hi(wqk_h[1][:, :, :, :], raw_qk[1][:, :, :, :], w_qk)
                qk_lo(n0, 1)
                layer_norm(ln_l1(ph))
                with pool.Fori(0, PAIRS - 1) as p:
                    pair(n0 + p, False)
                pair(n0 + (PAIRS - 1), True)
            layer_norm(LN_MLP1)

        @block.scalar
        def _(act):
            count_reg = act.alloc_register()
            act.wait_ge(d_vec, 16)

            def ln_out(call, dst, scale, offset):
                _, t0, n, _ = call
                for j in range(n // 2):
                    count = held(act, count_reg, t0 // 2 + j + 1)
                    act.wait_ge(d_vec, 16)
                    act.wait_ge(ln_mm, count)
                    for k in range(KD):
                        act.activation(dst[:, k, 2 * j * P:(2 * j + 2) * P], bank[6 + j % 2][:, k * S:(k + 1) * S],
                                       ACT.Identity, bias=offset(k), scale=scale(k)).then_inc(ln_ev, 1)

            def attention0(a, kind):
                act.wait_ge(a_vmm, a + 1)
                for t in range(QT):
                    act.activation(v0[:, t, :, 0:HD0], bank[5][:, t * D:(t + 1) * D].rearrange(
                        "p (h d) -> p h d", h=H0), ACT.Copy).then_inc(a_vev, 1)
                if kind == 1:
                    ln_cross()

                def probs(h):
                    g = a * H0 + h
                    act.wait_ge(a_u, g * 2 + 2)
                    for t in range(QT):
                        act.activation(p0[h % 2][:, t, :], um[h % 2][:, t, :], ACT.Exp, bias=umin[:, h % 2, t:t + 1],
                                       scale=-1.0).then_inc(a_p, 1)

                def pt(h):
                    act.wait_ge(a_tmm, a * H0 + h + 1)
                    act.activation(pt0[h % 2][:, :, :], bank[2 + h % 2][:, :], ACT.Copy).then_inc(a_tev, 1)

                for h in range(H0):
                    probs(h)
                    if h >= 1:
                        pt(h - 1)
                pt(H0 - 1)
                act.wait_ge(a_cmm, a + 1)
                for k in range(KD):
                    act.activation(ct0[:, k, :], bank[7][:, k * S:(k + 1) * S], ACT.Identity,
                                   bias=col(("bv_s", "bv_c")[kind], k), scale=1.0).then_inc(a_cev, 1)

            for j in range(NT // 2):
                act.wait_ge(enc_mm, j + 1)
                for k in range(KD):
                    act.activation(encT[:, k, 2 * j * P:(2 * j + 2) * P], bank[j % 2][:, k * S:(k + 1) * S],
                                   ACT.Copy).then_inc(enc_ev, 1)
            with act.Fori(0, B) as b:
                ln_out(ln_l0(b, 0), hb, lambda k: col("ln1_s", k), lambda k: col("ln1_b", k))
                attention0(b * 2, 0)

                def ln_cross():
                    ln_out(ln_l0(b, 1), hb, lambda k: col("ln2_s", k), lambda k: col("ln2_b", k))

                attention0(b * 2 + 1, 1)

            def mlp(call, m, func, scale, offset, bias):
                ln_out(call, hT, scale, offset)
                for c in range(TOK // CH):
                    for f in range(NF):
                        act.wait_ge(m_up, (2 * m + c) * NF + f + 1)
                        act.activation(gelu[:, f, :], bank[f % 4][:, :], func, bias=bias(f),
                                       scale=1.0).then_inc(m_gelu, 1)

            mlp(LN_MLP0, 0, ACT.Gelu_apprx_tanh, lambda k: col("ln3_s", k), lambda k: col("ln3_b", k),
                lambda f: col("b1", f))

            def group_hi(n, i, hd):
                slot, c, which = hd, (i % 4) // 2, i % 2
                return slot, c, which

            def proj_hi(grp, hh, i, head):
                c = i // 2
                count = held(act, count_reg, grp + 1)
                act.wait_ge(d_vec, 16)
                act.wait_ge(g_mm, count)
                if i % 2 == 0:
                    act.activation(qh[:, hh, c * CH:(c + 1) * CH], bank[6 + i % 2][:, :], ACT.Identity,
                                   bias=col("bq", head), scale=1.0).then_inc(g_hi, 1)
                else:
                    act.activation(kh[:, hh, 2 * c:2 * c + 2, 0:S], bank[6 + i % 2][:, :].rearrange(
                        "p (b s) -> p b s", b=2), ACT.Identity, bias=col("bk", head), scale=1.0).then_inc(g_hi, 1)

            def pt_hi(g, s):
                act.wait_ge(t_mm, g + 1)
                act.activation(pth[s % 2][:, :, :], bank[4][:, :], ACT.Copy).then_inc(t_hi, 1)

            def ctx_hi(g, s, n):
                hh, b = s // B, s % B
                count = held(act, count_reg, g + 1)
                act.wait_ge(d_vec, 16)
                act.wait_ge(pv_mm, count)
                act.activation(ch[:, hh, b * S:(b + 1) * S], bank[5][:, 0:S], ACT.Identity,
                               bias=col("bias_v", n * 2 + hh), scale=1.0).then_inc(c_hi, 1)

            def exps(g, s):
                act.wait_ge(s_nm, g + 1)
                for t in range(QT):
                    act.activation(pr[s % 4][:, t, :], bank[2 * (s % 2) + t][:, 0:S + 1], ACT.Exp,
                                   bias=nm[:, s % 4, t:t + 1], scale=float(HD1) ** -0.5,
                                   accum_out=sums[:, s % 4, t:t + 1]).then_inc(s_exp, 1)

            def tails(n):
                g = n * STEPS
                pt_hi(g + 6, 6)
                ctx_hi(g + 5, 5, n)
                pt_hi(g + 7, 7)
                ctx_hi(g + 6, 6, n)
                ctx_hi(g + 7, 7, n)

            def pair(n, first, last):
                if not first:
                    tails(n - 1)
                for j in range(B):
                    act.wait_ge(v_t, n * 4 + j + 1)
                    if j == 0:
                        act.wait_ge(pv_mm, n * STEPS)
                    act.activation(vh[:, 2 * j:2 * j + 2, :], vt[j % 2][:, :, :], ACT.Copy).then_inc(v_hi, 1)
                for s in range(STEPS):
                    g = n * STEPS + s
                    if s >= 2:
                        pt_hi(g - 2, s - 2)
                    exps(g, s)
                    if s < 4:
                        proj_hi(n * 8 + 4 + s, 1, s, n * 2 + 1)
                    elif not last:
                        proj_hi(n * 8 + 4 + s, 0, s - 4, n * 2 + 2)
                    if s >= 3:
                        ctx_hi(g - 3, s - 3, n)

            with act.Fori(0, PH) as ph:
                n0 = ph * PAIRS
                ln_out(ln_l1(ph), hT, lambda k: col("lnx_s", ph * 2 + k), lambda k: col("lnx_b", ph * 2 + k))
                act.wait_ge(ln_ev, ln_l1(ph)[1] + NT)
                act.activation(hTh[:, :, :], hT[:, :, :], ACT.Copy).then_inc(hsp, 1)
                for i in range(4):
                    proj_hi(n0 * 8 + i, 0, i, n0 * 2)
                pair(n0, True, False)
                with act.Fori(1, PAIRS - 1) as p:
                    pair(n0 + p, False, False)
                pair(n0 + (PAIRS - 1), False, True)
                tails(n0 + (PAIRS - 1))
            mlp(LN_MLP1, 1, ACT.Gelu, lambda k: col("lnm_s", k), lambda k: col("lnm_b", k),
                lambda f: col("b_fc1", f))

        @block.vector
        def _(dve):
            count_reg = dve.alloc_register()
            other_reg = dve.alloc_register()
            def layer_norm(call):
                c, t0, n, x0 = call
                for t in range(n):
                    dve.bn_stats(stats[:, t, :], x_acc[:, ds(x0 + t, 1), :].rearrange(
                        "p a d -> p (a d)")).then_inc(ln_st, 1)
                for t in range(n):
                    count = held(dve, count_reg, t0 + t + 1)
                    dve.wait_ge(d_x, 16)
                    dve.wait_ge(ln_st, count)
                    dve.bn_aggr(mean_var[:, t, :], stats[:, t, :]).then_inc(ln_mv, 1)
                dve.wait_ge(ln_rstd, c + 1)
                for t in range(n):
                    if t == 0:
                        dve.wait_ge(ln_mm, t0 // 2)
                    dve.tensor_scalar(xn[:, t, :], x_acc[:, ds(x0 + t, 1), :].rearrange("p a d -> p (a d)"),
                                      mean_var[:, t, 0:1], rstd[:, t:t + 1], ALU.subtract,
                                      ALU.mult).then_inc(ln_xn, 1)

            def attention0(a, kind, b):
                def keys():
                    dve.wait_ge(a_kmm, a + 1)
                    for e in range(2):
                        for m in range(KD):
                            dve.tensor_scalar(k0[e][:, m, :], bank[4][:, m * S:(m + 1) * S],
                                              col(("bk_s", "bk_c")[kind], m), even_odd[e], ALU.add,
                                              ALU.mult).then_inc(a_kev, 1)

                def queries():
                    dve.wait_ge(a_qmm, a + 1)
                    for m in range(KD):
                        dve.tensor_scalar(q0[:, m, :], bank[6][:, m * S:(m + 1) * S],
                                          col(("bq_s", "bq_c")[kind], m), -float(HD0) ** -0.5, ALU.add,
                                          ALU.mult).then_inc(a_qev, 1)

                def masked(h):
                    g = a * H0 + h
                    dve.wait_ge(a_s, g + 1)
                    dve.tensor_tensor(tm[h % 2][:, :, :].rearrange("p t k -> p (t k)"), bank[h % 2][:, :],
                                      msk[kind][:, :, :].rearrange("p t k -> p (t k)"), ALU.mult).then_inc(a_t, 1)
                    count = held(dve, count_reg, g + 1)
                    if h >= 2:
                        used = held(dve, other_reg, g * 2 - 2)
                    dve.wait_ge(a_pen, 1)
                    if h >= 2:
                        dve.wait_ge(a_p, used)
                    dve.wait_ge(a_t, count)
                    for t in range(QT):
                        dve.tensor_tensor_reduce(um[h % 2][:, t, :], tm[h % 2][:, t, :], pen[kind][:, t, :], 1.0,
                                                 3.0e38, ALU.add, ALU.min, umin[:, h % 2, t:t + 1]).then_inc(a_u, 1)

                if kind == 1:
                    keys()
                    layer_norm(ln_l0(b, 1))
                    queries()
                    dve.wait_ge(a_pen, b + 2)
                    dve.wait_ge(d_mc, b * 16 + 16)
                else:
                    keys_after = queries()
                    keys()
                for h in range(H0):
                    masked(h)
                dve.wait_ge(a_pv, (a + 1) * H0)
                for t in range(QT):
                    o = bank[4 + t][:, 0:H0 * (HD0 + 1)].rearrange("p (h d) -> p h d", h=H0)
                    dve.reciprocal(rsum0[:, t, :], o[:, :, HD0]).then_inc(a_rs, 1)
                for t in range(QT):
                    o = bank[4 + t][:, 0:H0 * (HD0 + 1)].rearrange("p (h d) -> p h d", h=H0)
                    dve.wait_ge(a_rs, a * 2 + t + 1)
                    dve.tensor_tensor(cn0[:, t, :, :], o[:, :, 0:HD0], rsum0[:, t, :].unsqueeze(2).to_broadcast(
                        [P, H0, HD0]), ALU.mult).then_inc(a_cn, 1)
                dve.wait_ge(a_omm, a + 1)
                xs = x_acc[:, ds(b * 2, QT), :]
                dve.tensor_tensor(xs, xs, bank[6][:, :].rearrange("p (t d) -> p t d", t=QT), ALU.add).then_inc(a_x, 1)
                dve.wait_ge(a_x, a + 1)

            dve.wait_ge(d_x, 16)
            dve.wait_ge(d_vec, 16)
            dve.wait_ge(d_const, 16)
            dve.wait_ge(a_pen, 1)
            dve.wait_ge(d_ms, 16)
            dve.wait_ge(enc_mm, NT // 2)
            with dve.Fori(0, B) as b:
                layer_norm(ln_l0(b, 0))
                attention0(b * 2, 0, b)
                attention0(b * 2 + 1, 1, b)

            def mlp(call, m):
                layer_norm(call)
                for c in range(TOK // CH):
                    for j in range(2):
                        g = 2 * (2 * m + c) + j
                        dve.wait_ge(m_down, g + 1)
                        xs = x_acc[:, 4 * c + 2 * j:4 * c + 2 * j + 2, :]
                        dve.tensor_tensor(xs, xs, bank[4 + j][:, :].rearrange("p (t d) -> p t d", t=2),
                                          ALU.add).then_inc(m_x, 1)

            mlp(LN_MLP0, 0)
            dve.wait_ge(m_x, NT // 2)

            def proj_lo(grp, hh, i, head):
                c = i // 2
                dve.wait_ge(g_hi, grp + 1)
                if i % 2 == 0:
                    dve.scalar_tensor_tensor(out=ql[:, hh, c * CH:(c + 1) * CH], in0=bank[6][:, :],
                                             scalar=col("bq", head), in1=qh[:, hh, c * CH:(c + 1) * CH],
                                             op0=ALU.add, op1=ALU.subtract).then_inc(g_lo, 1)
                else:
                    dve.scalar_tensor_tensor(out=kl[:, hh, 2 * c:2 * c + 2, 0:S],
                                             in0=bank[7][:, :].rearrange("p (b s) -> p b s", b=2),
                                             scalar=col("bk", head), in1=kh[:, hh, 2 * c:2 * c + 2, 0:S],
                                             op0=ALU.add, op1=ALU.subtract).then_inc(g_lo, 1)

            def pt_lo(g, s):
                dve.wait_ge(t_hi, g + 1)
                dve.tensor_tensor(ptl[s % 2][:, :, :].rearrange("p t k -> p (t k)"), bank[4][:, :],
                                  pth[s % 2][:, :, :].rearrange("p t k -> p (t k)"), ALU.subtract).then_inc(t_lo, 1)

            def ctx_lo(g, s, n):
                hh, b = s // B, s % B
                dve.wait_ge(c_hi, g + 1)
                dve.scalar_tensor_tensor(out=cl[:, hh, b * S:(b + 1) * S], in0=bank[5][:, 0:S],
                                         scalar=col("bias_v", n * 2 + hh), in1=ch[:, hh, b * S:(b + 1) * S],
                                         op0=ALU.add, op1=ALU.subtract).then_inc(c_lo, 1)

            def row_max(g, s):
                dve.wait_ge(s_mm, g + 1)
                for t in range(QT):
                    dve.tensor_reduce(mx[:, s % 4, t:t + 1], bank[2 * (s % 2) + t][:, 0:S + 1], AX.X,
                                      ALU.max).then_inc(s_max, 1)
                dve.wait_ge(s_max, g * 2 + 2)
                dve.tensor_scalar(nm[:, s % 4, :], mx[:, s % 4, :], -float(HD1) ** -0.5, None,
                                  ALU.mult).then_inc(s_nm, 1)

            def row_recip(g, s):
                dve.wait_ge(s_exp, g * 2 + 2)
                dve.reciprocal(rs[:, s % 4, :], sums[:, s % 4, :]).then_inc(s_rs, 1)

            def values(n, j):
                dve.wait_ge(v_mm, n * 4 + j + 1)
                if j == 0:
                    dve.wait_ge(w_vb, n + 1)
                if j >= 2:
                    dve.wait_ge(v_lo, n * 4 + j - 1)
                dve.tensor_tensor(vt[j % 2][:, :, :], bank[6 + j % 2][:, :].rearrange("p (t m) -> p t m", t=2),
                                  v_bias[:, :].unsqueeze(1).to_broadcast([P, 2, 2 * HD1]), ALU.add).then_inc(v_t, 1)

            def add_out(n):
                for j in range(B):
                    dve.wait_ge(o_mm, n * 4 + j + 1)
                    xs = x_acc[:, 2 * j:2 * j + 2, :]
                    dve.tensor_tensor(xs, xs, bank[6 + j % 2][:, :].rearrange("p (t d) -> p t d", t=2),
                                      ALU.add).then_inc(o_x, 1)

            def pair(n, first, last):
                g = n * STEPS
                if not first:
                    pt_lo(g - 2, 6)
                    ctx_lo(g - 3, 5, n - 1)
                values(n, 0)
                if not first:
                    pt_lo(g - 1, 7)
                    ctx_lo(g - 2, 6, n - 1)
                values(n, 1)
                if not first:
                    ctx_lo(g - 1, 7, n - 1)
                values(n, 2)
                values(n, 3)
                if not first:
                    add_out(n - 1)
                for s in range(STEPS):
                    g = n * STEPS + s
                    row_max(g, s)
                    if s >= 2:
                        pt_lo(g - 2, s - 2)
                    if s < 4:
                        proj_lo(n * 8 + 4 + s, 1, s, n * 2 + 1)
                    elif not last:
                        proj_lo(n * 8 + 4 + s, 0, s - 4, n * 2 + 2)
                    if s >= 3:
                        ctx_lo(g - 3, s - 3, n)
                    row_recip(g, s)

            with dve.Fori(0, PH) as ph:
                n0 = ph * PAIRS
                layer_norm(ln_l1(ph))
                dve.wait_ge(hsp, ph * 2 + 1)
                dve.tensor_tensor(hTl[:, :, :], hT[:, :, :], hTh[:, :, :], ALU.subtract).then_inc(hsp, 1)
                for i in range(4):
                    proj_lo(n0 * 8 + i, 0, i, n0 * 2)
                pair(n0, True, False)
                with dve.Fori(1, PAIRS - 1) as p:
                    pair(n0 + p, False, False)
                pair(n0 + (PAIRS - 1), False, True)
                g = (n0 + PAIRS) * STEPS
                pt_lo(g - 2, 6)
                ctx_lo(g - 3, 5, n0 + (PAIRS - 1))
                pt_lo(g - 1, 7)
                ctx_lo(g - 2, 6, n0 + (PAIRS - 1))
                ctx_lo(g - 1, 7, n0 + (PAIRS - 1))
                add_out(n0 + (PAIRS - 1))
                dve.wait_ge(o_x, (n0 + PAIRS) * 4)
            mlp(LN_MLP1, 1)

        @block.tensor
        def _(pe):
            count_reg = pe.alloc_register()
            pe.wait_ge(d_const, 16)
            pe.wait_ge(d_enc, 16)

            def transposes(src, j, bk, signal):
                for k in range(KD):
                    for t in range(2):
                        last = pe.transpose(bank[bk][:, k * S + t * P:k * S + (t + 1) * P],
                                            src[:, 2 * j + t, k * P:(k + 1) * P], ident)
                last.then_inc(signal, 1)

            for j in range(NT // 2):
                if j >= 2:
                    pe.wait_ge(enc_ev, 2 * (j - 1))
                transposes(xn, j, j % 2, enc_mm)

            def layer_norm(call):
                _, t0, n, _ = call
                for j in range(n // 2):
                    pe.wait_ge(ln_xn, t0 + 2 * j + 2)
                    if j >= 2:
                        pe.wait_ge(ln_ev, t0 + 2 * j - 2)
                    transposes(xn, j, 6 + j % 2, ln_mm)

            def mm_bias(dst, r, first=True):
                pe.matmul(dst, ones[0:1, :], row[0:1, ds(r, 1), :].rearrange("p a d -> p (a d)"),
                          start=first, stop=False)

            def attention0(a, kind):
                wsrc, koff, voff = ((w_qkv, D, 2 * D), (w_kv, 0, D))[kind]
                kv_src = (hb, encb)[kind]

                def keys():
                    for m in range(KD):
                        for k in range(KD):
                            last = pe.matmul(bank[4][:, m * S:(m + 1) * S], wsrc[:, k, koff + m * P:koff + (m + 1) * P],
                                             kv_src[:, k, :], start=(k == 0), stop=(k == KD - 1))
                    last.then_inc(a_kmm, 1)

                def vals():
                    for t in range(QT):
                        for k in range(KD):
                            last = pe.matmul(bank[5][:, t * D:(t + 1) * D], kv_src[:, k, t * P:(t + 1) * P],
                                             wsrc[:, k, voff:voff + D], start=(k == 0), stop=(k == KD - 1))
                    last.then_inc(a_vmm, 1)

                def queries():
                    wq = (w_qkv, w_q)[kind]
                    for m in range(KD):
                        for k in range(KD):
                            last = pe.matmul(bank[6][:, m * S:(m + 1) * S], wq[:, k, m * P:(m + 1) * P],
                                             hb[:, k, :], start=(k == 0), stop=(k == KD - 1))
                    last.then_inc(a_qmm, 1)

                if kind == 0:
                    pe.wait_ge(ln_ev, a * 2 + 2)
                    queries()
                    keys()
                    vals()
                else:
                    pe.wait_ge(a_encb, (a + 1) // 2)
                    keys()
                    vals()
                    layer_norm((a, a * 2, QT, 0))
                    pe.wait_ge(ln_ev, a * 2 + 2)
                    queries()
                pe.wait_ge(a_qev, a * 2 + 2)
                pe.wait_ge(a_kev, a * 4 + 4)

                def scores(h):
                    m, r, e = h // 8, (h % 8) // 2 * 32, h % 2
                    if h >= 2:
                        pe.wait_ge(a_t, a * H0 + h - 1)
                    for t in range(QT):
                        last = pe.matmul(bank[h % 2][:, t * S:(t + 1) * S], q0[r:r + 32, m, t * P:(t + 1) * P],
                                         k0[e][r:r + 32, m, :], start=True, stop=True)
                    last.then_inc(a_s, 1)

                def turn(h):
                    pe.wait_ge(a_p, (a * H0 + h) * 2 + 2)
                    if h >= 2:
                        pe.wait_ge(a_tev, a * H0 + h - 1)
                    for kt in range(QT):
                        for t in range(QT):
                            last = pe.transpose(bank[2 + h % 2][:, kt * S + t * P:kt * S + (t + 1) * P],
                                                p0[h % 2][:, t, kt * P:(kt + 1) * P], ident)
                    last.then_inc(a_tmm, 1)

                def pv(h):
                    pe.wait_ge(a_tev, a * H0 + h + 1)
                    if h == 0:
                        pe.wait_ge(a_vev, a * 2 + 2)
                    for t in range(QT):
                        for kt in range(QT):
                            last = pe.matmul(bank[4 + t][:, h * (HD0 + 1):(h + 1) * (HD0 + 1)],
                                             pt0[h % 2][:, kt, t * P:(t + 1) * P], v0[:, kt, h, :],
                                             start=(kt == 0), stop=(kt == QT - 1))
                    last.then_inc(a_pv, 1)

                for h in range(H0 + 2):
                    if h < H0:
                        scores(h)
                    if 1 <= h <= H0:
                        turn(h - 1)
                    if h >= 2:
                        pv(h - 2)
                pe.wait_ge(a_cn, a * 2 + 2)
                cn = cn0[:, :, :, :].rearrange("p t h d -> p t (h d)")
                transposes(cn, 0, 7, a_cmm)
                pe.wait_ge(a_cev, a * 2 + 2)
                wout = (w_ao, w_co)[kind]
                for t in range(QT):
                    mm_bias(bank[6][:, t * D:(t + 1) * D], kind)
                    for k in range(KD):
                        last = pe.matmul(bank[6][:, t * D:(t + 1) * D], ct0[:, k, t * P:(t + 1) * P],
                                         wout[:, k, :], start=False, stop=(k == KD - 1))
                last.then_inc(a_omm, 1)

            pe.wait_ge(d_w0, 5 * 16)
            pe.wait_ge(d_row, 16)
            pe.wait_ge(init, 3)
            with pe.Fori(0, B) as b:
                layer_norm(ln_l0(b, 0))
                attention0(b * 2, 0)
                attention0(b * 2 + 1, 1)

            def mlp(call, m, bias_row):
                layer_norm(call)
                pe.wait_ge(ln_ev, call[1] + NT)
                for c in range(TOK // CH):
                    for f in range(NF):
                        n = (2 * m + c) * NF + f
                        if c > 0 or f >= 4:
                            pe.wait_ge(m_gelu, n - 3)
                        for k in range(KD):
                            last = pe.matmul(bank[f % 4][:, :], w_up[:, k, f * P:(f + 1) * P],
                                             hT[:, k, c * CH:(c + 1) * CH], start=(k == 0), stop=(k == KD - 1))
                        last.then_inc(m_up, 1)
                    pe.wait_ge(m_gelu, (2 * m + c + 1) * NF)
                    for j in range(2):
                        if c > 0:
                            pe.wait_ge(m_x, 2 * (2 * m + c) + j - 1)
                        for t in range(2):
                            dst = bank[4 + j][:, t * D:(t + 1) * D]
                            mm_bias(dst, bias_row)
                            for f in range(NF):
                                last = pe.matmul(dst, gelu[:, f, (2 * j + t) * P:(2 * j + t + 1) * P], w_down[:, f, :],
                                                 start=False, stop=(f == NF - 1))
                        last.then_inc(m_down, 1)

            pe.wait_ge(d_up, 32)
            mlp(LN_MLP0, 0, 2)

            def mm3(dst, lh, ll, rh, rl, start, stop):
                pe.matmul(dst, lh, rh, start=start, stop=False)
                pe.matmul(dst, ll, rh, start=False, stop=False)
                return pe.matmul(dst, lh, rl, start=False, stop=stop)

            def proj(hh, i):
                c, w = i // 2, i % 2
                src_h, src_l = ((hTh, hTl), (encTh, encTl))[w]
                for k in range(KD):
                    last = mm3(bank[6 + w][:, :], wqk_h[hh][:, w, k, :], wqk_l[hh][:, w, k, :],
                               src_h[:, k, c * CH:(c + 1) * CH], src_l[:, k, c * CH:(c + 1) * CH],
                               k == 0, k == KD - 1)
                last.then_inc(g_mm, 1)

            def scores(g, s):
                hh, b = s // B, s % B
                for t in range(QT):
                    at = b * S + t * P
                    last = mm3(bank[2 * (s % 2) + t][:, 0:SP], qh[:, hh, at:at + P], ql[:, hh, at:at + P],
                               kh[:, hh, b, :], kl[:, hh, b, :], True, True)
                last.then_inc(s_mm, 1)

            def turn(g, s):
                pe.wait_ge(s_pn, g * 2 + 2)
                for kt in range(QT):
                    for t in range(QT):
                        last = pe.transpose(bank[4][:, kt * S + t * P:kt * S + (t + 1) * P],
                                            pn[s % 2][:, t, kt * P:(kt + 1) * P], ident)
                last.then_inc(t_mm, 1)

            def pv(g, s, n):
                hh, b = s // B, s % B
                pe.wait_ge(t_lo, g + 1)
                pe.wait_ge(v_lo, n * 4 + b + 1)
                pe.wait_ge(c_lo, g)
                for kt in range(QT):
                    last = mm3(bank[5][:, 0:S], vh[:, 2 * b + kt, hh * P:(hh + 1) * P],
                               vl[:, 2 * b + kt, hh * P:(hh + 1) * P], pth[s % 2][:, kt, :], ptl[s % 2][:, kt, :],
                               kt == 0, kt == QT - 1)
                last.then_inc(pv_mm, 1)

            def values(n, j, free, count):
                pe.wait_ge(free, count)
                for t in range(2):
                    at = (2 * j + t) * P
                    for k in range(KD):
                        last = mm3(bank[6 + j % 2][:, t * S:(t + 1) * S], encTh[:, k, at:at + P],
                                   encTl[:, k, at:at + P], wv_h[:, k, :], wv_l[:, k, :], k == 0, k == KD - 1)
                last.then_inc(v_mm, 1)

            def attn_out(n, bias_row):
                pe.wait_ge(c_lo, (n + 1) * STEPS)
                pe.wait_ge(w_o, n * 2 + 2)
                for j in range(B):
                    if j >= 2:
                        count = held(pe, count_reg, n * 4 + j - 1)
                        pe.wait_ge(d_row, 16)
                        pe.wait_ge(o_x, count)
                    for t in range(2):
                        at = (2 * j + t) * P
                        dst = bank[6 + j % 2][:, t * D:(t + 1) * D]
                        if bias_row is not None:
                            mm_bias(dst, bias_row)
                        for hh in range(2):
                            last = mm3(dst, ch[:, hh, at:at + P], cl[:, hh, at:at + P], wo_h[:, hh, :],
                                       wo_l[:, hh, :], bias_row is None and hh == 0, hh == 1)
                    last.then_inc(o_mm, 1)

            def pair(n, first, last):
                g = n * STEPS
                if not first:
                    pe.wait_ge(t_lo, g - 2)
                    turn(g - 2, 6)
                    pv(g - 3, 5, n - 1)
                pe.wait_ge(w_v, n * 2 + 2)
                values(n, 0, g_lo, n * 8 + 3)
                if not first:
                    pe.wait_ge(t_lo, g - 1)
                    turn(g - 1, 7)
                    pv(g - 2, 6, n - 1)
                values(n, 1, g_lo, n * 8 + 4)
                if not first:
                    pv(g - 1, 7, n - 1)
                values(n, 2, v_t, n * 4 + 1)
                values(n, 3, v_t, n * 4 + 2)
                pe.wait_ge(v_t, n * 4 + 4)
                if not first:
                    attn_out(n - 1, None)
                for s in range(STEPS):
                    g = n * STEPS + s
                    if s == 0:
                        pe.wait_ge(kb, n * 4 + 2)
                        pe.wait_ge(w_qk, n * 4 + 4)
                    if s == 4:
                        pe.wait_ge(kb, n * 4 + 4)
                    if s % 4 == 0:
                        pe.wait_ge(g_lo, n * 8 + s + 2 if s else n * 8 + 4)
                    if s % 4 == 2:
                        pe.wait_ge(g_lo, n * 8 + s + 2)
                    if s >= 2:
                        pe.wait_ge(s_exp, g * 2 - 2)
                    scores(g, s)
                    if s >= 2:
                        pe.wait_ge(t_lo, g - 2)
                        turn(g - 2, s - 2)
                    if s < 4 or not last:
                        if s == 4:
                            pe.wait_ge(w_qk, n * 4 + 6)
                        if s >= 2:
                            pe.wait_ge(g_lo, n * 8 + s + 3)
                        elif not first:
                            pe.wait_ge(o_x, n * 4 + s - 1)
                        proj(s // 4 ^ 1, s % 4)
                    if s >= 3:
                        pv(g - 3, s - 3, n)

            pe.wait_ge(enc_lo, 1)
            with pe.Fori(0, PH) as ph:
                n0 = ph * PAIRS
                layer_norm(ln_l1(ph))
                pe.wait_ge(hsp, ph * 2 + 2)
                pe.wait_ge(ln_ev, ln_l1(ph)[1] + NT)
                pe.wait_ge(w_qk, n0 * 4 + 2)
                for i in range(4):
                    if i >= 2:
                        pe.wait_ge(g_lo, n0 * 8 + i - 1)
                    proj(0, i)
                pair(n0, True, False)
                with pe.Fori(1, PAIRS - 1) as p:
                    pair(n0 + p, False, False)
                pair(n0 + (PAIRS - 1), False, True)
                g = (n0 + PAIRS) * STEPS
                n = n0 + (PAIRS - 1)
                pe.wait_ge(t_lo, g - 2)
                turn(g - 2, 6)
                pv(g - 3, 5, n)
                pe.wait_ge(t_lo, g - 1)
                turn(g - 1, 7)
                pv(g - 2, 6, n)
                pv(g - 1, 7, n)
                attn_out(n, ph + 3)
            pe.wait_ge(d_up2, 32)
            mlp(LN_MLP1, 1, 5)


def kernel(**inputs):
    import numpy as _np
    import concourse.bacc as _bacc
    from concourse import mybir as _mybir
    from concourse.bass_utils import run_bass_kernel_spmd as _run

    a = {k: _np.ascontiguousarray(v) for k, v in inputs.items()}
    L0 = {k[len("L0_xattn_"):]: v for k, v in a.items() if k.startswith("L0_")}
    L1 = {k[len("L1_xattn_"):]: v for k, v in a.items() if k.startswith("L1_")}

    def cols(v):
        return v.reshape(-1, P).T

    bqkv, bkv = L0["b_qkv"], L0["b_kv"]
    packs = {
        "ln1_s": L0["ln1_s"], "ln1_b": L0["ln1_b"], "bq_s": bqkv[:D], "bk_s": bqkv[D:2 * D], "bv_s": bqkv[2 * D:],
        "ln2_s": L0["ln2_s"], "ln2_b": L0["ln2_b"], "bq_c": L0["b_q"], "bk_c": bkv[:D], "bv_c": bkv[D:],
        "ln3_s": L0["ln3_s"], "ln3_b": L0["ln3_b"], "b1": L0["b1"],
        "lnx_s": _np.concatenate([L1["ln1_scale"], L1["ln2_scale"]]),
        "lnx_b": _np.concatenate([L1["ln1_offset"], L1["ln2_offset"]]),
        "bq": _np.concatenate([L1["bq1"], L1["bq2"]]), "bk": _np.concatenate([L1["bk1"], L1["bk2"]]),
        "bias_k": _np.concatenate([L1["bias_k1"].reshape(-1), L1["bias_k2"].reshape(-1)]),
        "bias_v": _np.concatenate([L1["bias_v1"].reshape(-1), L1["bias_v2"].reshape(-1)]),
        "lnm_s": L1["ln_mlp_scale"], "lnm_b": L1["ln_mlp_offset"], "b_fc1": L1["b_fc1"],
    }
    vec = _np.concatenate([cols(packs[k]) for k in VEC], axis=1)
    row = _np.stack([L0["b_ao"], L0["b_co"], L0["b2"], L1["bo1"], L1["bo2"], L1["b_fc2"]])[None]
    strip = (_np.arange(P) // HD0) % 2
    consts = _np.concatenate([_np.eye(P), (strip == 0)[:, None], (strip == 1)[:, None]], axis=1).astype(_np.float32)

    def heads(w):
        return w.reshape(KD, P, H1, HD1).transpose(2, 1, 0, 3)

    wqk = _np.stack([_np.stack([heads(L1[f"wq{i}"]), heads(L1[f"wk{i}"])], axis=2) for i in (1, 2)])
    wqk = wqk.reshape(PH * H1, P, 2 * KD * HD1)
    wv = _np.stack([L1[f"wv{i}"].reshape(KD, P, PAIRS, 2 * HD1).transpose(2, 1, 0, 3) for i in (1, 2)])
    wv = wv.reshape(PH * PAIRS, P, KD * 2 * HD1)
    wo = _np.stack([L1[f"wo{i}"].reshape(PAIRS, 2, HD1, D).transpose(0, 2, 1, 3) for i in (1, 2)])
    wo = wo.reshape(PH * PAIRS, P, 2 * D)
    vb = _np.stack([_np.stack([L1[f"bv{i}"].reshape(PAIRS, 2 * HD1), L1[f"bias_v{i}"].reshape(PAIRS, 2 * HD1)],
                              axis=1) for i in (1, 2)]).reshape(PH * PAIRS, 4 * HD1)
    feeds = {
        "x": a["x"].reshape(TOK, D), "enc": a["ctx_2048"].reshape(TOK, D),
        "mask_self": a["mask_1x1xSxS2_fc1"].reshape(S, S), "mask_cross": a["mask_Bx1xSxS2_ff1"].reshape(B * S, S),
        "consts": consts, "vec": vec, "row": row,
        "w_qkv": L0["w_qkv"], "w_ao": L0["w_ao"], "w_q": L0["w_q"], "w_kv": L0["w_kv"], "w_co": L0["w_co"],
        "w1": L0["w1"], "w2": L0["w2"], "wf1": L1["w_fc1"], "wf2": L1["w_fc2"],
        "wqk": wqk, "wv": wv, "wo": wo, "vb": vb,
    }
    nc = _bacc.Bacc("TRN2", target_bir_lowering=False, num_devices=1)
    arrays, args = {}, []
    for name, v in feeds.items():
        v = _np.ascontiguousarray(v)
        arrays[f"in_{name}"] = v
        args.append(nc.dram_tensor(f"in_{name}", v.shape, _mybir.dt.from_np(v.dtype), kind="ExternalInput").ap())
    out = nc.dram_tensor("out_x", (TOK, D), _mybir.dt.float32, kind="ExternalOutput").ap()
    build(nc, *args, out)
    r = _run(nc, [arrays], core_ids=[0])
    return r.results[0]["out_x"].reshape(B, S, D)
```

```python
from contextlib import ExitStack

import concourse.bass as bass
import concourse.mybir as mybir

P = 128
B, S, D = 4, 256, 256
TOK = B * S
NT = TOK // P
KD = D // P
QT = S // P
H0, HD0 = 16, 16
H1, HD1 = 16, 128
FF = 1024
NF = FF // P
CH = 512
PAIRS = H1 // 2
PH = 2
STEPS = 2 * B
EPS = 1e-5
MASKED = 10000.0
HG = P // HD0
TURN_LAG, PV_LAG = 3, 4
SP = S + 2

VEC = {}
_at = 0
for _name, _n in (("ln1_s", 2), ("ln1_b", 2), ("bq_s", 2), ("bk_s", 2), ("bv_s", 2), ("ln2_s", 2), ("ln2_b", 2),
                  ("bq_c", 2), ("bk_c", 2), ("bv_c", 2), ("ln3_s", 2), ("ln3_b", 2), ("b1", 8),
                  ("lnx_s", 4), ("lnx_b", 4), ("bq", 32), ("bk", 32), ("bias_k", 32), ("bias_v", 32),
                  ("lnm_s", 2), ("lnm_b", 2), ("b_fc1", 8)):
    VEC[_name] = _at
    _at += _n
NVEC = _at
ROWS = ("b_ao", "b_co", "b2", "bo1", "bo2", "b_fc2")


def build(nc, x_in, enc_in, mask_self, mask_cross, consts, vec_in, row_in, w_qkv_in, w_ao_in, w_q_in, w_kv_in,
          w_co_in, w1_in, w2_in, wf1_in, wf2_in, wqk_in, wv_in, wo_in, vb_in, out):
    f32, f32r = mybir.dt.float32, mybir.dt.float32r
    ALU = mybir.AluOpType
    ACT = mybir.ActivationFunctionType
    AX = mybir.AxisListType
    ds = bass.ds

    with ExitStack() as ctx:
        def sb(name, shape, dt=f32):
            return in_turn.enter_context(nc.sbuf_tensor(name, shape, dt))

        def sem(name):
            return ctx.enter_context(nc.semaphore(name))

        in_turn = ctx
        x_acc = sb("x_acc", [P, NT, D])
        encT = sb("encT", [P, KD, TOK], f32)
        encTh = sb("encTh", [P, KD, TOK], f32r)
        encTl = sb("encTl", [P, KD, TOK], f32r)
        const = sb("const", [P, P + HG])
        ident = const[:, 0:P]
        head_rows = [const[:, P + j:P + j + 1] for j in range(HG)]
        vec = sb("vec", [P, NVEC])
        row = sb("row", [1, len(ROWS), D])
        ones = sb("ones", [1, P])
        neg_half = sb("neg_half", [P, NT])
        stats = sb("stats", [P, NT, 6])
        mean_var = sb("mean_var", [P, NT, 2])
        var_eps = sb("var_eps", [P, NT])
        rstd = sb("rstd", [P, NT])
        xn = sb("xn", [P, NT, D])
        w_up = sb("w_up", [P, KD, FF])
        w_down = sb("w_down", [P, NF, D])
        hT = sb("hT", [P, KD, TOK])
        raw_qk = [sb(f"raw_qk{i}", [P, 2, KD, HD1]) for i in range(2)]
        raw_v = sb("raw_v", [P, KD, 2 * HD1])
        raw_o = sb("raw_o", [P, 2, D])
        raw_vb = sb("raw_vb", [P, 2, 2 * HD1])
        bkh = sb("bkh", [P, PH * H1], f32r)
        bkl = sb("bkl", [P, PH * H1], f32r)
        in_turn = ExitStack()
        gelu = sb("gelu", [P, NF, CH])
        in_turn.close()
        in_turn = ctx
        ch = sb("ch", [P, 2, TOK], f32r)
        cl = sb("cl", [P, 2, TOK], f32r)
        first = ExitStack()
        in_turn = first
        w_qkv = sb("w_qkv", [P, KD, 3 * D])
        w_ao = sb("w_ao", [P, KD, D])
        w_q = sb("w_q", [P, KD, D])
        w_kv = sb("w_kv", [P, KD, 2 * D])
        w_co = sb("w_co", [P, KD, D])
        hb = sb("hb", [P, KD, S])
        encb = sb("encb", [P, KD, S])
        q0 = sb("q0", [P, KD, S])
        kx = sb("kx", [P, KD, S])
        kp = [sb(f"kp{i}", [P, S]) for i in range(4)]
        v0 = sb("v0", [P, QT, H0, HD0 + P])
        msk_next, msk, pen = sb("msk_next", [P, QT, S]), sb("msk", [P, QT, S]), sb("pen", [P, QT, S])
        tm = [sb(f"tm{i}", [P, QT, S]) for i in range(2)]
        um = [sb(f"um{i}", [P, QT, S]) for i in range(2)]
        umin = sb("umin", [P, 2, QT])
        p0 = [sb(f"p0_{i}", [P, QT, S]) for i in range(2)]
        psum0 = sb("psum0", [P, 4, QT])
        rsum0 = sb("rsum0", [P, 4, QT])
        pn0 = [sb(f"pn0_{i}", [P, QT, S]) for i in range(4)]
        pt0 = [sb(f"pt0_{i}", [P, QT, S]) for i in range(2)]
        ct0 = sb("ct0", [P, KD, S])
        first.close()
        in_turn = ctx
        hTh = sb("hTh", [P, KD, TOK], f32r)
        hTl = sb("hTl", [P, KD, TOK], f32r)
        wqk_h = [sb(f"wqk_h{i}", [P, 2, KD, HD1], f32r) for i in range(2)]
        wqk_l = [sb(f"wqk_l{i}", [P, 2, KD, HD1], f32r) for i in range(2)]
        wv_h = sb("wv_h", [P, KD, 2 * HD1], f32r)
        wv_l = sb("wv_l", [P, KD, 2 * HD1], f32r)
        wo_h = sb("wo_h", [P, 2, D], f32r)
        wo_l = sb("wo_l", [P, 2, D], f32r)
        v_bias = sb("v_bias", [P, 2 * HD1])
        qh = sb("qh", [P, 2, TOK], f32r)
        ql = sb("ql", [P, 2, TOK], f32r)
        kh = sb("kh", [P, 2, B, SP], f32r)
        kl = sb("kl", [P, 2, B, SP], f32r)
        vt = [sb(f"vt{i}", [P, 2, 2 * HD1]) for i in range(2)]
        vh = sb("vh", [P, NT, 2 * HD1], f32r)
        vl = sb("vl", [P, NT, 2 * HD1], f32r)
        mx = sb("mx", [P, 4, QT])
        nm = sb("nm", [P, 4, QT])
        sums = sb("sums", [P, 4, QT])
        rs = sb("rs", [P, 4, QT])
        pr = [sb(f"pr{i}", [P, QT, S + 1]) for i in range(4)]
        pn = [sb(f"pn{i}", [P, QT, S]) for i in range(2)]
        pth = [sb(f"pth{i}", [P, QT, S], f32r) for i in range(2)]
        ptl = [sb(f"ptl{i}", [P, QT, S], f32r) for i in range(2)]

        bank = [ctx.enter_context(nc.psum_tensor(f"bank{i}", [P, CH], f32)) for i in range(8)]

        d_x, d_enc, d_const, d_vec, d_row = sem("d_x"), sem("d_enc"), sem("d_const"), sem("d_vec"), sem("d_row")
        d_m, d_w0, d_up = sem("d_m"), sem("d_w0"), sem("d_up")
        d_up2 = sem("d_up2")
        d_qk = [sem("d_qk0"), sem("d_qk1")]
        d_v, d_o, d_vb, d_out = sem("d_v"), sem("d_o"), sem("d_vb"), sem("d_out")
        init = sem("init")
        enc_mm, enc_ev = sem("enc_mm"), sem("enc_ev")
        enc_hi, enc_lo = sem("enc_hi"), sem("enc_lo")
        ln_st, ln_mv, ln_eps, ln_rstd, ln_xn = (sem(n) for n in ("ln_st", "ln_mv", "ln_eps", "ln_rstd", "ln_xn"))
        ln_mm, ln_ev = sem("ln_mm"), sem("ln_ev")
        hsp = sem("hsp")
        a_encb, a_mask = sem("a_encb"), sem("a_mask")
        a_qmm, a_qev, a_kmm, a_kev, a_vmm, a_vev = (sem(n) for n in ("a_qmm", "a_qev", "a_kmm", "a_kev", "a_vmm", "a_vev"))
        a_kp, a_s, a_t, a_u, a_p, a_rs, a_pn, a_tmm, a_tev, a_pv, a_cev = (sem(n) for n in (
            "a_kp", "a_s", "a_t", "a_u", "a_p", "a_rs", "a_pn", "a_tmm", "a_tev", "a_pv", "a_cev"))
        a_omm, a_x = sem("a_omm"), sem("a_x")
        m_up, m_gelu, m_down, m_x = (sem(n) for n in ("m_up", "m_gelu", "m_down", "m_x"))
        w_qk, w_v, w_o, w_vb, kb = (sem(n) for n in ("w_qk", "w_v", "w_o", "w_vb", "kb"))
        g_mm, g_hi, g_lo = sem("g_mm"), sem("g_hi"), sem("g_lo")
        v_mm, v_t, v_hi, v_lo = sem("v_mm"), sem("v_t"), sem("v_hi"), sem("v_lo")
        s_mm, s_max, s_nm, s_exp, s_rs, s_pn = (sem(n) for n in ("s_mm", "s_max", "s_nm", "s_exp", "s_rs", "s_pn"))
        t_mm, t_hi, t_lo = sem("t_mm"), sem("t_hi"), sem("t_lo")
        pv_mm, c_hi, c_lo = sem("pv_mm"), sem("c_hi"), sem("c_lo")
        o_mm, o_x = sem("o_mm"), sem("o_x")

        PAST = 1

        def start_counts(eng, *signals):
            for signal in signals:
                eng.sem_inc(signal, PAST)

        def col(name, i=0):
            return vec[:, ds(VEC[name] + i, 1)]

        def ln_l0(a, b):
            return (a, 2 * a, QT, 2 * b)
        LN_MLP0 = (2 * B, 4 * B, NT, 0)

        def ln_l1(ph):
            return (2 * B + 1 + ph, 4 * B + NT + ph * NT, NT, 0)
        LN_MLP1 = (2 * B + 1 + PH, 4 * B + NT * (1 + PH), NT, 0)

        def before(a, kind, b):
            return (0, B - 1) if isinstance(a, int) and a == B else (kind, b - 1)

        def held(eng, reg, value):
            if isinstance(value, int):
                return value
            eng.reg_mov(reg, value)
            return reg

        def all_l0(attention):
            def loop(eng):
                attention(0, 0, 0, True, (0, 1))
                with eng.Fori(1, B - 1) as b:
                    attention(b, 0, b, False, (0, b + 1))
                attention(B - 1, 0, B - 1, False, (1, 0))
                attention(B, 1, 0, False, (1, 1))
                with eng.Fori(1, B - 1) as b:
                    attention(b + B, 1, b, False, (1, b + 1))
                attention(2 * B - 1, 1, B - 1, False, None)
            return loop

        block = ctx.enter_context(nc.Block())

        @block.sync
        def _(sp):
            count_reg = sp.alloc_register()
            sp.dma_start(x_acc[:, :, :], x_in.rearrange("(t p) d -> p t d", p=P)).then_inc(d_x, 16)
            sp.dma_start(xn[:, :, :], enc_in.rearrange("(t p) d -> p t d", p=P)).then_inc(d_enc, 16)
            for wt, src in ((w_qkv, w_qkv_in), (w_ao, w_ao_in), (w_q, w_q_in), (w_kv, w_kv_in), (w_co, w_co_in)):
                sp.dma_start(wt[:, :, :], src.rearrange("(k p) n -> p k n", p=P)).then_inc(d_w0, 16)
            sp.dma_start(msk_next[:, :, :], mask_self.rearrange("(t p) k -> p t k", p=P)).then_inc(d_m, 16)
            sp.dma_start(w_up[:, :, :], w1_in.rearrange("(k p) n -> p k n", p=P)).then_inc(d_up, 16)
            sp.dma_start(w_down[:, :, :], w2_in.rearrange("(k p) n -> p k n", p=P)).then_inc(d_up, 16)

            def load_pair(n, first):
                for i in range(2):
                    if not first:
                        sp.wait_ge(w_qk, n * 4 + 2 * i - 2)
                    sp.dma_start(raw_qk[i][:, :, :, :], wqk_in[ds(n * 2 + i, 1)].rearrange(
                        "a p (c k m) -> p (a c) k m", c=2, k=KD)).then_inc(d_qk[i], 16)
                    if i == 0:
                        if not first:
                            sp.wait_ge(w_v, n * 2)
                        sp.dma_start(raw_v[:, :, :], wv_in[ds(n, 1)].rearrange(
                            "a p (k m) -> p (a k) m", k=KD)).then_inc(d_v, 16)
                        if not first:
                            sp.wait_ge(w_vb, n)
                        sp.dma_start(raw_vb[:, :, :], vb_in[ds(n, 1)].rearrange(
                            "a (c m) -> a c m", c=2).to_broadcast([P, 2, 2 * HD1])).then_inc(d_vb, 16)
                if not first:
                    sp.wait_ge(w_o, n * 2)
                sp.dma_start(raw_o[:, :, :], wo_in[ds(n, 1)].rearrange(
                    "a p (c m) -> p (a c) m", c=2)).then_inc(d_o, 16)

            load_pair(0, True)
            sp.wait_ge(a_mask, 2)
            sp.dma_start(msk_next[:, :, :], mask_cross[0:S, :].rearrange("(t p) k -> p t k", p=P)).then_inc(d_m, 16)
            with sp.Fori(1, B) as b:
                count = held(sp, count_reg, b * 2 + 2)
                sp.wait_ge(d_x, 16)
                sp.wait_ge(a_mask, count)
                sp.dma_start(msk_next[:, :, :], mask_cross[ds(b * S, S), :].rearrange(
                    "(t p) k -> p t k", p=P)).then_inc(d_m, 16)
            sp.wait_ge(m_down, 4)
            sp.dma_start(w_up[:, :, :], wf1_in.rearrange("(k p) n -> p k n", p=P)).then_inc(d_up2, 16)
            sp.dma_start(w_down[:, :, :], wf2_in.rearrange("(k p) n -> p k n", p=P)).then_inc(d_up2, 16)
            with sp.Fori(1, PH * PAIRS) as n:
                load_pair(n, False)
            for j in range(NT // 2):
                sp.wait_ge(m_x, NT // 2 + j + 1)
                sp.dma_start(out[2 * j * P:(2 * j + 2) * P, :].rearrange("(t p) d -> p t d", p=P),
                             x_acc[:, 2 * j:2 * j + 2, :]).then_inc(d_out, 16)
            sp.wait_ge(d_out, 16 * (NT // 2))

        @block.gpsimd
        def _(pool):
            count_reg = pool.alloc_register()
            other_reg = pool.alloc_register()
            pool.dma_start(const[:, :], consts).then_inc(d_const, 16)
            pool.dma_start(vec[:, :], vec_in).then_inc(d_vec, 16)
            pool.dma_start(row[:, :, :], row_in).then_inc(d_row, 16)
            pool.memset(ones[:, :], 1.0).then_inc(init, 1)
            pool.memset(neg_half[:, :], -0.5).then_inc(init, 1)
            pool.memset(v0[:, :, :, HD0:HD0 + P], 0.0).then_inc(init, 1)
            pool.wait_ge(init, 3)
            pool.wait_ge(d_vec, 16)
            pool.tensor_scalar(bkh[:, :], vec[:, VEC["bias_k"]:VEC["bias_k"] + PH * H1], 1.0, 1.0,
                               ALU.mult, ALU.mult).then_inc(init, 1)
            pool.wait_ge(init, 4)
            pool.tensor_tensor(bkl[:, :], vec[:, VEC["bias_k"]:VEC["bias_k"] + PH * H1], bkh[:, :],
                               ALU.subtract).then_inc(init, 1)

            def layer_norm(call):
                c, t0, n, _ = call
                count = held(pool, count_reg, t0 + n)
                pool.wait_ge(init, 3)
                pool.wait_ge(ln_mv, count)
                pool.tensor_scalar(var_eps[:, 0:n], mean_var[:, 0:n, 1], 1.0, EPS, ALU.mult,
                                   ALU.add).then_inc(ln_eps, 1)
                pool.wait_ge(ln_eps, c + 1)
                pool.tensor_tensor(rstd[:, 0:n], var_eps[:, 0:n], neg_half[:, 0:n], ALU.pow).then_inc(ln_rstd, 1)

            pool.wait_ge(enc_ev, 2 * NT // 2)
            pool.wait_ge(d_const, 16)

            def key_rows(g, h, unit):
                if h % HG == 0:
                    count = held(pool, count_reg, unit + 1)
                else:
                    count = None
                if isinstance(g, int) and g < 4:
                    used = None
                else:
                    used = held(pool, other_reg, g - 3)
                pool.wait_ge(init, 3)
                if count is not None:
                    pool.wait_ge(a_kev, count)
                if used is not None:
                    pool.wait_ge(a_s, used)
                pool.tensor_scalar(kp[h % 4][:, :], kx[:, h // HG, :], head_rows[h % HG], 1.0, ALU.mult,
                                   ALU.mult).then_inc(a_kp, 1)

            def normalise(g, h):
                count = held(pool, count_reg, g + 1)
                turned = None if isinstance(g, int) and g < 4 else held(pool, other_reg, g - 3)
                pool.wait_ge(init, 3)
                pool.wait_ge(a_rs, count)
                if turned is not None:
                    pool.wait_ge(a_tmm, turned)
                for t in range(QT):
                    pool.tensor_scalar(pn0[h % 4][:, t, :], p0[h % 2][:, t, :], rsum0[:, h % 4, t:t + 1], 1.0,
                                       ALU.mult, ALU.mult).then_inc(a_pn, 1)

            def attention0(a, kind, b, first, next):
                g = a * H0
                if first:
                    layer_norm(ln_l0(0, 0))
                    key_rows(0, 0, 0)
                    key_rows(1, 1, 0)
                for s in range(H0):
                    if s + 2 < H0:
                        key_rows(g + s + 2, s + 2, a * 2 + (s + 2) // HG)
                    elif next is not None:
                        key_rows(g + s + 2, s + 2 - H0, a * 2 + 2)
                    if s >= 1:
                        normalise(g + s - 1, s - 1)
                    elif not first:
                        normalise(g - 1, H0 - 1)
                    if s == 5 and next is not None:
                        layer_norm(ln_l0(a + 1, 0))
                        if next[0] == 1:
                            pool.wait_ge(a_vmm, a * 2 + 2)
                            pool.tensor_copy(encb[:, :, :], encT[:, :, ds(next[1] * S, S)]).then_inc(a_encb, 1)
                if next is None:
                    normalise(g + H0 - 1, H0 - 1)

            all_l0(attention0)(pool)
            pool.tensor_scalar(encTh[:, :, :], encT[:, :, :], 1.0, 1.0, ALU.mult, ALU.mult).then_inc(enc_hi, 1)
            pool.wait_ge(enc_hi, 1)
            pool.tensor_tensor(encTl[:, :, :], encT[:, :, :], encTh[:, :, :], ALU.subtract).then_inc(enc_lo, 1)
            layer_norm(LN_MLP0)

            def split_hi(hi, raw, s, inc=1):
                pool.tensor_scalar(hi, raw, 1.0, 1.0, ALU.mult, ALU.mult).then_inc(s, inc)

            def split_lo(lo, raw, hi, s):
                pool.tensor_tensor(lo, raw, hi, ALU.subtract).then_inc(s, 1)

            def qk_hi(n, i):
                count = held(pool, count_reg, PAST + n * 8 + 4 * i - 4)
                loaded = held(pool, other_reg, n * 16 + 16)
                pool.wait_ge(init, 3)
                pool.wait_ge(d_qk[i], loaded)
                pool.wait_ge(g_mm, count)
                split_hi(wqk_h[i][:, :, :, :], raw_qk[i][:, :, :, :], w_qk)

            def qk_lo(n, i):
                pool.wait_ge(w_qk, n * 4 + 2 * i + 1)
                split_lo(wqk_l[i][:, :, :, :], raw_qk[i][:, :, :, :], wqk_h[i][:, :, :, :], w_qk)

            def v_hi_(n):
                count = held(pool, count_reg, PAST + n * 4)
                loaded = held(pool, other_reg, n * 16 + 16)
                pool.wait_ge(init, 3)
                pool.wait_ge(d_v, loaded)
                pool.wait_ge(v_mm, count)
                split_hi(wv_h[:, :, :], raw_v[:, :, :], w_v)

            def v_lo_(n):
                pool.wait_ge(w_v, n * 2 + 1)
                split_lo(wv_l[:, :, :], raw_v[:, :, :], wv_h[:, :, :], w_v)

            def v_bias_(n):
                pool.wait_ge(d_vb, n * 16 + 16)
                pool.wait_ge(v_t, PAST + n * 4)
                split_lo(v_bias[:, :], raw_vb[:, 0, :], raw_vb[:, 1, :], w_vb)

            def o_hi_(n):
                count = held(pool, count_reg, PAST + n * 4)
                loaded = held(pool, other_reg, n * 16 + 16)
                pool.wait_ge(init, 3)
                pool.wait_ge(d_o, loaded)
                pool.wait_ge(o_mm, count)
                split_hi(wo_h[:, :, :], raw_o[:, :, :], w_o)

            def o_lo_(n):
                pool.wait_ge(w_o, n * 2 + 1)
                split_lo(wo_l[:, :, :], raw_o[:, :, :], wo_h[:, :, :], w_o)

            def key_bias(n, i, scores_done):
                if scores_done is not None:
                    pool.wait_ge(s_mm, PAST + scores_done)
                hd = n * 2 + i
                for dst, src in ((kh, bkh), (kl, bkl)):
                    pool.tensor_copy(dst[:, i, :, S:SP], src[:, ds(hd, 1)].unsqueeze(2).to_broadcast(
                        [P, B, 2])).then_inc(kb, 1)

            def norm(g, s):
                count = held(pool, count_reg, g + 1)
                if s >= 2:
                    turned = held(pool, other_reg, g - 1)
                pool.wait_ge(init, 3)
                if s >= 2:
                    pool.wait_ge(t_mm, turned)
                pool.wait_ge(s_rs, count)
                for t in range(QT):
                    pool.tensor_scalar(pn[s % 2][:, t, :], pr[s % 4][:, t, 0:S], rs[:, s % 4, t:t + 1], 1.0,
                                       ALU.mult, ALU.mult).then_inc(s_pn, 1)

            def pair(n, last):
                for j in range(B):
                    pool.wait_ge(v_hi, n * 4 + j + 1)
                    pool.tensor_tensor(vl[:, 2 * j:2 * j + 2, :], vt[j % 2][:, :, :], vh[:, 2 * j:2 * j + 2, :],
                                       ALU.subtract).then_inc(v_lo, 1)
                key_bias(n, 1, n * STEPS)
                for s in range(STEPS):
                    g = n * STEPS + s
                    if s == 4 and not last:
                        key_bias(n + 1, 0, g)
                    norm(g, s)
                    if not last:
                        if s == 0:
                            qk_hi(n + 1, 0)
                        if s == 1:
                            qk_lo(n + 1, 0)
                        if s == 2:
                            v_hi_(n + 1)
                        if s == 3:
                            v_lo_(n + 1)
                            v_bias_(n + 1)
                        if s == 4:
                            qk_hi(n + 1, 1)
                        if s == 5:
                            qk_lo(n + 1, 1)
                    if s == 6:
                        o_hi_(n)
                    if s == 7:
                        o_lo_(n)

            with pool.Fori(0, PH) as ph:
                n0 = ph * PAIRS
                key_bias(n0, 0, n0 * STEPS)
                count = held(pool, count_reg, n0 * 16 + 16)
                pool.wait_ge(init, 3)
                pool.wait_ge(d_qk[0], count)
                split_hi(wqk_h[0][:, :, :, :], raw_qk[0][:, :, :, :], w_qk)
                qk_lo(n0, 0)
                v_hi_(n0)
                v_lo_(n0)
                v_bias_(n0)
                count = held(pool, count_reg, n0 * 16 + 16)
                used = held(pool, other_reg, PAST + n0 * 8)
                pool.wait_ge(init, 3)
                pool.wait_ge(g_mm, used)
                pool.wait_ge(d_qk[1], count)
                split_hi(wqk_h[1][:, :, :, :], raw_qk[1][:, :, :, :], w_qk)
                qk_lo(n0, 1)
                layer_norm(ln_l1(ph))
                with pool.Fori(0, PAIRS - 1) as p:
                    pair(n0 + p, False)
                pair(n0 + (PAIRS - 1), True)
            layer_norm(LN_MLP1)

        @block.scalar
        def _(act):
            count_reg = act.alloc_register()
            act.wait_ge(d_vec, 16)

            def ln_out(call, dst, scale, offset):
                _, t0, n, _ = call
                for j in range(n // 2):
                    count = held(act, count_reg, t0 // 2 + j + 1)
                    act.wait_ge(d_vec, 16)
                    act.wait_ge(ln_mm, count)
                    for k in range(KD):
                        act.activation(dst[:, k, 2 * j * P:(2 * j + 2) * P], bank[6 + j % 2][:, k * S:(k + 1) * S],
                                       ACT.Identity, bias=offset(k), scale=scale(k)).then_inc(ln_ev, 1)

            def keys(unit, kind):
                u, m = unit
                act.wait_ge(a_kmm, u + 1)
                act.activation(kx[:, m, :], bank[6 + m][:, 0:S], ACT.Identity,
                               bias=col(("bk_s", "bk_c")[kind], m), scale=1.0).then_inc(a_kev, 1)

            def vals(unit):
                u, m = unit
                act.wait_ge(a_vmm, u + 1)
                for t in range(QT):
                    act.activation(v0[:, t, m * HG:(m + 1) * HG, 0:HD0], bank[7 - m][:, t * P:(t + 1) * P].rearrange(
                        "p (h d) -> p h d", h=HG), ACT.Copy).then_inc(a_vev, 1)

            def context(unit, kind):
                u, m = unit
                act.wait_ge(a_pv, u * HG + HG)
                act.activation(ct0[:, m, :], bank[4 + m][:, 0:S], ACT.Identity,
                               bias=col(("bv_s", "bv_c")[kind], m), scale=1.0).then_inc(a_cev, 1)

            def attention0(a, kind, b, first, next):
                g = a * H0

                def normed(a, kind):
                    names = (("ln1_s", "ln1_b"), ("ln2_s", "ln2_b"))[kind]
                    ln_out(ln_l0(a, 0), hb, lambda k: col(names[0], k), lambda k: col(names[1], k))

                def pt(g, h):
                    act.wait_ge(a_tmm, g + 1)
                    if not (isinstance(g, int) and g < 2):
                        act.wait_ge(a_pv, g - 1)
                    act.activation(pt0[h % 2][:, :, :], bank[2 + h % 2][:, :], ACT.Copy).then_inc(a_tev, 1)

                if first:
                    normed(0, 0)
                    keys((0, 0), 0)
                    vals((0, 0))
                for s in range(H0):
                    act.wait_ge(a_u, (g + s) * 2 + 2)
                    if not (isinstance(g, int) and g + s < 2):
                        act.wait_ge(a_pn, (g + s) * 2 - 2)
                    for t in range(QT):
                        act.activation(p0[s % 2][:, t, :], um[s % 2][:, t, :], ACT.Exp, bias=umin[:, s % 2, t:t + 1],
                                       scale=-1.0, accum_out=psum0[:, s % 4, t:t + 1]).then_inc(a_p, 1)
                    if s >= TURN_LAG or not first:
                        pt(g + s - TURN_LAG, (s - TURN_LAG) % H0)
                    if s == 2:
                        keys((a * 2 + 1, 1), kind)
                    if s == 4:
                        vals((a * 2 + 1, 1))
                        if not first:
                            context((a * 2 - 1, 1), before(a, kind, b)[0])
                    if s == 7 and next is not None:
                        normed(a + 1, next[0])
                    if s == 10 and next is not None:
                        keys((a * 2 + 2, 0), next[0])
                    if s == 12:
                        context((a * 2, 0), kind)
                        if next is not None:
                            vals((a * 2 + 2, 0))
                if next is None:
                    for s in range(TURN_LAG):
                        pt(g + H0 + s - TURN_LAG, H0 + s - TURN_LAG)
                    context((a * 2 + 1, 1), kind)

            for j in range(NT // 2):
                act.wait_ge(enc_mm, j + 1)
                for k in range(KD):
                    act.activation(encT[:, k, 2 * j * P:(2 * j + 2) * P], bank[j % 2][:, k * S:(k + 1) * S],
                                   ACT.Copy).then_inc(enc_ev, 1)
            all_l0(attention0)(act)

            def mlp(call, m, func, scale, offset, bias):
                ln_out(call, hT, scale, offset)
                for c in range(TOK // CH):
                    for f in range(NF):
                        act.wait_ge(m_up, (2 * m + c) * NF + f + 1)
                        act.activation(gelu[:, f, :], bank[f % 4][:, :], func, bias=bias(f),
                                       scale=1.0).then_inc(m_gelu, 1)

            mlp(LN_MLP0, 0, ACT.Gelu_apprx_tanh, lambda k: col("ln3_s", k), lambda k: col("ln3_b", k),
                lambda f: col("b1", f))

            def group_hi(n, i, hd):
                slot, c, which = hd, (i % 4) // 2, i % 2
                return slot, c, which

            def proj_hi(grp, hh, i, head):
                c = i // 2
                count = held(act, count_reg, PAST + grp + 1)
                act.wait_ge(d_vec, 16)
                act.wait_ge(g_mm, count)
                if i % 2 == 0:
                    act.activation(qh[:, hh, c * CH:(c + 1) * CH], bank[6 + i % 2][:, :], ACT.Identity,
                                   bias=col("bq", head), scale=1.0).then_inc(g_hi, 1)
                else:
                    act.activation(kh[:, hh, 2 * c:2 * c + 2, 0:S], bank[6 + i % 2][:, :].rearrange(
                        "p (b s) -> p b s", b=2), ACT.Identity, bias=col("bk", head), scale=1.0).then_inc(g_hi, 1)

            def pt_hi(g, s):
                act.wait_ge(t_mm, g + 1)
                act.activation(pth[s % 2][:, :, :], bank[4][:, :], ACT.Copy).then_inc(t_hi, 1)

            def ctx_hi(g, s, n):
                hh, b = s // B, s % B
                count = held(act, count_reg, PAST + g + 1)
                act.wait_ge(d_vec, 16)
                act.wait_ge(pv_mm, count)
                act.activation(ch[:, hh, b * S:(b + 1) * S], bank[5][:, 0:S], ACT.Identity,
                               bias=col("bias_v", n * 2 + hh), scale=1.0).then_inc(c_hi, 1)

            def exps(g, s):
                act.wait_ge(s_nm, g + 1)
                for t in range(QT):
                    act.activation(pr[s % 4][:, t, :], bank[2 * (s % 2) + t][:, 0:S + 1], ACT.Exp,
                                   bias=nm[:, s % 4, t:t + 1], scale=float(HD1) ** -0.5,
                                   accum_out=sums[:, s % 4, t:t + 1]).then_inc(s_exp, 1)

            def tails(n):
                g = n * STEPS
                pt_hi(g + 6, 6)
                ctx_hi(g + 5, 5, n)
                pt_hi(g + 7, 7)
                ctx_hi(g + 6, 6, n)
                ctx_hi(g + 7, 7, n)

            def pair(n, first, last):
                if not first:
                    tails(n - 1)
                for j in range(B):
                    act.wait_ge(v_t, PAST + n * 4 + j + 1)
                    if j == 0:
                        act.wait_ge(pv_mm, PAST + n * STEPS)
                    act.activation(vh[:, 2 * j:2 * j + 2, :], vt[j % 2][:, :, :], ACT.Copy).then_inc(v_hi, 1)
                for s in range(STEPS):
                    g = n * STEPS + s
                    if s >= 2:
                        pt_hi(g - 2, s - 2)
                    exps(g, s)
                    if s < 4:
                        proj_hi(n * 8 + 4 + s, 1, s, n * 2 + 1)
                    elif not last:
                        proj_hi(n * 8 + 4 + s, 0, s - 4, n * 2 + 2)
                    if s >= 3:
                        ctx_hi(g - 3, s - 3, n)

            with act.Fori(0, PH) as ph:
                n0 = ph * PAIRS
                ln_out(ln_l1(ph), hT, lambda k: col("lnx_s", ph * 2 + k), lambda k: col("lnx_b", ph * 2 + k))
                act.wait_ge(ln_ev, ln_l1(ph)[1] + NT)
                act.activation(hTh[:, :, :], hT[:, :, :], ACT.Copy).then_inc(hsp, 1)
                for i in range(4):
                    proj_hi(n0 * 8 + i, 0, i, n0 * 2)
                pair(n0, True, False)
                with act.Fori(1, PAIRS - 1) as p:
                    pair(n0 + p, False, False)
                pair(n0 + (PAIRS - 1), False, True)
                tails(n0 + (PAIRS - 1))
            mlp(LN_MLP1, 1, ACT.Gelu, lambda k: col("lnm_s", k), lambda k: col("lnm_b", k),
                lambda f: col("b_fc1", f))

        @block.vector
        def _(dve):
            count_reg = dve.alloc_register()
            other_reg = dve.alloc_register()
            start_counts(dve, v_t, c_lo, t_lo)
            def ln_stats(call):
                c, t0, n, x0 = call
                for t in range(n):
                    dve.bn_stats(stats[:, t, :], x_acc[:, ds(x0 + t, 1), :].rearrange(
                        "p a d -> p (a d)")).then_inc(ln_st, 1)
                for t in range(n):
                    count = held(dve, count_reg, t0 + t + 1)
                    dve.wait_ge(d_x, 16)
                    dve.wait_ge(ln_st, count)
                    dve.bn_aggr(mean_var[:, t, :], stats[:, t, :]).then_inc(ln_mv, 1)

            def ln_rows(call):
                c, t0, n, x0 = call
                dve.wait_ge(ln_rstd, c + 1)
                for t in range(n):
                    if t == 0 and not (isinstance(c, int) and c == 0):
                        dve.wait_ge(ln_mm, t0 // 2)
                    dve.tensor_scalar(xn[:, t, :], x_acc[:, ds(x0 + t, 1), :].rearrange("p a d -> p (a d)"),
                                      mean_var[:, t, 0:1], rstd[:, t:t + 1], ALU.subtract,
                                      ALU.mult).then_inc(ln_xn, 1)

            def layer_norm(call):
                ln_stats(call)
                ln_rows(call)

            def queries(unit, kind):
                u, m = unit
                dve.wait_ge(a_qmm, u + 1)
                dve.tensor_scalar(q0[:, m, :], bank[7 - m][:, 0:S], col(("bq_s", "bq_c")[kind], m),
                                  -float(HD0) ** -0.5, ALU.add, ALU.mult).then_inc(a_qev, 1)

            def take_mask(i, a):
                if i > 0:
                    loaded = held(dve, count_reg, i * 16 + 16)
                    used = held(dve, other_reg, a * (2 * H0))
                    dve.wait_ge(d_x, 16)
                    dve.wait_ge(a_u, used)
                    dve.wait_ge(d_m, loaded)
                else:
                    dve.wait_ge(d_m, 16)
                dve.tensor_copy(msk[:, :, :], msk_next[:, :, :]).then_inc(a_mask, 1)
                dve.tensor_scalar(pen[:, :, :], msk_next[:, :, :], -MASKED, MASKED, ALU.mult,
                                  ALU.add).then_inc(a_mask, 1)
                dve.wait_ge(a_mask, i * 2 + 2)

            def add_out0(a, b):
                dve.wait_ge(a_omm, a + 1)
                xs = x_acc[:, ds(b * QT, QT), :]
                dve.tensor_tensor(xs, xs, bank[7][:, :].rearrange("p (t d) -> p t d", t=QT), ALU.add).then_inc(a_x, 1)

            def row_sums(g, h):
                dve.wait_ge(a_p, g * 2 + 2)
                dve.reciprocal(rsum0[:, h % 4, :], psum0[:, h % 4, :]).then_inc(a_rs, 1)

            def attention0(a, kind, b, first, next):
                if first:
                    layer_norm(ln_l0(0, 0))
                    queries((0, 0), 0)
                    take_mask(0, 0)
                elif kind == 1:
                    take_mask(b + 1, a)
                for s in range(H0):
                    g = a * H0 + s
                    dve.wait_ge(a_s, g + 1)
                    dve.tensor_tensor(tm[s % 2][:, :, :].rearrange("p t k -> p (t k)"), bank[s % 2][:, :],
                                      msk[:, :, :].rearrange("p t k -> p (t k)"), ALU.mult).then_inc(a_t, 1)
                    if s >= 1 or not first:
                        row_sums(g - 1, (s - 1) % H0)
                    count = held(dve, count_reg, g + 1)
                    used = None if isinstance(g, int) and g < 2 else held(dve, other_reg, g * 2 - 2)
                    dve.wait_ge(a_mask, 2)
                    if used is not None:
                        dve.wait_ge(a_p, used)
                    dve.wait_ge(a_t, count)
                    for t in range(QT):
                        dve.tensor_tensor_reduce(um[s % 2][:, t, :], tm[s % 2][:, t, :], pen[:, t, :], 1.0,
                                                 3.0e38, ALU.add, ALU.min, umin[:, s % 2, t:t + 1]).then_inc(a_u, 1)
                    if s == 1:
                        queries((a * 2 + 1, 1), kind)
                    if s == 4 and next is not None:
                        if next[0] == 1:
                            count = held(dve, count_reg, a - 2)
                            dve.wait_ge(d_x, 16)
                            dve.wait_ge(a_x, count)
                        ln_stats(ln_l0(a + 1, next[1]))
                    if s == 6 and next is not None:
                        ln_rows(ln_l0(a + 1, next[1]))
                    if s == 7 and not first:
                        add_out0(a - 1, before(a, kind, b)[1])
                    if s == 9 and next is not None:
                        queries((a * 2 + 2, 0), next[0])
                if next is None:
                    row_sums(a * H0 + H0 - 1, H0 - 1)
                    add_out0(a, b)
                    dve.wait_ge(a_x, a + 1)

            dve.wait_ge(d_x, 16)
            dve.wait_ge(d_vec, 16)
            dve.wait_ge(d_const, 16)
            dve.wait_ge(enc_mm, NT // 2)
            all_l0(attention0)(dve)

            def mlp(call, m):
                layer_norm(call)
                for c in range(TOK // CH):
                    for j in range(2):
                        g = 2 * (2 * m + c) + j
                        dve.wait_ge(m_down, g + 1)
                        xs = x_acc[:, 4 * c + 2 * j:4 * c + 2 * j + 2, :]
                        dve.tensor_tensor(xs, xs, bank[4 + j][:, :].rearrange("p (t d) -> p t d", t=2),
                                          ALU.add).then_inc(m_x, 1)

            mlp(LN_MLP0, 0)
            dve.wait_ge(m_x, NT // 2)

            def proj_lo(grp, hh, i, head):
                c = i // 2
                dve.wait_ge(g_hi, grp + 1)
                if i % 2 == 0:
                    dve.scalar_tensor_tensor(out=ql[:, hh, c * CH:(c + 1) * CH], in0=bank[6][:, :],
                                             scalar=col("bq", head), in1=qh[:, hh, c * CH:(c + 1) * CH],
                                             op0=ALU.add, op1=ALU.subtract).then_inc(g_lo, 1)
                else:
                    dve.scalar_tensor_tensor(out=kl[:, hh, 2 * c:2 * c + 2, 0:S],
                                             in0=bank[7][:, :].rearrange("p (b s) -> p b s", b=2),
                                             scalar=col("bk", head), in1=kh[:, hh, 2 * c:2 * c + 2, 0:S],
                                             op0=ALU.add, op1=ALU.subtract).then_inc(g_lo, 1)

            def pt_lo(g, s):
                dve.wait_ge(t_hi, g + 1)
                dve.tensor_tensor(ptl[s % 2][:, :, :].rearrange("p t k -> p (t k)"), bank[4][:, :],
                                  pth[s % 2][:, :, :].rearrange("p t k -> p (t k)"), ALU.subtract).then_inc(t_lo, 1)

            def ctx_lo(g, s, n):
                hh, b = s // B, s % B
                dve.wait_ge(c_hi, g + 1)
                dve.scalar_tensor_tensor(out=cl[:, hh, b * S:(b + 1) * S], in0=bank[5][:, 0:S],
                                         scalar=col("bias_v", n * 2 + hh), in1=ch[:, hh, b * S:(b + 1) * S],
                                         op0=ALU.add, op1=ALU.subtract).then_inc(c_lo, 1)

            def row_max(g, s):
                dve.wait_ge(s_mm, PAST + g + 1)
                for t in range(QT):
                    dve.tensor_reduce(mx[:, s % 4, t:t + 1], bank[2 * (s % 2) + t][:, 0:S + 1], AX.X,
                                      ALU.max).then_inc(s_max, 1)
                dve.wait_ge(s_max, g * 2 + 2)
                dve.tensor_scalar(nm[:, s % 4, :], mx[:, s % 4, :], -float(HD1) ** -0.5, None,
                                  ALU.mult).then_inc(s_nm, 1)

            def row_recip(g, s):
                dve.wait_ge(s_exp, g * 2 + 2)
                dve.reciprocal(rs[:, s % 4, :], sums[:, s % 4, :]).then_inc(s_rs, 1)

            def values(n, j):
                dve.wait_ge(v_mm, PAST + n * 4 + j + 1)
                if j == 0:
                    dve.wait_ge(w_vb, n + 1)
                if j >= 2:
                    dve.wait_ge(v_lo, n * 4 + j - 1)
                dve.tensor_tensor(vt[j % 2][:, :, :], bank[6 + j % 2][:, :].rearrange("p (t m) -> p t m", t=2),
                                  v_bias[:, :].unsqueeze(1).to_broadcast([P, 2, 2 * HD1]), ALU.add).then_inc(v_t, 1)

            def add_out(n):
                for j in range(B):
                    dve.wait_ge(o_mm, PAST + n * 4 + j + 1)
                    xs = x_acc[:, 2 * j:2 * j + 2, :]
                    dve.tensor_tensor(xs, xs, bank[6 + j % 2][:, :].rearrange("p (t d) -> p t d", t=2),
                                      ALU.add).then_inc(o_x, 1)

            def pair(n, first, last):
                g = n * STEPS
                if not first:
                    pt_lo(g - 2, 6)
                    ctx_lo(g - 3, 5, n - 1)
                values(n, 0)
                if not first:
                    pt_lo(g - 1, 7)
                    ctx_lo(g - 2, 6, n - 1)
                values(n, 1)
                if not first:
                    ctx_lo(g - 1, 7, n - 1)
                values(n, 2)
                values(n, 3)
                if not first:
                    add_out(n - 1)
                for s in range(STEPS):
                    g = n * STEPS + s
                    row_max(g, s)
                    if s >= 2:
                        pt_lo(g - 2, s - 2)
                    if s < 4:
                        proj_lo(n * 8 + 4 + s, 1, s, n * 2 + 1)
                    elif not last:
                        proj_lo(n * 8 + 4 + s, 0, s - 4, n * 2 + 2)
                    if s >= 3:
                        ctx_lo(g - 3, s - 3, n)
                    row_recip(g, s)

            with dve.Fori(0, PH) as ph:
                n0 = ph * PAIRS
                layer_norm(ln_l1(ph))
                dve.wait_ge(hsp, ph * 2 + 1)
                dve.tensor_tensor(hTl[:, :, :], hT[:, :, :], hTh[:, :, :], ALU.subtract).then_inc(hsp, 1)
                for i in range(4):
                    proj_lo(n0 * 8 + i, 0, i, n0 * 2)
                pair(n0, True, False)
                with dve.Fori(1, PAIRS - 1) as p:
                    pair(n0 + p, False, False)
                pair(n0 + (PAIRS - 1), False, True)
                g = (n0 + PAIRS) * STEPS
                pt_lo(g - 2, 6)
                ctx_lo(g - 3, 5, n0 + (PAIRS - 1))
                pt_lo(g - 1, 7)
                ctx_lo(g - 2, 6, n0 + (PAIRS - 1))
                ctx_lo(g - 1, 7, n0 + (PAIRS - 1))
                add_out(n0 + (PAIRS - 1))
                dve.wait_ge(o_x, (n0 + PAIRS) * 4)
            mlp(LN_MLP1, 1)

        @block.tensor
        def _(pe):
            count_reg = pe.alloc_register()
            start_counts(pe, s_mm, g_mm, v_mm, o_mm, pv_mm)
            pe.wait_ge(d_const, 16)
            pe.wait_ge(d_enc, 16)

            def transposes(src, j, bk, signal):
                for k in range(KD):
                    for t in range(2):
                        last = pe.transpose(bank[bk][:, k * S + t * P:k * S + (t + 1) * P],
                                            src[:, 2 * j + t, k * P:(k + 1) * P], ident)
                last.then_inc(signal, 1)

            for j in range(NT // 2):
                if j >= 2:
                    pe.wait_ge(enc_ev, 2 * (j - 1))
                transposes(xn, j, j % 2, enc_mm)

            def layer_norm(call):
                _, t0, n, _ = call
                for j in range(n // 2):
                    pe.wait_ge(ln_xn, t0 + 2 * j + 2)
                    if j >= 2:
                        pe.wait_ge(ln_ev, t0 + 2 * j - 2)
                    transposes(xn, j, 6 + j % 2, ln_mm)

            def mm_bias(dst, r, first=True):
                pe.matmul(dst, ones[0:1, :], row[0:1, ds(r, 1), :].rearrange("p a d -> p (a d)"),
                          start=first, stop=False)

            def source(kind):
                return ((w_qkv, D, 2 * D, hb), (w_kv, 0, D, encb))[kind]

            def queries(unit, kind):
                u, m = unit
                wq = (w_qkv, w_q)[kind]
                for k in range(KD):
                    last = pe.matmul(bank[7 - m][:, 0:S], wq[:, k, m * P:(m + 1) * P], hb[:, k, :],
                                     start=(k == 0), stop=(k == KD - 1))
                last.then_inc(a_qmm, 1)

            def keys(unit, kind):
                u, m = unit
                w, koff, _, src = source(kind)
                for k in range(KD):
                    last = pe.matmul(bank[6 + m][:, 0:S], w[:, k, koff + m * P:koff + (m + 1) * P], src[:, k, :],
                                     start=(k == 0), stop=(k == KD - 1))
                last.then_inc(a_kmm, 1)

            def vals(unit, kind):
                u, m = unit
                w, _, voff, src = source(kind)
                for t in range(QT):
                    for k in range(KD):
                        last = pe.matmul(bank[7 - m][:, t * P:(t + 1) * P], src[:, k, t * P:(t + 1) * P],
                                         w[:, k, voff + m * P:voff + (m + 1) * P], start=(k == 0), stop=(k == KD - 1))
                last.then_inc(a_vmm, 1)

            def scores0(a, s):
                g = a * H0 + s
                if s % HG == 0:
                    pe.wait_ge(a_qev, a * 2 + s // HG + 1)
                pe.wait_ge(a_kp, g + 1)
                if not (isinstance(g, int) and g < 2):
                    pe.wait_ge(a_t, g - 1)
                for t in range(QT):
                    last = pe.matmul(bank[s % 2][:, t * S:(t + 1) * S], q0[:, s // HG, t * P:(t + 1) * P],
                                     kp[s % 4][:, :], start=True, stop=True)
                last.then_inc(a_s, 1)

            def turn0(g, h):
                pe.wait_ge(a_pn, g * 2 + 2)
                if not (isinstance(g, int) and g < 2):
                    pe.wait_ge(a_tev, g - 1)
                for kt in range(QT):
                    for t in range(QT):
                        last = pe.transpose(bank[2 + h % 2][:, kt * S + t * P:kt * S + (t + 1) * P],
                                            pn0[h % 4][:, t, kt * P:(kt + 1) * P], ident)
                last.then_inc(a_tmm, 1)

            def pv0(a, h):
                g, m, j = a * H0 + h, h // HG, h % HG
                if j == 0:
                    pe.wait_ge(a_vev, a * 4 + 2 * m + 2)
                    if not (isinstance(a, int) and a == 0):
                        pe.wait_ge(a_cev, a * 2 + m - 1)
                pe.wait_ge(a_tev, g + 1)
                at = h * (HD0 + P) - j * HD0
                for kt in range(QT):
                    last = pe.matmul(bank[4 + m][:, 0:S],
                                     v0[:, kt, :, :].rearrange("p h d -> p (h d)")[:, at:at + P],
                                     pt0[h % 2][:, kt, :], start=(j == 0 and kt == 0),
                                     stop=(j == HG - 1 and kt == QT - 1))
                last.then_inc(a_pv, 1)

            def out0(a, kind, t):
                if t == 0:
                    pe.wait_ge(a_cev, a * 2 + 2)
                    if not (isinstance(a, int) and a == 0):
                        pe.wait_ge(a_x, a)
                mm_bias(bank[7][:, t * D:(t + 1) * D], kind)
                for k in range(KD):
                    last = pe.matmul(bank[7][:, t * D:(t + 1) * D], ct0[:, k, t * P:(t + 1) * P],
                                     (w_ao, w_co)[kind][:, k, :], start=False, stop=(k == KD - 1))
                if t == QT - 1:
                    last.then_inc(a_omm, 1)

            def attention0(a, kind, b, first, next):
                if first:
                    layer_norm(ln_l0(0, 0))
                    pe.wait_ge(ln_ev, 2)
                    queries((0, 0), 0)
                    keys((0, 0), 0)
                    pe.wait_ge(a_qev, 1)
                    vals((0, 0), 0)
                for s in range(H0):
                    scores0(a, s)
                    if s >= TURN_LAG:
                        turn0(a * H0 + s - TURN_LAG, s - TURN_LAG)
                    elif not first:
                        turn0(a * H0 + s - TURN_LAG, s - TURN_LAG + H0)
                    if s >= PV_LAG:
                        pv0(a, s - PV_LAG)
                    elif not first:
                        pv0(a - 1, s - PV_LAG + H0)
                    if s == 1:
                        queries((a * 2 + 1, 1), kind)
                    if s == 2:
                        pe.wait_ge(a_vev, a * 4 + 2)
                        keys((a * 2 + 1, 1), kind)
                    if s == 3:
                        pe.wait_ge(a_qev, a * 2 + 2)
                        vals((a * 2 + 1, 1), kind)
                    if s == 5:
                        pe.wait_ge(a_kev, a * 2 + 2)
                    if s in (5, 6) and not first:
                        out0(a - 1, before(a, kind, b)[0], s - 5)
                    if next is not None:
                        if s == 7:
                            pe.wait_ge(a_vev, a * 4 + 4)
                            layer_norm(ln_l0(a + 1, 0))
                        if s == 9:
                            pe.wait_ge(ln_ev, a * 2 + 4)
                            if not first:
                                pe.wait_ge(a_x, a)
                            queries((a * 2 + 2, 0), next[0])
                        if s == 10:
                            if next[0] == 1:
                                pe.wait_ge(a_encb, a - (B - 2))
                            keys((a * 2 + 2, 0), next[0])
                        if s == 12:
                            pe.wait_ge(a_qev, a * 2 + 3)
                            vals((a * 2 + 2, 0), next[0])
                if next is None:
                    for s in range(H0, H0 + PV_LAG):
                        if s - TURN_LAG < H0:
                            turn0(a * H0 + s - TURN_LAG, s - TURN_LAG)
                        pv0(a, s - PV_LAG)
                    for t in range(QT):
                        out0(a, kind, t)

            pe.wait_ge(d_w0, 5 * 16)
            pe.wait_ge(d_row, 16)
            pe.wait_ge(init, 3)
            all_l0(attention0)(pe)

            def mlp(call, m, bias_row):
                layer_norm(call)
                pe.wait_ge(ln_ev, call[1] + NT)
                for c in range(TOK // CH):
                    for f in range(NF):
                        n = (2 * m + c) * NF + f
                        if c > 0 or f >= 4:
                            pe.wait_ge(m_gelu, n - 3)
                        for k in range(KD):
                            last = pe.matmul(bank[f % 4][:, :], w_up[:, k, f * P:(f + 1) * P],
                                             hT[:, k, c * CH:(c + 1) * CH], start=(k == 0), stop=(k == KD - 1))
                        last.then_inc(m_up, 1)
                    pe.wait_ge(m_gelu, (2 * m + c + 1) * NF)
                    for j in range(2):
                        if c > 0:
                            pe.wait_ge(m_x, 2 * (2 * m + c) + j - 1)
                        for t in range(2):
                            dst = bank[4 + j][:, t * D:(t + 1) * D]
                            mm_bias(dst, bias_row)
                            for f in range(NF):
                                last = pe.matmul(dst, gelu[:, f, (2 * j + t) * P:(2 * j + t + 1) * P], w_down[:, f, :],
                                                 start=False, stop=(f == NF - 1))
                        last.then_inc(m_down, 1)

            pe.wait_ge(d_up, 32)
            mlp(LN_MLP0, 0, 2)

            def mm3(dst, lh, ll, rh, rl, start, stop):
                pe.matmul(dst, lh, rh, start=start, stop=False)
                pe.matmul(dst, ll, rh, start=False, stop=False)
                return pe.matmul(dst, lh, rl, start=False, stop=stop)

            def proj(hh, i):
                c, w = i // 2, i % 2
                src_h, src_l = ((hTh, hTl), (encTh, encTl))[w]
                for k in range(KD):
                    last = mm3(bank[6 + w][:, :], wqk_h[hh][:, w, k, :], wqk_l[hh][:, w, k, :],
                               src_h[:, k, c * CH:(c + 1) * CH], src_l[:, k, c * CH:(c + 1) * CH],
                               k == 0, k == KD - 1)
                last.then_inc(g_mm, 1)

            def scores(g, s):
                hh, b = s // B, s % B
                for t in range(QT):
                    at = b * S + t * P
                    last = mm3(bank[2 * (s % 2) + t][:, 0:SP], qh[:, hh, at:at + P], ql[:, hh, at:at + P],
                               kh[:, hh, b, :], kl[:, hh, b, :], True, True)
                last.then_inc(s_mm, 1)

            def turn(g, s):
                pe.wait_ge(s_pn, g * 2 + 2)
                for kt in range(QT):
                    for t in range(QT):
                        last = pe.transpose(bank[4][:, kt * S + t * P:kt * S + (t + 1) * P],
                                            pn[s % 2][:, t, kt * P:(kt + 1) * P], ident)
                last.then_inc(t_mm, 1)

            def pv(g, s, n):
                hh, b = s // B, s % B
                pe.wait_ge(t_lo, PAST + g + 1)
                pe.wait_ge(v_lo, n * 4 + b + 1)
                pe.wait_ge(c_lo, PAST + g)
                for kt in range(QT):
                    last = mm3(bank[5][:, 0:S], vh[:, 2 * b + kt, hh * P:(hh + 1) * P],
                               vl[:, 2 * b + kt, hh * P:(hh + 1) * P], pth[s % 2][:, kt, :], ptl[s % 2][:, kt, :],
                               kt == 0, kt == QT - 1)
                last.then_inc(pv_mm, 1)

            def values(n, j, free, count):
                pe.wait_ge(free, count)
                for t in range(2):
                    at = (2 * j + t) * P
                    for k in range(KD):
                        last = mm3(bank[6 + j % 2][:, t * S:(t + 1) * S], encTh[:, k, at:at + P],
                                   encTl[:, k, at:at + P], wv_h[:, k, :], wv_l[:, k, :], k == 0, k == KD - 1)
                last.then_inc(v_mm, 1)

            def attn_out(n, bias_row):
                pe.wait_ge(c_lo, PAST + (n + 1) * STEPS)
                pe.wait_ge(w_o, n * 2 + 2)
                for j in range(B):
                    if j >= 2:
                        count = held(pe, count_reg, n * 4 + j - 1)
                        pe.wait_ge(d_row, 16)
                        pe.wait_ge(o_x, count)
                    for t in range(2):
                        at = (2 * j + t) * P
                        dst = bank[6 + j % 2][:, t * D:(t + 1) * D]
                        if bias_row is not None:
                            mm_bias(dst, bias_row)
                        for hh in range(2):
                            last = mm3(dst, ch[:, hh, at:at + P], cl[:, hh, at:at + P], wo_h[:, hh, :],
                                       wo_l[:, hh, :], bias_row is None and hh == 0, hh == 1)
                    last.then_inc(o_mm, 1)

            def pair(n, first, last):
                g = n * STEPS
                if not first:
                    pe.wait_ge(t_lo, PAST + g - 2)
                    turn(g - 2, 6)
                    pv(g - 3, 5, n - 1)
                pe.wait_ge(w_v, n * 2 + 2)
                values(n, 0, g_lo, n * 8 + 3)
                if not first:
                    pe.wait_ge(t_lo, PAST + g - 1)
                    turn(g - 1, 7)
                    pv(g - 2, 6, n - 1)
                values(n, 1, g_lo, n * 8 + 4)
                if not first:
                    pv(g - 1, 7, n - 1)
                values(n, 2, v_t, PAST + n * 4 + 1)
                values(n, 3, v_t, PAST + n * 4 + 2)
                pe.wait_ge(v_t, PAST + n * 4 + 4)
                if not first:
                    attn_out(n - 1, None)
                for s in range(STEPS):
                    g = n * STEPS + s
                    if s == 0:
                        pe.wait_ge(kb, n * 4 + 2)
                        pe.wait_ge(w_qk, n * 4 + 4)
                    if s == 4:
                        pe.wait_ge(kb, n * 4 + 4)
                    if s % 4 == 0:
                        pe.wait_ge(g_lo, n * 8 + s + 2 if s else n * 8 + 4)
                    if s % 4 == 2:
                        pe.wait_ge(g_lo, n * 8 + s + 2)
                    if s >= 2:
                        pe.wait_ge(s_exp, g * 2 - 2)
                    scores(g, s)
                    if s >= 2:
                        pe.wait_ge(t_lo, PAST + g - 2)
                        turn(g - 2, s - 2)
                    if s < 4 or not last:
                        if s == 4:
                            pe.wait_ge(w_qk, n * 4 + 6)
                        if s >= 2:
                            pe.wait_ge(g_lo, n * 8 + s + 3)
                        elif not first:
                            pe.wait_ge(o_x, n * 4 + s - 1)
                        proj(s // 4 ^ 1, s % 4)
                    if s >= 3:
                        pv(g - 3, s - 3, n)

            pe.wait_ge(enc_lo, 1)
            with pe.Fori(0, PH) as ph:
                n0 = ph * PAIRS
                layer_norm(ln_l1(ph))
                pe.wait_ge(hsp, ph * 2 + 2)
                pe.wait_ge(ln_ev, ln_l1(ph)[1] + NT)
                pe.wait_ge(w_qk, n0 * 4 + 2)
                for i in range(4):
                    if i >= 2:
                        pe.wait_ge(g_lo, n0 * 8 + i - 1)
                    proj(0, i)
                pair(n0, True, False)
                with pe.Fori(1, PAIRS - 1) as p:
                    pair(n0 + p, False, False)
                pair(n0 + (PAIRS - 1), False, True)
                g = (n0 + PAIRS) * STEPS
                n = n0 + (PAIRS - 1)
                pe.wait_ge(t_lo, PAST + g - 2)
                turn(g - 2, 6)
                pv(g - 3, 5, n)
                pe.wait_ge(t_lo, PAST + g - 1)
                turn(g - 1, 7)
                pv(g - 2, 6, n)
                pv(g - 1, 7, n)
                attn_out(n, ph + 3)
            pe.wait_ge(d_up2, 32)
            mlp(LN_MLP1, 1, 5)


def kernel(**inputs):
    import numpy as _np
    import concourse.bacc as _bacc
    from concourse import mybir as _mybir
    from concourse.bass_utils import run_bass_kernel_spmd as _run

    a = {k: _np.ascontiguousarray(v) for k, v in inputs.items()}
    L0 = {k[len("L0_xattn_"):]: v for k, v in a.items() if k.startswith("L0_")}
    L1 = {k[len("L1_xattn_"):]: v for k, v in a.items() if k.startswith("L1_")}

    def cols(v):
        return v.reshape(-1, P).T

    bqkv, bkv = L0["b_qkv"], L0["b_kv"]
    packs = {
        "ln1_s": L0["ln1_s"], "ln1_b": L0["ln1_b"], "bq_s": bqkv[:D], "bk_s": bqkv[D:2 * D], "bv_s": bqkv[2 * D:],
        "ln2_s": L0["ln2_s"], "ln2_b": L0["ln2_b"], "bq_c": L0["b_q"], "bk_c": bkv[:D], "bv_c": bkv[D:],
        "ln3_s": L0["ln3_s"], "ln3_b": L0["ln3_b"], "b1": L0["b1"],
        "lnx_s": _np.concatenate([L1["ln1_scale"], L1["ln2_scale"]]),
        "lnx_b": _np.concatenate([L1["ln1_offset"], L1["ln2_offset"]]),
        "bq": _np.concatenate([L1["bq1"], L1["bq2"]]), "bk": _np.concatenate([L1["bk1"], L1["bk2"]]),
        "bias_k": _np.concatenate([L1["bias_k1"].reshape(-1), L1["bias_k2"].reshape(-1)]),
        "bias_v": _np.concatenate([L1["bias_v1"].reshape(-1), L1["bias_v2"].reshape(-1)]),
        "lnm_s": L1["ln_mlp_scale"], "lnm_b": L1["ln_mlp_offset"], "b_fc1": L1["b_fc1"],
    }
    vec = _np.concatenate([cols(packs[k]) for k in VEC], axis=1)
    row = _np.stack([L0["b_ao"], L0["b_co"], L0["b2"], L1["bo1"], L1["bo2"], L1["b_fc2"]])[None]
    rows_of = _np.arange(P)[:, None] // HD0 == _np.arange(HG)[None]
    consts = _np.concatenate([_np.eye(P), rows_of], axis=1).astype(_np.float32)

    def heads(w):
        return w.reshape(KD, P, H1, HD1).transpose(2, 1, 0, 3)

    wqk = _np.stack([_np.stack([heads(L1[f"wq{i}"]), heads(L1[f"wk{i}"])], axis=2) for i in (1, 2)])
    wqk = wqk.reshape(PH * H1, P, 2 * KD * HD1)
    wv = _np.stack([L1[f"wv{i}"].reshape(KD, P, PAIRS, 2 * HD1).transpose(2, 1, 0, 3) for i in (1, 2)])
    wv = wv.reshape(PH * PAIRS, P, KD * 2 * HD1)
    wo = _np.stack([L1[f"wo{i}"].reshape(PAIRS, 2, HD1, D).transpose(0, 2, 1, 3) for i in (1, 2)])
    wo = wo.reshape(PH * PAIRS, P, 2 * D)
    vb = _np.stack([_np.stack([L1[f"bv{i}"].reshape(PAIRS, 2 * HD1), L1[f"bias_v{i}"].reshape(PAIRS, 2 * HD1)],
                              axis=1) for i in (1, 2)]).reshape(PH * PAIRS, 4 * HD1)
    feeds = {
        "x": a["x"].reshape(TOK, D), "enc": a["ctx_2048"].reshape(TOK, D),
        "mask_self": a["mask_1x1xSxS2_fc1"].reshape(S, S), "mask_cross": a["mask_Bx1xSxS2_ff1"].reshape(B * S, S),
        "consts": consts, "vec": vec, "row": row,
        "w_qkv": L0["w_qkv"], "w_ao": L0["w_ao"], "w_q": L0["w_q"], "w_kv": L0["w_kv"], "w_co": L0["w_co"],
        "w1": L0["w1"], "w2": L0["w2"], "wf1": L1["w_fc1"], "wf2": L1["w_fc2"],
        "wqk": wqk, "wv": wv, "wo": wo, "vb": vb,
    }
    nc = _bacc.Bacc("TRN2", target_bir_lowering=False, num_devices=1)
    arrays, args = {}, []
    for name, v in feeds.items():
        v = _np.ascontiguousarray(v)
        arrays[f"in_{name}"] = v
        args.append(nc.dram_tensor(f"in_{name}", v.shape, _mybir.dt.from_np(v.dtype), kind="ExternalInput").ap())
    out = nc.dram_tensor("out_x", (TOK, D), _mybir.dt.float32, kind="ExternalOutput").ap()
    build(nc, *args, out)
    r = _run(nc, [arrays], core_ids=[0])
    return r.results[0]["out_x"].reshape(B, S, D)
```

```python
from contextlib import ExitStack

import concourse.bass as bass
import concourse.mybir as mybir

P = 128
B, S, D = 4, 256, 256
TOK = B * S
NT = TOK // P
KD = D // P
QT = S // P
H0, HD0 = 16, 16
H1, HD1 = 16, 128
FF = 1024
NF = FF // P
CH = 512
PAIRS = H1 // 2
PH = 2
STEPS = 2 * B
EPS = 1e-5
MASKED = 10000.0
HG = P // HD0
TURN_LAG, PV_LAG = 3, 4
SP = S + 2

VEC = {}
_at = 0
for _name, _n in (("ln1_s", 2), ("ln1_b", 2), ("bq_s", 2), ("bk_s", 2), ("bv_s", 2), ("ln2_s", 2), ("ln2_b", 2),
                  ("bq_c", 2), ("bk_c", 2), ("bv_c", 2), ("ln3_s", 2), ("ln3_b", 2), ("b1", 8),
                  ("lnx_s", 6), ("lnx_b", 6), ("bq", 32), ("bk", 32), ("bias_k", 32), ("bias_v", 32),
                  ("b_fc1", 8)):
    VEC[_name] = _at
    _at += _n
NVEC = _at
ROWS = ("b_ao", "b_co", "b2", "bo1", "bo2", "b_fc2")


def build(nc, x_in, enc_in, mask_self, mask_cross, consts, vec_in, row_in, w_qkv_in, w_ao_in, w_q_in, w_kv_in,
          w_co_in, w1_in, w2_in, wf1_in, wf2_in, wqk_in, wv_in, wo_in, vb_in, out):
    f32, f32r = mybir.dt.float32, mybir.dt.float32r
    ALU = mybir.AluOpType
    ACT = mybir.ActivationFunctionType
    AX = mybir.AxisListType
    ds = bass.ds

    with ExitStack() as ctx:
        def sb(name, shape, dt=f32):
            return in_turn.enter_context(nc.sbuf_tensor(name, shape, dt))

        def sem(name):
            return ctx.enter_context(nc.semaphore(name))

        in_turn = ctx
        x_acc = sb("x_acc", [P, NT, D])
        encT = sb("encT", [P, KD, TOK], f32)
        encTh = sb("encTh", [P, KD, TOK], f32r)
        encTl = sb("encTl", [P, KD, TOK], f32r)
        const = sb("const", [P, P + HG])
        ident = const[:, 0:P]
        head_rows = [const[:, P + j:P + j + 1] for j in range(HG)]
        vec = sb("vec", [P, NVEC])
        row_hi_lo = sb("row_hi_lo", [2, len(ROWS), D], f32r)
        ones = sb("ones", [2, P])
        ones_r = sb("ones_r", [2, P], f32r)
        neg_half = sb("neg_half", [P, NT])
        zeros = sb("zeros", [P, 1])
        stats = sb("stats", [P, NT, 6])
        mean_var = sb("mean_var", [P, NT, 2])
        var_eps = sb("var_eps", [P, NT])
        rstd = sb("rstd", [P, NT])
        xn = sb("xn", [P, NT, D])
        w_up = sb("w_up", [P, KD, FF])
        w_down = sb("w_down", [P, NF, D])
        hT = sb("hT", [P, KD, TOK])
        enc_tok = hT[:, :, :].rearrange("p k (h n) -> p (k h) n", n=D)
        raw_qk = [sb(f"raw_qk{i}", [P, 2, KD, HD1]) for i in range(2)]
        raw_v = sb("raw_v", [P, KD, 2 * HD1])
        raw_o = sb("raw_o", [P, 2, D])
        raw_vb = sb("raw_vb", [P, 2, 2 * HD1])
        bkh = sb("bkh", [P, PH * H1], f32r)
        bkl = sb("bkl", [P, PH * H1], f32r)
        in_turn = ExitStack()
        gelu_h = sb("gelu_h", [P, NF, CH], f32r)
        in_turn.close()
        in_turn = ExitStack()
        row = sb("row", [2, len(ROWS), D])
        row_h = sb("row_h", [2, len(ROWS), D], f32r)
        in_turn.close()
        in_turn = ctx
        ch = sb("ch", [P, 2, TOK], f32r)
        cl = sb("cl", [P, 2, TOK], f32r)
        first = ExitStack()
        in_turn = first
        w_qkv = sb("w_qkv", [P, KD, 3 * D])
        w_ao = sb("w_ao", [P, KD, D])
        w_q = sb("w_q", [P, KD, D])
        w_kv = sb("w_kv", [P, KD, 2 * D])
        hb = sb("hb", [P, KD, S])
        encb = sb("encb", [P, KD, S])
        q0h, q0l = sb("q0h", [P, KD, S], f32r), sb("q0l", [P, KD, S], f32r)
        kxh, kxl = sb("kxh", [P, KD, S], f32r), sb("kxl", [P, KD, S], f32r)
        kph = [sb(f"kph{i}", [P, S], f32r) for i in range(4)]
        kpl = [sb(f"kpl{i}", [P, S], f32r) for i in range(4)]
        v0 = sb("v0", [P, QT, H0, HD0 + P])
        msk_next, msk, pen = sb("msk_next", [P, QT, S]), sb("msk", [P, QT, S]), sb("pen", [P, QT, S])
        tm = [sb(f"tm{i}", [P, QT, S]) for i in range(2)]
        um = [sb(f"um{i}", [P, QT, S]) for i in range(2)]
        umin = sb("umin", [P, 2, QT])
        p0 = [sb(f"p0_{i}", [P, QT, S]) for i in range(2)]
        psum0 = sb("psum0", [P, 4, QT])
        rsum0 = sb("rsum0", [P, 4, QT])
        pn0 = [sb(f"pn0_{i}", [P, QT, S]) for i in range(4)]
        pt0 = [sb(f"pt0_{i}", [P, QT, S]) for i in range(2)]
        ct0 = sb("ct0", [P, KD, S])
        row_top = sb("row_top", [2, len(ROWS), D])
        w_co = sb("w_co", [P, KD, D])
        first.close()
        in_turn = ctx
        hTh = sb("hTh", [P, KD, TOK], f32r)
        hTl = sb("hTl", [P, KD, TOK], f32r)
        in_turn = ExitStack()
        w_up_h, w_up_l = sb("w_up_h", [P, KD, FF], f32r), sb("w_up_l", [P, KD, FF], f32r)
        w_down_h, w_down_l = sb("w_down_h", [P, NF, D], f32r), sb("w_down_l", [P, NF, D], f32r)
        gelu_l = sb("gelu_l", [P, NF, CH], f32r)
        gelu = [sb(f"gelu{i}", [P, CH]) for i in range(2)]
        in_turn.close()
        in_turn = ctx
        qh = sb("qh", [P, 2, TOK], f32r)
        ql = sb("ql", [P, 2, TOK], f32r)
        kh = sb("kh", [P, 2, B, SP], f32r)
        kl = sb("kl", [P, 2, B, SP], f32r)
        vh = sb("vh", [P, NT, 2 * HD1], f32r)
        vl = sb("vl", [P, NT, 2 * HD1], f32r)
        pr = [sb(f"pr{i}", [P, QT, S + 1]) for i in range(4)]
        wqk_h = [sb(f"wqk_h{i}", [P, 2, KD, HD1], f32r) for i in range(2)]
        wqk_l = [sb(f"wqk_l{i}", [P, 2, KD, HD1], f32r) for i in range(2)]
        wv_h = sb("wv_h", [P, KD, 2 * HD1], f32r)
        wv_l = sb("wv_l", [P, KD, 2 * HD1], f32r)
        wo_h = sb("wo_h", [P, 2, D], f32r)
        wo_l = sb("wo_l", [P, 2, D], f32r)
        v_bias = sb("v_bias", [P, 2 * HD1])
        vt = [sb(f"vt{i}", [P, 2, 2 * HD1]) for i in range(2)]
        mx = sb("mx", [P, 4, QT])
        nm = sb("nm", [P, 4, QT])
        sums = sb("sums", [P, 4, QT])
        rs = sb("rs", [P, 4, QT])
        pn = [sb(f"pn{i}", [P, QT, S]) for i in range(2)]
        pth = [sb(f"pth{i}", [P, QT, S], f32r) for i in range(2)]
        ptl = [sb(f"ptl{i}", [P, QT, S], f32r) for i in range(2)]

        bank = [ctx.enter_context(nc.psum_tensor(f"bank{i}", [P, CH], f32)) for i in range(8)]

        d_wqkv = sem("d_wqkv")
        d_x0 = sem("d_x0")
        d_x, d_enc, d_const, d_vec, d_row = sem("d_x"), sem("d_enc"), sem("d_const"), sem("d_vec"), sem("d_row")
        d_m, d_w0, d_up = sem("d_m"), sem("d_w0"), sem("d_up")
        d_up2 = sem("d_up2")
        d_qk = [sem("d_qk0"), sem("d_qk1")]
        d_v, d_o, d_vb, d_out = sem("d_v"), sem("d_o"), sem("d_vb"), sem("d_out")
        b_ones, b_hi, b_lo, b_top, b_rows = (sem(n) for n in ("b_ones", "b_hi", "b_lo", "b_top", "b_rows"))
        init = sem("init")
        enc_mm, enc_ev = sem("enc_mm"), sem("enc_ev")
        enc_hi, enc_lo = sem("enc_hi"), sem("enc_lo")
        ln_st, ln_mv, ln_eps, ln_rstd, ln_xn = (sem(n) for n in ("ln_st", "ln_mv", "ln_eps", "ln_rstd", "ln_xn"))
        ln_mm, ln_ev = sem("ln_mm"), sem("ln_ev")
        h_hi, h_lo = sem("h_hi"), sem("h_lo")
        a_encb, a_mask = sem("a_encb"), sem("a_mask")
        a_qmm, a_qev, a_kmm, a_kev, a_vmm, a_vev = (sem(n) for n in ("a_qmm", "a_qev", "a_kmm", "a_kev", "a_vmm", "a_vev"))
        a_kp, a_s, a_t, a_u, a_p, a_rs, a_pn, a_tmm, a_tev, a_pv, a_cev = (sem(n) for n in (
            "a_kp", "a_s", "a_t", "a_u", "a_p", "a_rs", "a_pn", "a_tmm", "a_tev", "a_pv", "a_cev"))
        a_qhi, a_khi = sem("a_qhi"), sem("a_khi")
        a_zero = sem("a_zero")
        a_omm, a_x = sem("a_omm"), sem("a_x")
        m_up, m_gelu, m_ghi, m_glo, m_down, m_x = (sem(n) for n in ("m_up", "m_gelu", "m_ghi", "m_glo", "m_down", "m_x"))
        m_whi, m_wlo = sem("m_whi"), sem("m_wlo")
        w_qk, w_v, w_o, w_vb, kb = (sem(n) for n in ("w_qk", "w_v", "w_o", "w_vb", "kb"))
        g_mm, g_hi, g_lo = sem("g_mm"), sem("g_hi"), sem("g_lo")
        v_mm, v_t, v_hi, v_lo = sem("v_mm"), sem("v_t"), sem("v_hi"), sem("v_lo")
        s_mm, s_max, s_nm, s_exp, s_rs, s_pn = (sem(n) for n in ("s_mm", "s_max", "s_nm", "s_exp", "s_rs", "s_pn"))
        t_mm, t_hi, t_lo = sem("t_mm"), sem("t_hi"), sem("t_lo")
        pv_mm, c_hi, c_lo = sem("pv_mm"), sem("c_hi"), sem("c_lo")
        o_mm, o_x = sem("o_mm"), sem("o_x")

        PAST = 4

        def start_counts(eng, *signals):
            for signal in signals:
                eng.sem_inc(signal, PAST)

        def col(name, i=0):
            return vec[:, ds(VEC[name] + i, 1)]

        HALF = NT // 2

        def ln_l0(a, b):
            return (a, 2 * a, QT, 2 * b, 0)

        def ln_half(k, half):
            return (2 * B + 2 * k + half, 4 * B + NT * k + HALF * half, HALF, HALF * half, HALF * half)

        def before(a, kind, b):
            return (0, B - 1) if isinstance(a, int) and a == B else (kind, b - 1)

        def group_is_key(i):
            return i % 2 == 0

        def group_head(i):
            return (i % 4) // 2

        def held(eng, reg, value):
            if isinstance(value, int):
                return value
            eng.reg_mov(reg, value)
            return reg

        def all_l0(attention):
            def loop(eng):
                attention(0, 0, 0, True, (0, 1))
                with eng.Fori(1, B - 1) as b:
                    attention(b, 0, b, False, (0, b + 1))
                attention(B - 1, 0, B - 1, False, (1, 0))
                attention(B, 1, 0, False, (1, 1))
                with eng.Fori(1, B - 1) as b:
                    attention(b + B, 1, b, False, (1, b + 1))
                attention(2 * B - 1, 1, B - 1, False, None)
            return loop

        def weight_part(i):
            if i < NF // 2:
                at = slice(i * 2 * P, (i + 1) * 2 * P)
                return tuple(w[:, :, at] for w in (w_up, w_up_h, w_up_l))
            at = slice(2 * i - NF, 2 * i - NF + 2)
            return tuple(w[:, at, :] for w in (w_down, w_down_h, w_down_l))

        block = ctx.enter_context(nc.Block())

        @block.sync
        def _(sp):
            count_reg = sp.alloc_register()
            x_tiles = x_in.rearrange("(t p) d -> p t d", p=P)
            sp.dma_start(x_acc[:, 0:QT, :], x_tiles[:, 0:QT, :]).then_inc(d_x0, 16)
            sp.dma_start(const[:, :], consts).then_inc(d_const, 16)
            sp.dma_start(vec[:, :], vec_in).then_inc(d_vec, 16)
            sp.dma_start(row[:, :, :], row_in.to_broadcast([2, len(ROWS), D])).then_inc(d_row, 16)
            sp.dma_start(w_qkv[:, :, :], w_qkv_in.rearrange("(k p) n -> p k n", p=P)).then_inc(d_wqkv, 16)
            sp.dma_start(msk_next[:, :, :], mask_self.rearrange("(t p) k -> p t k", p=P)).then_inc(d_m, 16)
            sp.dma_start(x_acc[:, QT:NT, :], x_tiles[:, QT:NT, :]).then_inc(d_x, 16)
            sp.dma_start(enc_tok, enc_in.rearrange("(t p) d -> p t d", p=P)).then_inc(d_enc, 16)
            for wt, src in ((w_ao, w_ao_in), (w_q, w_q_in), (w_kv, w_kv_in), (w_co, w_co_in)):
                sp.dma_start(wt[:, :, :], src.rearrange("(k p) n -> p k n", p=P)).then_inc(d_w0, 16)
            sp.dma_start(w_up[:, :, :], w1_in.rearrange("(k p) n -> p k n", p=P)).then_inc(d_up, 16)
            sp.dma_start(w_down[:, :, :], w2_in.rearrange("(k p) n -> p k n", p=P)).then_inc(d_up, 16)

            def load_pair(n, first):
                for i in range(2):
                    if not first:
                        sp.wait_ge(w_qk, n * 4 + 2 * i - 2)
                    sp.dma_start(raw_qk[i][:, :, :, :], wqk_in[ds(n * 2 + i, 1)].rearrange(
                        "a p (c k m) -> p (a c) k m", c=2, k=KD)).then_inc(d_qk[i], 16)
                    if i == 0:
                        if not first:
                            sp.wait_ge(w_v, n * 2)
                        sp.dma_start(raw_v[:, :, :], wv_in[ds(n, 1)].rearrange(
                            "a p (k m) -> p (a k) m", k=KD)).then_inc(d_v, 16)
                        if not first:
                            sp.wait_ge(w_vb, n)
                        sp.dma_start(raw_vb[:, :, :], vb_in[ds(n, 1)].rearrange(
                            "a (c m) -> a c m", c=2).to_broadcast([P, 2, 2 * HD1])).then_inc(d_vb, 16)
                if not first:
                    sp.wait_ge(w_o, n * 2)
                sp.dma_start(raw_o[:, :, :], wo_in[ds(n, 1)].rearrange(
                    "a p (c m) -> p (a c) m", c=2)).then_inc(d_o, 16)

            load_pair(0, True)
            sp.wait_ge(a_mask, 2)
            sp.dma_start(msk_next[:, :, :], mask_cross[0:S, :].rearrange("(t p) k -> p t k", p=P)).then_inc(d_m, 16)
            with sp.Fori(1, B) as b:
                count = held(sp, count_reg, b * 2 + 2)
                sp.wait_ge(d_x, 16)
                sp.wait_ge(a_mask, count)
                sp.dma_start(msk_next[:, :, :], mask_cross[ds(b * S, S), :].rearrange(
                    "(t p) k -> p t k", p=P)).then_inc(d_m, 16)
            sp.wait_ge(m_wlo, NF)
            sp.dma_start(w_up[:, :, :], wf1_in.rearrange("(k p) n -> p k n", p=P)).then_inc(d_up2, 16)
            sp.dma_start(w_down[:, :, :], wf2_in.rearrange("(k p) n -> p k n", p=P)).then_inc(d_up2, 16)
            with sp.Fori(1, PH * PAIRS) as n:
                load_pair(n, False)
            for j in range(NT // 2):
                sp.wait_ge(m_x, NT // 2 + j + 1)
                sp.dma_start(out[2 * j * P:(2 * j + 2) * P, :].rearrange("(t p) d -> p t d", p=P),
                             x_acc[:, 2 * j:2 * j + 2, :]).then_inc(d_out, 16)
            sp.wait_ge(d_out, 16 * (NT // 2))

        @block.gpsimd
        def _(pool):
            count_reg = pool.alloc_register()
            other_reg = pool.alloc_register()
            start_counts(pool, v_lo)
            pool.memset(ones[:, :], 1.0).then_inc(init, 1)
            pool.memset(neg_half[:, :], -0.5).then_inc(init, 1)
            pool.memset(zeros[:, :], 0.0).then_inc(init, 1)
            pool.wait_ge(init, 3)
            pool.wait_ge(d_vec, 16)
            pool.tensor_scalar(bkh[:, :], vec[:, VEC["bias_k"]:VEC["bias_k"] + PH * H1], 1.0, 1.0,
                               ALU.mult, ALU.mult).then_inc(init, 1)
            pool.wait_ge(init, 4)
            pool.tensor_tensor(bkl[:, :], vec[:, VEC["bias_k"]:VEC["bias_k"] + PH * H1], bkh[:, :],
                               ALU.subtract).then_inc(init, 1)

            def layer_norm(call):
                c, t0, n, _, at = call
                count = held(pool, count_reg, t0 + n)
                pool.wait_ge(init, 3)
                pool.wait_ge(ln_mv, count)
                pool.tensor_scalar(var_eps[:, at:at + n], mean_var[:, at:at + n, 1], 1.0, EPS, ALU.mult,
                                   ALU.add).then_inc(ln_eps, 1)
                pool.wait_ge(ln_eps, c + 1)
                pool.tensor_tensor(rstd[:, at:at + n], var_eps[:, at:at + n], neg_half[:, 0:n], ALU.pow).then_inc(ln_rstd, 1)

            pool.wait_ge(d_const, 16)

            def key_rows(g, h, unit):
                if h % HG == 0:
                    count = held(pool, count_reg, unit + 1)
                else:
                    count = None
                if isinstance(g, int) and g < 4:
                    used = None
                else:
                    used = held(pool, other_reg, g - 3)
                pool.wait_ge(init, 3)
                if count is not None:
                    pool.wait_ge(a_kev, count)
                if used is not None:
                    pool.wait_ge(a_s, used)
                for dst, src in ((kph, kxh), (kpl, kxl)):
                    pool.tensor_scalar(dst[h % 4][:, :], src[:, h // HG, :], head_rows[h % HG],
                                       -float(HD0) ** -0.5, ALU.mult, ALU.mult).then_inc(a_kp, 1)

            def normalise(g, h):
                count = held(pool, count_reg, g + 1)
                turned = None if isinstance(g, int) and g < 4 else held(pool, other_reg, g - 3)
                pool.wait_ge(init, 3)
                pool.wait_ge(a_rs, count)
                if turned is not None:
                    pool.wait_ge(a_tmm, turned)
                for t in range(QT):
                    pool.tensor_scalar(pn0[h % 4][:, t, :], p0[h % 2][:, t, :], rsum0[:, h % 4, t:t + 1], 1.0,
                                       ALU.mult, ALU.mult).then_inc(a_pn, 1)

            def attention0(a, kind, b, first, next):
                g = a * H0
                if first:
                    layer_norm(ln_l0(0, 0))
                    pool.wait_ge(b_hi, 1)
                    pool.tensor_scalar(row_top[:, :, :], row_h[:, :, :], ident[0:2, 0:1], 1.0, ALU.mult,
                                       ALU.mult).then_inc(b_top, 1)
                    key_rows(0, 0, 0)
                    key_rows(1, 1, 0)
                for s in range(H0):
                    if s + 2 < H0:
                        key_rows(g + s + 2, s + 2, a * 2 + (s + 2) // HG)
                    elif next is not None:
                        key_rows(g + s + 2, s + 2 - H0, a * 2 + 2)
                    if s >= 1:
                        normalise(g + s - 1, s - 1)
                    elif not first:
                        normalise(g - 1, H0 - 1)
                    if s == 5 and next is not None:
                        layer_norm(ln_l0(a + 1, 0))
                        if next[0] == 1:
                            pool.wait_ge(enc_ev, NT)
                            pool.wait_ge(a_vmm, a * 2 + 2)
                            pool.tensor_copy(encb[:, :, :], encT[:, :, ds(next[1] * S, S)]).then_inc(a_encb, 1)
                    if s == 5 and next is None:
                        layer_norm(ln_half(0, 0))
                if next is None:
                    normalise(g + H0 - 1, H0 - 1)

            all_l0(attention0)(pool)

            def mlp_weights_lo(m, parts):
                for i in parts:
                    raw, hi, lo = weight_part(i)
                    pool.wait_ge(m_whi, NF * m + i + 1)
                    pool.tensor_tensor(lo, raw, hi, ALU.subtract).then_inc(m_wlo, 1)

            mlp_weights_lo(0, range(NF // 2))
            layer_norm(ln_half(0, 1))
            mlp_weights_lo(0, range(NF // 2, NF))
            pool.wait_ge(enc_hi, 1)
            pool.tensor_tensor(encTl[:, :, :], encT[:, :, :], encTh[:, :, :], ALU.subtract).then_inc(enc_lo, 1)
            layer_norm(ln_half(1, 0))

            def split_lo(lo, raw, hi, s):
                pool.tensor_tensor(lo, raw, hi, ALU.subtract).then_inc(s, 1)

            def qk_lo(n, i):
                pool.wait_ge(w_qk, n * 4 + 2 * i + 1)
                split_lo(wqk_l[i][:, :, :, :], raw_qk[i][:, :, :, :], wqk_h[i][:, :, :, :], w_qk)

            def v_lo_(n):
                pool.wait_ge(w_v, n * 2 + 1)
                split_lo(wv_l[:, :, :], raw_v[:, :, :], wv_h[:, :, :], w_v)

            def v_bias_(n):
                pool.wait_ge(d_vb, n * 16 + 16)
                pool.wait_ge(v_t, PAST + n * 4)
                split_lo(v_bias[:, :], raw_vb[:, 0, :], raw_vb[:, 1, :], w_vb)

            def o_lo_(n):
                pool.wait_ge(w_o, n * 2 + 1)
                split_lo(wo_l[:, :, :], raw_o[:, :, :], wo_h[:, :, :], w_o)

            def key_bias(n, c, scores_done):
                count = held(pool, count_reg, PAST + scores_done)
                pool.wait_ge(init, 3)
                pool.wait_ge(s_mm, count)
                for dst, src in ((kh, bkh), (kl, bkl)):
                    pool.tensor_copy(dst[:, :, 2 * c:2 * c + 2, S:SP], src[:, ds(n * 2, 2)].unsqueeze(
                        2).unsqueeze(3).to_broadcast([P, 2, 2, 2])).then_inc(kb, 1)

            def norm(g, s):
                count = held(pool, count_reg, g + 1)
                turned = held(pool, other_reg, PAST + g - 1)
                pool.wait_ge(init, 3)
                pool.wait_ge(t_mm, turned)
                pool.wait_ge(s_rs, count)
                for t in range(QT):
                    pool.tensor_scalar(pn[s % 2][:, t, :], pr[s % 4][:, t, 0:S], rs[:, s % 4, t:t + 1], 1.0,
                                       ALU.mult, ALU.mult).then_inc(s_pn, 1)

            def value_lo(n, j):
                pool.wait_ge(v_hi, n * 4 + j + 1)
                pool.tensor_tensor(vl[:, 2 * j:2 * j + 2, :], vt[j % 2][:, :, :], vh[:, 2 * j:2 * j + 2, :],
                                   ALU.subtract).then_inc(v_lo, 1)

            def pair(n, first, last):
                for s in range(STEPS):
                    g = n * STEPS + s
                    if s >= 1 or not first:
                        norm(g - 1, (s - 1) % STEPS)
                    if s == 0:
                        key_bias(n, 1, g)
                    if s == 1 and not first:
                        value_lo(n, 1)
                    if s == 3:
                        value_lo(n, 2)
                    if not last:
                        if s == 2:
                            qk_lo(n + 1, 0)
                        if s == 4:
                            v_bias_(n + 1)
                            v_lo_(n + 1)
                    if s == 5:
                        o_lo_(n)
                        if not last:
                            key_bias(n + 1, 0, n * STEPS + 4)
                    if s == 6:
                        if not last:
                            qk_lo(n + 1, 1)
                        value_lo(n, 3)
                    if s == 7 and not last:
                        value_lo(n + 1, 0)
                if last:
                    norm(n * STEPS + STEPS - 1, STEPS - 1)

            with pool.Fori(0, PH) as ph:
                n0 = ph * PAIRS
                v_lo_(n0)
                v_bias_(n0)
                qk_lo(n0, 0)
                layer_norm(ln_half(ph + 1, 1))
                qk_lo(n0, 1)
                key_bias(n0, 0, n0 * STEPS)
                value_lo(n0, 0)
                value_lo(n0, 1)
                pair(n0, True, False)
                with pool.Fori(1, PAIRS - 1) as p:
                    pair(n0 + p, False, False)
                pair(n0 + (PAIRS - 1), False, True)
                layer_norm(ln_half(ph + 2, 0))
            mlp_weights_lo(1, range(NF // 2))
            layer_norm(ln_half(PH + 1, 1))
            mlp_weights_lo(1, range(NF // 2, NF))

        @block.scalar
        def _(act):
            count_reg = act.alloc_register()
            start_counts(act, s_exp)
            act.wait_ge(init, 3)
            act.activation(v0[:, :, :, HD0:HD0 + P], zeros[:, 0:1].unsqueeze(2).unsqueeze(3).to_broadcast(
                [P, QT, H0, P]), ACT.Copy).then_inc(a_zero, 1)
            act.activation(ones_r[:, :], ones[:, :], ACT.Copy).then_inc(b_ones, 1)
            act.wait_ge(d_row, 16)
            act.activation(row_h[:, :, :], row[:, :, :], ACT.Copy).then_inc(b_hi, 1)
            act.wait_ge(d_vec, 16)

            def ln_out(call, dst, banks, scale, offset, part=None):
                _, t0, n, _, at = call
                for j in range(n // 2) if part is None else (part,):
                    count = held(act, count_reg, t0 // 2 + j + 1)
                    act.wait_ge(d_vec, 16)
                    act.wait_ge(ln_mm, count)
                    for k in range(KD):
                        act.activation(dst[:, k, (at + 2 * j) * P:(at + 2 * j + 2) * P],
                                       bank[banks[j]][:, k * S:(k + 1) * S],
                                       ACT.Identity, bias=offset(k), scale=scale(k)).then_inc(ln_ev, 1)
                    if dst is hT:
                        act.wait_ge(ln_ev, t0 + 2 * j + 2)
                        tokens = slice((at + 2 * j) * P, (at + 2 * j + 2) * P)
                        act.activation(hTh[:, :, tokens], hT[:, :, tokens], ACT.Copy).then_inc(h_hi, 1)

            def queries(unit, kind):
                u, m = unit
                act.wait_ge(a_qmm, u + 1)
                act.activation(q0h[:, m, :], bank[7 - m][:, 0:S], ACT.Identity,
                               bias=col(("bq_s", "bq_c")[kind], m), scale=1.0).then_inc(a_qhi, 1)

            def keys(unit, kind):
                u, m = unit
                act.wait_ge(a_kmm, u + 1)
                act.activation(kxh[:, m, :], bank[6 + m][:, 0:S], ACT.Identity,
                               bias=col(("bk_s", "bk_c")[kind], m), scale=1.0).then_inc(a_khi, 1)

            def vals(unit):
                u, m = unit
                act.wait_ge(a_vmm, u + 1)
                for t in range(QT):
                    act.activation(v0[:, t, m * HG:(m + 1) * HG, 0:HD0], bank[7 - m][:, t * P:(t + 1) * P].rearrange(
                        "p (h d) -> p h d", h=HG), ACT.Copy).then_inc(a_vev, 1)

            def context(unit, kind):
                u, m = unit
                act.wait_ge(a_pv, u * HG + HG)
                act.activation(ct0[:, m, :], bank[4 + m][:, 0:S], ACT.Identity,
                               bias=col(("bv_s", "bv_c")[kind], m), scale=1.0).then_inc(a_cev, 1)

            def attention0(a, kind, b, first, next):
                g = a * H0

                def normed(a, kind):
                    names = (("ln1_s", "ln1_b"), ("ln2_s", "ln2_b"))[kind]
                    ln_out(ln_l0(a, 0), hb, (6,), lambda k: col(names[0], k), lambda k: col(names[1], k))

                def pt(g, h):
                    act.wait_ge(a_tmm, g + 1)
                    if not (isinstance(g, int) and g < 2):
                        act.wait_ge(a_pv, g - 1)
                    act.activation(pt0[h % 2][:, :, :], bank[2 + h % 2][:, :], ACT.Copy).then_inc(a_tev, 1)

                if first:
                    normed(0, 0)
                    queries((0, 0), 0)
                    keys((0, 0), 0)
                    vals((0, 0))
                for s in range(H0):
                    if s >= TURN_LAG or not first:
                        pt(g + s - TURN_LAG, (s - TURN_LAG) % H0)
                    if s == 4 and not first:
                        context((a * 2 - 1, 1), before(a, kind, b)[0])
                    act.wait_ge(a_u, (g + s) * 2 + 2)
                    if not (isinstance(g, int) and g + s < 2):
                        act.wait_ge(a_pn, (g + s) * 2 - 2)
                    for t in range(QT):
                        act.activation(p0[s % 2][:, t, :], um[s % 2][:, t, :], ACT.Exp, bias=umin[:, s % 2, t:t + 1],
                                       scale=-1.0, accum_out=psum0[:, s % 4, t:t + 1]).then_inc(a_p, 1)
                    if first and s < NT // 2:
                        act.wait_ge(enc_mm, s + 1)
                        for k in range(KD):
                            act.activation(encT[:, k, 2 * s * P:(2 * s + 2) * P], bank[5][:, k * S:(k + 1) * S],
                                           ACT.Copy).then_inc(enc_ev, 1)
                    if s == 1:
                        queries((a * 2 + 1, 1), kind)
                    if s == 2:
                        keys((a * 2 + 1, 1), kind)
                    if s == 4:
                        vals((a * 2 + 1, 1))
                    if s == 7 and next is not None:
                        normed(a + 1, next[0])
                    if s in (10, 11) and next is None:
                        ln_out(ln_half(0, 0), hT, (6, 7), lambda k: col("ln3_s", k), lambda k: col("ln3_b", k), s - 10)
                    if s == 9 and next is not None:
                        queries((a * 2 + 2, 0), next[0])
                    if s == 10 and next is not None:
                        keys((a * 2 + 2, 0), next[0])
                    if s == 12:
                        context((a * 2, 0), kind)
                        if next is not None:
                            vals((a * 2 + 2, 0))
                if next is None:
                    for s in range(TURN_LAG):
                        pt(g + H0 + s - TURN_LAG, H0 + s - TURN_LAG)
                    context((a * 2 + 1, 1), kind)

            all_l0(attention0)(act)

            def mlp(call, m, func, scale, offset, bias):
                for i in range(NF):
                    if i == NF // 2 and m == 1:
                        ln_out(ln_half(call, 0), hT, (6, 7), scale, offset)
                    raw, hi, _ = weight_part(i)
                    act.activation(hi, raw, ACT.Copy).then_inc(m_whi, 1)
                for c in range(TOK // CH):
                    if c == 1:
                        ln_out(ln_half(call, c), hT, (6, 7), scale, offset)
                    for f in range(NF):
                        n = (2 * m + c) * NF + f
                        act.wait_ge(m_up, n + 1)
                        if n >= 2:
                            act.wait_ge(m_glo, n - 1)
                        act.activation(gelu[f % 2][:, :], bank[f % 4][:, :], func, bias=bias(f),
                                       scale=1.0).then_inc(m_gelu, 1)
                        act.wait_ge(m_gelu, n + 1)
                        act.activation(gelu_h[:, f, :], gelu[f % 2][:, :], ACT.Copy).then_inc(m_ghi, 1)

            act.wait_ge(d_up, 32)
            act.wait_ge(a_s, 2 * B * H0)
            act.wait_ge(a_pn, 2 * B * H0 * QT)
            act.wait_ge(a_pv, 2 * B * H0)
            mlp(0, 0, ACT.Gelu_apprx_tanh, lambda k: col("ln3_s", k), lambda k: col("ln3_b", k),
                lambda f: col("b1", f))

            def proj_hi(n, i, turn=None, bk=6):
                grp, head = n * 8 + (i if turn is None else turn), n * 2 + group_head(i)
                hh, c = group_head(i), i // 4
                count = held(act, count_reg, PAST + grp + 1)
                act.wait_ge(d_vec, 16)
                act.wait_ge(g_mm, count)
                if group_is_key(i):
                    act.activation(kh[:, hh, 2 * c:2 * c + 2, 0:S], bank[bk][:, :].rearrange(
                        "p (b s) -> p b s", b=2), ACT.Identity, bias=col("bk", head), scale=1.0).then_inc(g_hi, 1)
                else:
                    act.activation(qh[:, hh, c * CH:(c + 1) * CH], bank[bk][:, :], ACT.Identity,
                                   bias=col("bq", head), scale=1.0).then_inc(g_hi, 1)

            def split_hi(hi, raw, loaded, count, s):
                act.wait_ge(loaded, count)
                act.activation(hi, raw, ACT.Copy).then_inc(s, 1)

            def v_weights(n):
                act.wait_ge(v_mm, PAST + n * 4)
                split_hi(wv_h[:, :, :], raw_v[:, :, :], d_v, n * 16 + 16, w_v)

            def o_weights(n):
                act.wait_ge(o_mm, PAST + n * 4)
                split_hi(wo_h[:, :, :], raw_o[:, :, :], d_o, n * 16 + 16, w_o)

            def qk_weights(n, i, groups_done):
                act.wait_ge(g_mm, PAST + groups_done)
                split_hi(wqk_h[i][:, :, :, :], raw_qk[i][:, :, :, :], d_qk[i], n * 16 + 16, w_qk)

            def value_hi(n, j):
                act.wait_ge(v_t, PAST + n * 4 + j + 1)
                act.activation(vh[:, 2 * j:2 * j + 2, :], vt[j % 2][:, :, :], ACT.Copy).then_inc(v_hi, 1)

            def pt_hi(g, s):
                act.wait_ge(t_mm, PAST + g + 1)
                act.activation(pth[s % 2][:, :, :], bank[4][:, :], ACT.Copy).then_inc(t_hi, 1)

            def ctx_hi(g, s, n):
                hh, b = s % 2, s // 2
                count = held(act, count_reg, PAST + g + 1)
                act.wait_ge(d_vec, 16)
                act.wait_ge(pv_mm, count)
                act.activation(ch[:, hh, b * S:(b + 1) * S], bank[5][:, 0:S], ACT.Identity,
                               bias=col("bias_v", n * 2 + hh), scale=1.0).then_inc(c_hi, 1)

            def exps(g, s):
                act.wait_ge(s_nm, g + 1)
                for t in range(QT):
                    act.activation(pr[s % 4][:, t, :], bank[2 * (s % 2) + t][:, 0:S + 1], ACT.Exp,
                                   bias=nm[:, s % 4, t:t + 1], scale=float(HD1) ** -0.5,
                                   accum_out=sums[:, s % 4, t:t + 1]).then_inc(s_exp, 1)

            def normed_half(ph, half):
                call = ln_half(ph + 1, half)
                ln_out(call, hT, ((2, 3), (7, 5))[half], lambda k: col("lnx_s", ph * 2 + k),
                       lambda k: col("lnx_b", ph * 2 + k))

            def pair(n, first, last):
                for s in range(STEPS):
                    g = n * STEPS + s
                    if 1 <= s <= 4:
                        proj_hi(n, s + 3)
                    elif s >= 5 and not last:
                        proj_hi(n + 1, s - 5)
                    elif s == 0 and not first:
                        proj_hi(n, 3)
                    if s >= 4:
                        ctx_hi(g - 4, s - 4, n)
                    elif not first:
                        ctx_hi(g - 4, s + 4, n - 1)
                    if s >= 2 or not first:
                        pt_hi(g - 2, s % 2)
                    exps(g, s)
                    if s == 1 and not last:
                        qk_weights(n + 1, 0, n * 8 + 6)
                    if s == 3 and not last:
                        v_weights(n + 1)
                    if s == 4:
                        o_weights(n)
                    if s == 5 and not last:
                        qk_weights(n + 1, 1, n * 8 + 8)
                    if s == 0 and not first:
                        value_hi(n, 1)
                    if s == 2:
                        value_hi(n, 2)
                    if s == 4:
                        value_hi(n, 3)
                    if s == 6 and not last:
                        value_hi(n + 1, 0)

            with act.Fori(0, PH) as ph:
                n0 = ph * PAIRS
                v_weights(n0)
                qk_weights(n0, 0, n0 * 8)
                act.wait_ge(w_qk, n0 * 4 + 2)
                qk_weights(n0, 1, n0 * 8)
                normed_half(ph, 0)
                value_hi(n0, 0)
                proj_hi(n0, 0)
                value_hi(n0, 1)
                proj_hi(n0, 2, 1, 5)
                proj_hi(n0, 1, 2, 4)
                proj_hi(n0, 3)
                normed_half(ph, 1)
                pair(n0, True, False)
                with act.Fori(1, PAIRS - 1) as p:
                    pair(n0 + p, False, False)
                n = n0 + (PAIRS - 1)
                pair(n, False, True)
                g = n * STEPS
                ctx_hi(g + 4, 4, n)
                pt_hi(g + 6, 0)
                ctx_hi(g + 5, 5, n)
                pt_hi(g + 7, 1)
                ctx_hi(g + 6, 6, n)
                ctx_hi(g + 7, 7, n)
            act.wait_ge(d_up2, 32)
            act.wait_ge(s_mm, PAST + PH * PAIRS * STEPS)
            mlp(PH + 1, 1, ACT.Gelu, lambda k: col("lnx_s", PH * 2 + k), lambda k: col("lnx_b", PH * 2 + k),
                lambda f: col("b_fc1", f))

        @block.vector
        def _(dve):
            count_reg = dve.alloc_register()
            other_reg = dve.alloc_register()
            start_counts(dve, v_t, c_lo, t_lo, g_lo, o_x)
            def ln_stats(call):
                c, t0, n, x0, at = call
                for t in range(n):
                    dve.bn_stats(stats[:, at + t, :], x_acc[:, ds(x0 + t, 1), :].rearrange(
                        "p a d -> p (a d)")).then_inc(ln_st, 1)
                for t in range(n):
                    count = held(dve, count_reg, t0 + t + 1)
                    dve.wait_ge(d_x0, 16)
                    dve.wait_ge(ln_st, count)
                    dve.bn_aggr(mean_var[:, at + t, :], stats[:, at + t, :]).then_inc(ln_mv, 1)

            def ln_rows(call):
                c, t0, n, x0, at = call
                dve.wait_ge(ln_rstd, c + 1)
                if not (isinstance(c, int) and c == 0):
                    dve.wait_ge(ln_mm, t0 // 2 if n == QT or (isinstance(c, int) and c == 2 * B) else
                                (t0 - HALF) // 2)
                for t in range(n):
                    dve.tensor_scalar(xn[:, at + t, :], x_acc[:, ds(x0 + t, 1), :].rearrange("p a d -> p (a d)"),
                                      mean_var[:, at + t, 0:1], rstd[:, at + t:at + t + 1], ALU.subtract,
                                      ALU.mult).then_inc(ln_xn, 1)

            def hT_lo(call, half):
                for j in range(2):
                    dve.wait_ge(h_hi, 4 * call + 2 * half + j + 1)
                    at = slice((2 * half + j) * S, (2 * half + j + 1) * S)
                    dve.tensor_tensor(hTl[:, :, at], hT[:, :, at], hTh[:, :, at], ALU.subtract).then_inc(h_lo, 1)

            def layer_norm(call):
                ln_stats(call)
                ln_rows(call)

            def queries(unit, kind):
                u, m = unit
                dve.wait_ge(a_qhi, u + 1)
                dve.scalar_tensor_tensor(out=q0l[:, m, :], in0=bank[7 - m][:, 0:S], scalar=col(("bq_s", "bq_c")[kind], m),
                                         in1=q0h[:, m, :], op0=ALU.add, op1=ALU.subtract).then_inc(a_qev, 1)

            def keys(unit, kind):
                u, m = unit
                dve.wait_ge(a_khi, u + 1)
                dve.scalar_tensor_tensor(out=kxl[:, m, :], in0=bank[6 + m][:, 0:S], scalar=col(("bk_s", "bk_c")[kind], m),
                                         in1=kxh[:, m, :], op0=ALU.add, op1=ALU.subtract).then_inc(a_kev, 1)

            def take_mask(i, a):
                if i > 0:
                    loaded = held(dve, count_reg, i * 16 + 16)
                    used = held(dve, other_reg, a * (2 * H0))
                    dve.wait_ge(d_x, 16)
                    dve.wait_ge(a_u, used)
                    dve.wait_ge(d_m, loaded)
                else:
                    dve.wait_ge(d_m, 16)
                dve.tensor_copy(msk[:, :, :], msk_next[:, :, :]).then_inc(a_mask, 1)
                dve.tensor_scalar(pen[:, :, :], msk_next[:, :, :], -MASKED, MASKED, ALU.mult,
                                  ALU.add).then_inc(a_mask, 1)
                dve.wait_ge(a_mask, i * 2 + 2)

            def add_out0(a, b):
                dve.wait_ge(a_omm, a + 1)
                xs = x_acc[:, ds(b * QT, QT), :]
                dve.tensor_tensor(xs, xs, bank[7][:, :].rearrange("p (t d) -> p t d", t=QT), ALU.add).then_inc(a_x, 1)

            def row_sums(g, h):
                dve.wait_ge(a_p, g * 2 + 2)
                dve.reciprocal(rsum0[:, h % 4, :], psum0[:, h % 4, :]).then_inc(a_rs, 1)

            def attention0(a, kind, b, first, next):
                if first:
                    layer_norm(ln_l0(0, 0))
                    dve.wait_ge(b_hi, 1)
                    dve.tensor_tensor(row[:, :, :], row[:, :, :], row_h[:, :, :], ALU.subtract).then_inc(b_lo, 1)
                    dve.wait_ge(b_lo, 1)
                    dve.wait_ge(b_top, 1)
                    dve.scalar_tensor_tensor(out=row_hi_lo[:, :, :], in0=row[:, :, :], scalar=ident[0:2, 1:2],
                                             in1=row_top[:, :, :], op0=ALU.mult, op1=ALU.add).then_inc(b_rows, 1)
                    queries((0, 0), 0)
                    keys((0, 0), 0)
                    take_mask(0, 0)
                elif kind == 1:
                    take_mask(b + 1, a)
                for s in range(H0):
                    g = a * H0 + s
                    if s == 2:
                        queries((a * 2 + 1, 1), kind)
                    if s == 3:
                        keys((a * 2 + 1, 1), kind)
                    if s == 10 and next is not None:
                        queries((a * 2 + 2, 0), next[0])
                    if s == 11 and next is not None:
                        keys((a * 2 + 2, 0), next[0])
                    dve.wait_ge(a_s, g + 1)
                    dve.tensor_tensor(tm[s % 2][:, :, :].rearrange("p t k -> p (t k)"), bank[s % 2][:, :],
                                      msk[:, :, :].rearrange("p t k -> p (t k)"), ALU.mult).then_inc(a_t, 1)
                    count = held(dve, count_reg, g + 1)
                    used = None if isinstance(g, int) and g < 2 else held(dve, other_reg, g * 2 - 2)
                    dve.wait_ge(a_mask, 2)
                    if used is not None:
                        dve.wait_ge(a_p, used)
                    dve.wait_ge(a_t, count)
                    for t in range(QT):
                        dve.tensor_tensor_reduce(um[s % 2][:, t, :], tm[s % 2][:, t, :], pen[:, t, :], 1.0,
                                                 3.0e38, ALU.add, ALU.min, umin[:, s % 2, t:t + 1]).then_inc(a_u, 1)
                    if s >= 1 or not first:
                        row_sums(g - 1, (s - 1) % H0)
                    if s == 4 and first:
                        dve.wait_ge(d_x, 16)
                    if s == 4 and next is not None:
                        if next[0] == 1:
                            count = held(dve, count_reg, a - 2)
                            dve.wait_ge(d_x, 16)
                            dve.wait_ge(a_x, count)
                        ln_stats(ln_l0(a + 1, next[1]))
                    if s == 6 and next is not None:
                        ln_rows(ln_l0(a + 1, next[1]))
                    if s == 4 and next is None:
                        dve.wait_ge(a_x, a - 1)
                        ln_stats(ln_half(0, 0))
                    if s == 6 and next is None:
                        ln_rows(ln_half(0, 0))
                    if s == 13 and next is None:
                        hT_lo(0, 0)
                    if s == 7 and not first:
                        add_out0(a - 1, before(a, kind, b)[1])
                if next is None:
                    row_sums(a * H0 + H0 - 1, H0 - 1)
                    add_out0(a, b)
                    dve.wait_ge(a_x, a + 1)

            dve.wait_ge(d_x0, 16)
            dve.wait_ge(d_vec, 16)
            dve.wait_ge(d_const, 16)
            all_l0(attention0)(dve)

            def mlp(call, m):
                ln_stats(ln_half(call, 1))
                if m == 0:
                    dve.tensor_copy(encTh[:, :, :], encT[:, :, :]).then_inc(enc_hi, 1)
                if m == 1:
                    hT_lo(call, 0)
                for c in range(TOK // CH):
                    for f in range(NF):
                        n = (2 * m + c) * NF + f
                        if c == 0 and f == 3:
                            ln_rows(ln_half(call, 1))
                        if c == 1 and f == 5 and m == 0:
                            ln_rows(ln_half(1, 0))
                        dve.wait_ge(m_ghi, n + 1)
                        dve.tensor_tensor(gelu_l[:, f, :], gelu[f % 2][:, :], gelu_h[:, f, :],
                                          ALU.subtract).then_inc(m_glo, 1)
                    if c == 0:
                        hT_lo(call, 1)
                    for j in range(2):
                        g = 2 * (2 * m + c) + j
                        dve.wait_ge(m_down, g + 1)
                        xs = x_acc[:, 4 * c + 2 * j:4 * c + 2 * j + 2, :]
                        dve.tensor_tensor(xs, xs, bank[4 + j][:, :].rearrange("p (t d) -> p t d", t=2),
                                          ALU.add).then_inc(m_x, 1)
                    if c == 0 and m == 0:
                        dve.wait_ge(m_x, 2)
                        ln_stats(ln_half(1, 0))

            mlp(0, 0)
            dve.wait_ge(m_x, NT // 2)

            def proj_lo(n, i, turn=None, bk=6):
                head, hh, c = n * 2 + group_head(i), group_head(i), i // 4
                dve.wait_ge(g_hi, n * 8 + (i if turn is None else turn) + 1)
                if group_is_key(i):
                    dve.scalar_tensor_tensor(out=kl[:, hh, 2 * c:2 * c + 2, 0:S],
                                             in0=bank[bk][:, :].rearrange("p (b s) -> p b s", b=2),
                                             scalar=col("bk", head), in1=kh[:, hh, 2 * c:2 * c + 2, 0:S],
                                             op0=ALU.add, op1=ALU.subtract).then_inc(g_lo, 1)
                else:
                    dve.scalar_tensor_tensor(out=ql[:, hh, c * CH:(c + 1) * CH], in0=bank[bk][:, :],
                                             scalar=col("bq", head), in1=qh[:, hh, c * CH:(c + 1) * CH],
                                             op0=ALU.add, op1=ALU.subtract).then_inc(g_lo, 1)

            def pt_lo(g, s):
                dve.wait_ge(t_hi, g + 1)
                dve.tensor_tensor(ptl[s % 2][:, :, :].rearrange("p t k -> p (t k)"), bank[4][:, :],
                                  pth[s % 2][:, :, :].rearrange("p t k -> p (t k)"), ALU.subtract).then_inc(t_lo, 1)

            def ctx_lo(g, s, n):
                hh, b = s % 2, s // 2
                dve.wait_ge(c_hi, g + 1)
                dve.scalar_tensor_tensor(out=cl[:, hh, b * S:(b + 1) * S], in0=bank[5][:, 0:S],
                                         scalar=col("bias_v", n * 2 + hh), in1=ch[:, hh, b * S:(b + 1) * S],
                                         op0=ALU.add, op1=ALU.subtract).then_inc(c_lo, 1)

            def row_max(g, s):
                dve.wait_ge(s_mm, PAST + g + 1)
                for t in range(QT):
                    dve.tensor_reduce(mx[:, s % 4, t:t + 1], bank[2 * (s % 2) + t][:, 0:S + 1], AX.X,
                                      ALU.max).then_inc(s_max, 1)
                dve.wait_ge(s_max, g * 2 + 2)
                dve.tensor_scalar(nm[:, s % 4, :], mx[:, s % 4, :], -float(HD1) ** -0.5, None,
                                  ALU.mult).then_inc(s_nm, 1)

            def row_recip(g, s):
                dve.wait_ge(s_exp, PAST + g * 2 + 2)
                dve.reciprocal(rs[:, s % 4, :], sums[:, s % 4, :]).then_inc(s_rs, 1)

            def values(n, j):
                dve.wait_ge(w_vb, n + 1)
                dve.wait_ge(v_lo, PAST + n * 4 + j - 1)
                dve.wait_ge(v_mm, PAST + n * 4 + j + 1)
                dve.tensor_tensor(vt[j % 2][:, :, :], bank[7][:, :].rearrange("p (t m) -> p t m", t=2),
                                  v_bias[:, :].unsqueeze(1).to_broadcast([P, 2, 2 * HD1]), ALU.add).then_inc(v_t, 1)

            def add_out(n, j):
                dve.wait_ge(o_mm, PAST + n * 4 + j + 1)
                xs = x_acc[:, 2 * j:2 * j + 2, :]
                dve.tensor_tensor(xs, xs, bank[7][:, :].rearrange("p (t d) -> p t d", t=2),
                                  ALU.add).then_inc(o_x, 1)

            def pair(n, first, last, ph=None):
                for s in range(STEPS):
                    g = n * STEPS + s
                    if s >= 1 or not first:
                        row_recip(g - 1, (s - 1) % 4)
                    if 1 <= s <= 4:
                        proj_lo(n, s + 3)
                    elif s >= 5 and not last:
                        proj_lo(n + 1, s - 5)
                    elif s == 0 and not first:
                        proj_lo(n, 3)
                    row_max(g, s)
                    if s == 0 and first:
                        hT_lo(ph + 1, 1)
                    if s >= 4:
                        ctx_lo(g - 4, s - 4, n)
                    elif not first:
                        ctx_lo(g - 4, s + 4, n - 1)
                    if s >= 2 or not first:
                        pt_lo(g - 2, s % 2)
                    if s in (1, 3):
                        values(n, 2 + s // 2)
                    elif s in (5, 7) and not last:
                        values(n + 1, s // 2 - 2)
                    elif s in (0, 2, 4) and not first:
                        add_out(n - 1, 1 + s // 2)
                    elif s == 6:
                        add_out(n, 0)

            with dve.Fori(0, PH) as ph:
                n0 = ph * PAIRS
                ln_stats(ln_half(ph + 1, 1))
                values(n0, 0)
                proj_lo(n0, 0)
                hT_lo(ph + 1, 0)
                ln_rows(ln_half(ph + 1, 1))
                values(n0, 1)
                proj_lo(n0, 2, 1, 5)
                proj_lo(n0, 1, 2, 4)
                proj_lo(n0, 3)
                pair(n0, True, False, ph)
                with dve.Fori(1, PAIRS - 1) as p:
                    pair(n0 + p, False, False)
                n = n0 + (PAIRS - 1)
                pair(n, False, True)
                g = n * STEPS
                row_recip(g + 7, 3)
                ctx_lo(g + 4, 4, n)
                pt_lo(g + 6, 0)
                ctx_lo(g + 5, 5, n)
                pt_lo(g + 7, 1)
                add_out(n, 1)
                ctx_lo(g + 6, 6, n)
                whole = held(dve, count_reg, PAST + n * 4 + 2)
                dve.wait_ge(d_x, 16)
                dve.wait_ge(o_x, whole)
                ln_stats(ln_half(ph + 2, 0))
                add_out(n, 2)
                ctx_lo(g + 7, 7, n)
                ln_rows(ln_half(ph + 2, 0))
                add_out(n, 3)
                dve.wait_ge(o_x, PAST + (n0 + PAIRS) * 4)
            mlp(PH + 1, 1)

        @block.tensor
        def _(pe):
            count_reg = pe.alloc_register()
            other_reg = pe.alloc_register()
            start_counts(pe, s_mm, g_mm, v_mm, o_mm, pv_mm, t_mm)
            pe.wait_ge(d_const, 16)

            def mm3(dst, lh, ll, rh, rl, start, stop):
                pe.matmul(dst, lh, rh, start=start, stop=False)
                pe.matmul(dst, ll, rh, start=False, stop=False)
                return pe.matmul(dst, lh, rl, start=False, stop=stop)

            def transposes(src, j, bk, signal):
                for k in range(KD):
                    for t in range(2):
                        last = pe.transpose(bank[bk][:, k * S + t * P:k * S + (t + 1) * P],
                                            src[:, 2 * j + t, k * P:(k + 1) * P], ident)
                last.then_inc(signal, 1)


            def layer_norm(call, banks):
                _, t0, n, _, at = call
                for j in range(n // 2):
                    pe.wait_ge(ln_xn, t0 + 2 * j + 2)
                    transposes(xn, at // 2 + j, banks[j], ln_mm)

            def mm_bias(dst, r, first=True):
                pe.matmul(dst, ones_r[:, :], row_hi_lo[:, ds(r, 1), :].rearrange("p a d -> p (a d)"),
                          start=first, stop=False)

            def source(kind):
                return ((w_qkv, D, 2 * D, hb), (w_kv, 0, D, encb))[kind]

            def queries(unit, kind):
                u, m = unit
                wq = (w_qkv, w_q)[kind]
                for k in range(KD):
                    last = pe.matmul(bank[7 - m][:, 0:S], wq[:, k, m * P:(m + 1) * P], hb[:, k, :],
                                     start=(k == 0), stop=(k == KD - 1))
                last.then_inc(a_qmm, 1)

            def keys(unit, kind):
                u, m = unit
                w, koff, _, src = source(kind)
                for k in range(KD):
                    last = pe.matmul(bank[6 + m][:, 0:S], w[:, k, koff + m * P:koff + (m + 1) * P], src[:, k, :],
                                     start=(k == 0), stop=(k == KD - 1))
                last.then_inc(a_kmm, 1)

            def vals(unit, kind):
                u, m = unit
                w, _, voff, src = source(kind)
                for t in range(QT):
                    for k in range(KD):
                        last = pe.matmul(bank[7 - m][:, t * P:(t + 1) * P], src[:, k, t * P:(t + 1) * P],
                                         w[:, k, voff + m * P:voff + (m + 1) * P], start=(k == 0), stop=(k == KD - 1))
                last.then_inc(a_vmm, 1)

            def scores0(a, s):
                g = a * H0 + s
                if s % HG == 0:
                    pe.wait_ge(a_qev, a * 2 + s // HG + 1)
                pe.wait_ge(a_kp, g * 2 + 2)
                if not (isinstance(g, int) and g < 2):
                    pe.wait_ge(a_t, g - 1)
                for t in range(QT):
                    last = mm3(bank[s % 2][:, t * S:(t + 1) * S], q0h[:, s // HG, t * P:(t + 1) * P],
                               q0l[:, s // HG, t * P:(t + 1) * P], kph[s % 4][:, :], kpl[s % 4][:, :], True, True)
                last.then_inc(a_s, 1)

            def turn0(g, h):
                pe.wait_ge(a_pn, g * 2 + 2)
                if not (isinstance(g, int) and g < 2):
                    pe.wait_ge(a_tev, g - 1)
                for kt in range(QT):
                    for t in range(QT):
                        last = pe.transpose(bank[2 + h % 2][:, kt * S + t * P:kt * S + (t + 1) * P],
                                            pn0[h % 4][:, t, kt * P:(kt + 1) * P], ident)
                last.then_inc(a_tmm, 1)

            def pv0(a, h):
                g, m, j = a * H0 + h, h // HG, h % HG
                if j == 0:
                    pe.wait_ge(a_vev, a * 4 + 2 * m + 2)
                    if not (isinstance(a, int) and a == 0):
                        pe.wait_ge(a_cev, a * 2 + m - 1)
                pe.wait_ge(a_tev, g + 1)
                at = h * (HD0 + P) - j * HD0
                for kt in range(QT):
                    last = pe.matmul(bank[4 + m][:, 0:S],
                                     v0[:, kt, :, :].rearrange("p h d -> p (h d)")[:, at:at + P],
                                     pt0[h % 2][:, kt, :], start=(j == 0 and kt == 0),
                                     stop=(j == HG - 1 and kt == QT - 1))
                last.then_inc(a_pv, 1)

            def out0(a, kind, t):
                if t == 0:
                    pe.wait_ge(a_cev, a * 2 + 2)
                    if not (isinstance(a, int) and a == 0):
                        pe.wait_ge(a_x, a)
                mm_bias(bank[7][:, t * D:(t + 1) * D], kind)
                for k in range(KD):
                    last = pe.matmul(bank[7][:, t * D:(t + 1) * D], ct0[:, k, t * P:(t + 1) * P],
                                     (w_ao, w_co)[kind][:, k, :], start=False, stop=(k == KD - 1))
                if t == QT - 1:
                    last.then_inc(a_omm, 1)

            def attention0(a, kind, b, first, next):
                if first:
                    layer_norm(ln_l0(0, 0), (6,))
                    pe.wait_ge(ln_ev, 2)
                    pe.wait_ge(d_wqkv, 16)
                    queries((0, 0), 0)
                    keys((0, 0), 0)
                    pe.wait_ge(a_qev, 1)
                    vals((0, 0), 0)
                for s in range(H0):
                    if first and s == PV_LAG:
                        pe.wait_ge(d_w0, 4 * 16)
                        pe.wait_ge(b_ones, 1)
                        pe.wait_ge(b_rows, 1)
                    scores0(a, s)
                    if s >= TURN_LAG:
                        turn0(a * H0 + s - TURN_LAG, s - TURN_LAG)
                    elif not first:
                        turn0(a * H0 + s - TURN_LAG, s - TURN_LAG + H0)
                    if s >= PV_LAG:
                        pv0(a, s - PV_LAG)
                    elif not first:
                        pv0(a - 1, s - PV_LAG + H0)
                    if first and s < NT // 2:
                        if s == 0:
                            pe.wait_ge(d_enc, 16)
                        else:
                            pe.wait_ge(enc_ev, 2 * s)
                        transposes(enc_tok, s, 5, enc_mm)
                    if s == 1:
                        queries((a * 2 + 1, 1), kind)
                    if s == 2:
                        pe.wait_ge(a_vev, a * 4 + 2)
                        keys((a * 2 + 1, 1), kind)
                    if s == 3:
                        pe.wait_ge(a_qev, a * 2 + 2)
                        vals((a * 2 + 1, 1), kind)
                    if s == 5:
                        pe.wait_ge(a_kev, a * 2 + 2)
                    if s in (5, 6) and not first:
                        out0(a - 1, before(a, kind, b)[0], s - 5)
                    if s == 9 and next is None:
                        pe.wait_ge(a_vev, a * 4 + 4)
                        pe.wait_ge(a_x, a)
                        layer_norm(ln_half(0, 0), (6, 7))
                    if next is not None:
                        if s == 7:
                            pe.wait_ge(a_vev, a * 4 + 4)
                            layer_norm(ln_l0(a + 1, 0), (6,))
                        if s == 9:
                            pe.wait_ge(ln_ev, a * 2 + 4)
                            if not first:
                                pe.wait_ge(a_x, a)
                            queries((a * 2 + 2, 0), next[0])
                        if s == 10:
                            if next[0] == 1:
                                pe.wait_ge(a_encb, a - (B - 2))
                            keys((a * 2 + 2, 0), next[0])
                        if s == 12:
                            pe.wait_ge(a_qev, a * 2 + 3)
                            vals((a * 2 + 2, 0), next[0])
                if next is None:
                    for s in range(H0, H0 + PV_LAG):
                        if s - TURN_LAG < H0:
                            turn0(a * H0 + s - TURN_LAG, s - TURN_LAG)
                        pv0(a, s - PV_LAG)
                    pe.wait_ge(ln_ev, ln_half(0, 0)[1] + HALF)
                    for t in range(QT):
                        out0(a, kind, t)

            pe.wait_ge(init, 3)
            pe.wait_ge(a_zero, 1)
            all_l0(attention0)(pe)

            def mlp(call, m, bias_row):
                if m == 1:
                    layer_norm(ln_half(call, 0), (6, 7))
                for c in range(TOK // CH):
                    pe.wait_ge(h_lo, 4 * call + 2 * c + 2)
                    for f in range(NF):
                        n = (2 * m + c) * NF + f
                        if c > 0 or f >= 4:
                            pe.wait_ge(m_gelu, n - 3)
                        if c == 0 and f % 2 == 0:
                            pe.wait_ge(m_wlo, NF * m + f // 2 + 1)
                        at = slice(f * P, (f + 1) * P)
                        tokens = slice(c * CH, (c + 1) * CH)
                        for k in range(KD):
                            last = mm3(bank[f % 4][:, :], w_up_h[:, k, at], w_up_l[:, k, at],
                                       hTh[:, k, tokens], hTl[:, k, tokens], k == 0, k == KD - 1)
                        last.then_inc(m_up, 1)
                    if c == 0:
                        layer_norm(ln_half(call, 1), (6, 7))
                        pe.wait_ge(m_wlo, NF * m + NF)
                    for j in range(2):
                        if c > 0:
                            pe.wait_ge(m_x, 2 * (2 * m + c) + j - 1)
                        for t in range(2):
                            dst = bank[4 + j][:, t * D:(t + 1) * D]
                            at = slice((2 * j + t) * P, (2 * j + t + 1) * P)
                            mm_bias(dst, bias_row)
                            for f in range(NF):
                                if j == 0 and t == 0:
                                    pe.wait_ge(m_glo, (2 * m + c) * NF + f + 1)
                                last = mm3(dst, gelu_h[:, f, at], gelu_l[:, f, at], w_down_h[:, f, :],
                                           w_down_l[:, f, :], False, f == NF - 1)
                        last.then_inc(m_down, 1)

            pe.wait_ge(a_x, 2 * B)
            mlp(0, 0, 2)

            def proj(n, i, bk=6):
                hh, c, w = group_head(i), i // 4, int(group_is_key(i))
                src_h, src_l = ((hTh, hTl), (encTh, encTl))[w]
                for k in range(KD):
                    last = mm3(bank[bk][:, :], wqk_h[hh][:, w, k, :], wqk_l[hh][:, w, k, :],
                               src_h[:, k, c * CH:(c + 1) * CH], src_l[:, k, c * CH:(c + 1) * CH],
                               k == 0, k == KD - 1)
                last.then_inc(g_mm, 1)

            def scores(g, s):
                hh, b = s % 2, s // 2
                pe.wait_ge(s_exp, PAST + g * 2 - 2)
                for t in range(QT):
                    at = b * S + t * P
                    last = mm3(bank[2 * (s % 2) + t][:, 0:SP], qh[:, hh, at:at + P], ql[:, hh, at:at + P],
                               kh[:, hh, b, :], kl[:, hh, b, :], True, True)
                last.then_inc(s_mm, 1)

            def turn(g, s):
                pe.wait_ge(t_lo, PAST + g)
                pe.wait_ge(s_pn, g * 2 + 2)
                for kt in range(QT):
                    for t in range(QT):
                        last = pe.transpose(bank[4][:, kt * S + t * P:kt * S + (t + 1) * P],
                                            pn[s % 2][:, t, kt * P:(kt + 1) * P], ident)
                last.then_inc(t_mm, 1)

            def pv(g, s, n):
                hh, b = s % 2, s // 2
                pe.wait_ge(t_lo, PAST + g + 1)
                if hh == 0:
                    pe.wait_ge(v_lo, PAST + n * 4 + b + 1)
                pe.wait_ge(c_lo, PAST + g)
                for kt in range(QT):
                    last = mm3(bank[5][:, 0:S], vh[:, 2 * b + kt, hh * P:(hh + 1) * P],
                               vl[:, 2 * b + kt, hh * P:(hh + 1) * P], pth[s % 2][:, kt, :], ptl[s % 2][:, kt, :],
                               kt == 0, kt == QT - 1)
                last.then_inc(pv_mm, 1)

            def values(n, j, free, count):
                pe.wait_ge(free, PAST + count)
                for t in range(2):
                    at = (2 * j + t) * P
                    for k in range(KD):
                        last = mm3(bank[7][:, t * S:(t + 1) * S], encTh[:, k, at:at + P],
                                   encTl[:, k, at:at + P], wv_h[:, k, :], wv_l[:, k, :], k == 0, k == KD - 1)
                last.then_inc(v_mm, 1)

            def attn_out(n, j, free, count, bias_row=None):
                context = held(pe, count_reg, PAST + n * STEPS + 2 * j + 2)
                out = held(pe, other_reg, PAST + count)
                pe.wait_ge(d_row, 16)
                pe.wait_ge(free, out)
                pe.wait_ge(c_lo, context)
                for t in range(2):
                    at = (2 * j + t) * P
                    dst = bank[7][:, t * D:(t + 1) * D]
                    if bias_row is not None:
                        mm_bias(dst, bias_row)
                    for hh in range(2):
                        last = mm3(dst, ch[:, hh, at:at + P], cl[:, hh, at:at + P], wo_h[:, hh, :],
                                   wo_l[:, hh, :], bias_row is None and hh == 0, hh == 1)
                last.then_inc(o_mm, 1)

            def pair(n, first, last, bias_row=None, halves_split=None):
                for s in range(STEPS):
                    g = n * STEPS + s
                    if s % 4 == 0:
                        pe.wait_ge(kb, n * 4 + s // 2 + 2)
                    if s % 4 <= 1:
                        whole = 4 if first and s == 0 else s + 2 + s % 2
                        pe.wait_ge(g_lo, PAST + n * 8 + whole)
                    scores(g, s)
                    if s >= 2 or not first:
                        turn(g - 2, s % 2)
                    if s == 0 and not first:
                        attn_out(n - 1, 1, v_t, n * 4 + 2)
                    if s == 1 and first:
                        pe.wait_ge(h_lo, halves_split)
                    if s == 1:
                        if first:
                            values(n, 2, v_t, n * 4 + 2)
                        else:
                            values(n, 2, o_x, n * 4 - 2)
                    if s == 2 and not first:
                        attn_out(n - 1, 2, v_t, n * 4 + 3)
                    if s == 3:
                        if first:
                            values(n, 3, v_t, n * 4 + 3)
                        else:
                            values(n, 3, o_x, n * 4 - 1)
                    if s == 4 and not first:
                        attn_out(n - 1, 3, v_t, n * 4 + 4)
                    if s == 5 and not last:
                        pe.wait_ge(w_v, n * 2 + 4)
                        if first:
                            values(n + 1, 0, v_t, n * 4 + 4)
                        else:
                            values(n + 1, 0, o_x, n * 4)
                    if s == 6:
                        pe.wait_ge(w_o, n * 2 + 2)
                        if last:
                            attn_out(n, 0, o_x, n * 4, bias_row)
                        else:
                            attn_out(n, 0, v_t, n * 4 + 5)
                    if s == 7 and not last:
                        values(n + 1, 1, o_x, n * 4 + 1)
                    if s < 4:
                        pe.wait_ge(g_lo, PAST + n * 8 + 4 + s)
                        proj(n, 4 + s)
                    elif not last:
                        if s % 2 == 0:
                            pe.wait_ge(w_qk, n * 4 + s + 2)
                        pe.wait_ge(g_lo, PAST + n * 8 + 4 + s)
                        proj(n + 1, s - 4)
                    if s >= 3:
                        pv(g - 3, s - 3, n)
                    elif not first:
                        pv(g - 3, s + 5, n - 1)

            pe.wait_ge(enc_lo, 1)
            with pe.Fori(0, PH) as ph:
                n0 = ph * PAIRS
                layer_norm(ln_half(ph + 1, 0), (2, 3))
                pe.wait_ge(w_v, n0 * 2 + 2)
                values(n0, 0, o_x, n0 * 4)
                pe.wait_ge(w_qk, n0 * 4 + 2)
                pe.wait_ge(g_lo, PAST + n0 * 8)
                proj(n0, 0)
                values(n0, 1, v_t, n0 * 4 + 1)
                pe.wait_ge(w_qk, n0 * 4 + 4)
                pe.wait_ge(m_x, 4)
                proj(n0, 2, 5)
                pe.wait_ge(h_lo, ph * 4 + 6)
                proj(n0, 1, 4)
                pe.wait_ge(g_lo, PAST + n0 * 8 + 1)
                proj(n0, 3)
                pe.wait_ge(g_lo, PAST + n0 * 8 + 2)
                pe.wait_ge(v_t, PAST + n0 * 4 + 2)
                layer_norm(ln_half(ph + 1, 1), (7, 5))
                pair(n0, True, False, halves_split=ph * 4 + 8)
                with pe.Fori(1, PAIRS - 1) as p:
                    pair(n0 + p, False, False)
                n = n0 + (PAIRS - 1)
                pair(n, False, True, ph + 3)
                g = n * STEPS
                turn(g + 6, 0)
                pv(g + 5, 5, n)
                turn(g + 7, 1)
                attn_out(n, 1, o_x, n * 4 + 1, ph + 3)
                pv(g + 6, 6, n)
                attn_out(n, 2, o_x, n * 4 + 2, ph + 3)
                pv(g + 7, 7, n)
                attn_out(n, 3, o_x, n * 4 + 3, ph + 3)
            pe.wait_ge(o_x, PAST + PH * PAIRS * 4)
            mlp(PH + 1, 1, 5)


def kernel(**inputs):
    import numpy as _np
    import concourse.bacc as _bacc
    from concourse import mybir as _mybir
    from concourse.bass_utils import run_bass_kernel_spmd as _run

    a = {k: _np.ascontiguousarray(v) for k, v in inputs.items()}
    L0 = {k[len("L0_xattn_"):]: v for k, v in a.items() if k.startswith("L0_")}
    L1 = {k[len("L1_xattn_"):]: v for k, v in a.items() if k.startswith("L1_")}

    def cols(v):
        return v.reshape(-1, P).T

    bqkv, bkv = L0["b_qkv"], L0["b_kv"]
    packs = {
        "ln1_s": L0["ln1_s"], "ln1_b": L0["ln1_b"], "bq_s": bqkv[:D], "bk_s": bqkv[D:2 * D], "bv_s": bqkv[2 * D:],
        "ln2_s": L0["ln2_s"], "ln2_b": L0["ln2_b"], "bq_c": L0["b_q"], "bk_c": bkv[:D], "bv_c": bkv[D:],
        "ln3_s": L0["ln3_s"], "ln3_b": L0["ln3_b"], "b1": L0["b1"],
        "lnx_s": _np.concatenate([L1["ln1_scale"], L1["ln2_scale"], L1["ln_mlp_scale"]]),
        "lnx_b": _np.concatenate([L1["ln1_offset"], L1["ln2_offset"], L1["ln_mlp_offset"]]),
        "bq": _np.concatenate([L1["bq1"], L1["bq2"]]), "bk": _np.concatenate([L1["bk1"], L1["bk2"]]),
        "bias_k": _np.concatenate([L1["bias_k1"].reshape(-1), L1["bias_k2"].reshape(-1)]),
        "bias_v": _np.concatenate([L1["bias_v1"].reshape(-1), L1["bias_v2"].reshape(-1)]),
        "b_fc1": L1["b_fc1"],
    }
    vec = _np.concatenate([cols(packs[k]) for k in VEC], axis=1)
    row = _np.stack([L0["b_ao"], L0["b_co"], L0["b2"], L1["bo1"], L1["bo2"], L1["b_fc2"]])[None]
    rows_of = _np.arange(P)[:, None] // HD0 == _np.arange(HG)[None]
    consts = _np.concatenate([_np.eye(P), rows_of], axis=1).astype(_np.float32)

    def heads(w):
        return w.reshape(KD, P, H1, HD1).transpose(2, 1, 0, 3)

    wqk = _np.stack([_np.stack([heads(L1[f"wq{i}"]), heads(L1[f"wk{i}"])], axis=2) for i in (1, 2)])
    wqk = wqk.reshape(PH * H1, P, 2 * KD * HD1)
    wv = _np.stack([L1[f"wv{i}"].reshape(KD, P, PAIRS, 2 * HD1).transpose(2, 1, 0, 3) for i in (1, 2)])
    wv = wv.reshape(PH * PAIRS, P, KD * 2 * HD1)
    wo = _np.stack([L1[f"wo{i}"].reshape(PAIRS, 2, HD1, D).transpose(0, 2, 1, 3) for i in (1, 2)])
    wo = wo.reshape(PH * PAIRS, P, 2 * D)
    vb = _np.stack([_np.stack([L1[f"bv{i}"].reshape(PAIRS, 2 * HD1), L1[f"bias_v{i}"].reshape(PAIRS, 2 * HD1)],
                              axis=1) for i in (1, 2)]).reshape(PH * PAIRS, 4 * HD1)
    feeds = {
        "x": a["x"].reshape(TOK, D), "enc": a["ctx_2048"].reshape(TOK, D),
        "mask_self": a["mask_1x1xSxS2_fc1"].reshape(S, S), "mask_cross": a["mask_Bx1xSxS2_ff1"].reshape(B * S, S),
        "consts": consts, "vec": vec, "row": row,
        "w_qkv": L0["w_qkv"], "w_ao": L0["w_ao"], "w_q": L0["w_q"], "w_kv": L0["w_kv"], "w_co": L0["w_co"],
        "w1": L0["w1"], "w2": L0["w2"], "wf1": L1["w_fc1"], "wf2": L1["w_fc2"],
        "wqk": wqk, "wv": wv, "wo": wo, "vb": vb,
    }
    nc = _bacc.Bacc("TRN2", target_bir_lowering=False, num_devices=1)
    arrays, args = {}, []
    for name, v in feeds.items():
        v = _np.ascontiguousarray(v)
        arrays[f"in_{name}"] = v
        args.append(nc.dram_tensor(f"in_{name}", v.shape, _mybir.dt.from_np(v.dtype), kind="ExternalInput").ap())
    out = nc.dram_tensor("out_x", (TOK, D), _mybir.dt.float32, kind="ExternalOutput").ap()
    build(nc, *args, out)
    r = _run(nc, [arrays], core_ids=[0])
    return r.results[0]["out_x"].reshape(B, S, D)
```
